# Optimizing a Trainium2 kernel written in Bass

```python
import numpy as np
import jax
import jax.numpy as jnp

def _softmax(x, axis=-1):
    return jax.nn.softmax(x, axis=axis)

def _gelu(x):
    return jax.nn.gelu(x, approximate=True)

def _silu(x):
    return jax.nn.silu(x)

def _sigmoid(x):
    return jax.nn.sigmoid(x)

def _layernorm(x, axis=-1, eps=1e-05):
    m = jnp.mean(x, axis=axis, keepdims=True)
    v = jnp.var(x, axis=axis, keepdims=True)
    return (x - m) / jnp.sqrt(v + eps)

def _scatter_add(tgt, idx, src, axis=0):
    return tgt.at[idx].add(src)

def _segment_sum(src, seg, n):
    return jax.ops.segment_sum(src, seg, n)
kernel_name = 'mk_decoder_postln_d2_seqx_r4_9e74df'

def setup_inputs(seed: int=0):
    np.random.seed(seed)
    _w = jnp.asarray

    def _rec_inputs():
        import jax
        import jax.numpy as jnp
        _rk = jax.random.key(seed)
        x = -0.000929 + 1 * jax.random.normal(jax.random.fold_in(_rk, 1), (2, 1024, 256), jnp.float32)
        _lenS = 1024 - jax.random.randint(jax.random.fold_in(_rk, 7), (2,), 0, max(1, 1024 // 4) + 1, jnp.int32)
        _lenS2 = 154 - jax.random.randint(jax.random.fold_in(_rk, 8), (2,), 0, max(1, 154 // 4) + 1, jnp.int32)
        _ctx_1024P = jax.random.normal(jax.random.fold_in(_rk, 11), (2, 16, 256), jnp.float32)
        _ctx_1024c = jax.random.dirichlet(jax.random.fold_in(_rk, 511), 0.3 * jnp.ones((16,), jnp.float32), (2, 154))
        _ctx_1024t = jnp.einsum('bsk,bkd->bsd', _ctx_1024c, _ctx_1024P)
        _ctx_1024t = _ctx_1024t * jax.lax.rsqrt(jnp.mean(jnp.square(_ctx_1024t)) + 1e-12) * 0.953939
        ctx_1024 = -1.52775e-05 + 0.999936 * (_ctx_1024t + 0.3 * jax.random.normal(jax.random.fold_in(_rk, 611), (2, 154, 256), jnp.float32))
        _validS = jnp.arange(1024)[None, :] < _lenS[:, None]
        _validS2 = jnp.arange(154)[None, :] < _lenS2[:, None]
        _causal = jnp.tril(jnp.ones((1024, 1024), dtype=bool))
        mask_Bx1xS2_ik0 = jnp.where(jnp.broadcast_to(_validS2[:, None, :], (2, 1, 154)), 0, 1).astype(jnp.int32)
        return (x, ctx_1024, mask_Bx1xS2_ik0)
    x, ctx_1024, mask_Bx1xS2_ik0 = _rec_inputs()

    def _L0_attn_setup():
        import jax, jax.numpy as jnp
        import numpy as np
        NUM_HEADS = 16
        DIM = 256
        HARMONICS = 32
        B, L = (2, 512)

        def holo_linear(x, basis, phase, amp):
            resonance = jnp.einsum('bli,hi->blh', x, basis)
            w = amp * jnp.cos(phase)
            return jnp.einsum('blh,oh->blo', resonance, w)
        key = jax.random.key(seed)
        ks = jax.random.split(key, 13)
        two_pi = 2.0 * np.pi

        def make_proj(k0, k1):
            basis = jax.random.normal(k0, (HARMONICS, DIM), dtype=jnp.float32)
            basis = basis / jnp.linalg.norm(basis, axis=1, keepdims=True)
            phase = jax.random.normal(k1, (DIM, HARMONICS), dtype=jnp.float32) * two_pi
            amp = jnp.ones((DIM, HARMONICS), dtype=jnp.float32) / HARMONICS
            return (basis, phase, amp)
        x = jax.random.normal(ks[0], (B, L, DIM), dtype=jnp.float32)
        bq, pq, aq = make_proj(ks[1], ks[2])
        bk, pk, ak = make_proj(ks[3], ks[4])
        bv, pv, av = make_proj(ks[5], ks[6])
        bo, po, ao = make_proj(ks[7], ks[8])
        return {'x': x, 'basis_q': bq, 'phase_q': pq, 'amp_q': aq, 'basis_k': bk, 'phase_k': pk, 'amp_k': ak, 'basis_v': bv, 'phase_v': pv, 'amp_v': av, 'basis_o': bo, 'phase_o': po, 'amp_o': ao}
    _L0_attn_all = _L0_attn_setup()
    _L0_attn_in = {k: v for k, v in _L0_attn_all.items() if k in ('basis_q', 'phase_q', 'amp_q', 'basis_k', 'phase_k', 'amp_k', 'basis_v', 'phase_v', 'amp_v', 'basis_o', 'phase_o', 'amp_o')}
    del _L0_attn_all

    def _L0_xattn_setup():
        import jax, jax.numpy as jnp
        import numpy as np
        B, N, L, D, H = (8, 128, 1024, 256, 16)
        key = jax.random.key(seed)
        ks = jax.random.split(key, 7)
        s = 1.0 / np.sqrt(D)
        return {'q': jax.random.normal(ks[0], (B, N, D), dtype=jnp.float32), 'k': jax.random.normal(ks[1], (B, L, D), dtype=jnp.float32), 'v': jax.random.normal(ks[2], (B, L, D), dtype=jnp.float32), 'Wq': jax.random.normal(ks[3], (D, D), dtype=jnp.float32) * s, 'Wk': jax.random.normal(ks[4], (D, D), dtype=jnp.float32) * s, 'Wv': jax.random.normal(ks[5], (D, D), dtype=jnp.float32) * s, 'Wo': jax.random.normal(ks[6], (D, D), dtype=jnp.float32) * s}
    _L0_xattn_all = _L0_xattn_setup()
    _L0_xattn_in = {k: v for k, v in _L0_xattn_all.items() if k in ('Wq', 'Wk', 'Wv', 'Wo')}
    del _L0_xattn_all

    def _L0_ffn_setup():
        import jax, jax.numpy as jnp
        import numpy as np
        D_IN, D_HID = (256, 1024)

        def _ternary(key, shape):
            return jax.random.randint(key, shape, -1, 2).astype(jnp.float32)

        def _tlin(x, w, s):
            return jnp.einsum('bsi,oi->bso', x, w) * s
        key = jax.random.key(seed)
        ks = jax.random.split(key, 12)
        inv = lambda fan: 1.0 / np.sqrt(fan).astype(np.float32)
        return {'x': jax.random.normal(ks[0], (4, 512, D_IN), dtype=jnp.float32), 'w1_w': _ternary(ks[1], (D_HID, D_IN)), 'w1_s': jax.random.uniform(ks[2], (D_HID,), dtype=jnp.float32) * inv(D_IN), 'w2_w': _ternary(ks[3], (D_HID, D_IN)), 'w2_s': jax.random.uniform(ks[4], (D_HID,), dtype=jnp.float32) * inv(D_IN), 'h1_w': _ternary(ks[5], (D_HID, D_HID)), 'h1_s': jax.random.uniform(ks[6], (D_HID,), dtype=jnp.float32) * inv(D_HID), 'h2_w': _ternary(ks[7], (D_HID, D_HID)), 'h2_s': jax.random.uniform(ks[8], (D_HID,), dtype=jnp.float32) * inv(D_HID), 'w3_w': _ternary(ks[9], (D_IN, D_HID)), 'w3_s': jax.random.uniform(ks[10], (D_IN,), dtype=jnp.float32) * inv(D_HID)}
    _L0_ffn_all = _L0_ffn_setup()
    _L0_ffn_in = {k: v for k, v in _L0_ffn_all.items() if k in ('w1_w', 'w1_s', 'w2_w', 'w2_s', 'h1_w', 'h1_s', 'h2_w', 'h2_s', 'w3_w', 'w3_s')}
    del _L0_ffn_all

    def _L1_attn_setup():
        import jax, jax.numpy as jnp
        import numpy as np
        import math
        D = 256
        CHUNK = 64
        B = 4
        S = 1024

        def _layernorm(x, g, b, eps=1e-05):
            mu = jnp.mean(x, axis=-1, keepdims=True)
            var = jnp.mean((x - mu) ** 2, axis=-1, keepdims=True)
            return (x - mu) * jax.lax.rsqrt(var + eps) * g + b
        key = jax.random.key(seed)
        ks = jax.random.split(key, 8)
        lin = lambda k: jax.random.normal(k, (D, D), jnp.float32) * 0.02
        return {'x': jax.random.normal(ks[0], (B, S, D), jnp.float32), 'Wk': lin(ks[1]), 'bk': jnp.zeros((D,), jnp.float32), 'Wv': lin(ks[2]), 'bv': jnp.zeros((D,), jnp.float32), 'Wq': lin(ks[3]), 'bq': jnp.zeros((D,), jnp.float32), 'Wkp': lin(ks[4]), 'bkp': jnp.zeros((D,), jnp.float32), 'Wqp': lin(ks[5]), 'bqp': jnp.zeros((D,), jnp.float32), 'phase_scale': jnp.ones((D,), jnp.float32) * math.pi, 'ln_g': jnp.ones((D,), jnp.float32), 'ln_b': jnp.zeros((D,), jnp.float32), 'Wo': lin(ks[6]), 'bo': jnp.zeros((D,), jnp.float32)}
    _L1_attn_all = _L1_attn_setup()
    _L1_attn_in = {k: v for k, v in _L1_attn_all.items() if k in ('Wk', 'bk', 'Wv', 'bv', 'Wq', 'bq', 'Wkp', 'bkp', 'Wqp', 'bqp', 'phase_scale', 'ln_g', 'ln_b', 'Wo', 'bo')}
    del _L1_attn_all

    def _L1_xattn_setup():
        import jax, jax.numpy as jnp
        import numpy as np
        B, SQ, SK = (2, 512, 512)
        DQ = DK = DV = DM = DOUT = 256
        H = 16
        DHEAD = DM // H
        key = jax.random.key(seed)
        ks = jax.random.split(key, 12)
        s = 0.02
        return {'Q': jax.random.normal(ks[0], (B, SQ, DQ), jnp.float32), 'K': jax.random.normal(ks[1], (B, SK, DK), jnp.float32), 'V': jax.random.normal(ks[2], (B, SK, DV), jnp.float32), 'mask': jax.random.randint(ks[3], (B, 1, SK), 0, 2, jnp.int32), 'Wq': jax.random.normal(ks[4], (DQ, DM), jnp.float32) * s, 'bq': jnp.zeros((DM,), jnp.float32), 'Wk': jax.random.normal(ks[5], (DK, DM), jnp.float32) * s, 'bk': jnp.zeros((DM,), jnp.float32), 'Wv': jax.random.normal(ks[6], (DV, DM), jnp.float32) * s, 'bv': jnp.zeros((DM,), jnp.float32), 'Wo': jax.random.normal(ks[7], (DM, DOUT), jnp.float32) * s, 'bo': jnp.zeros((DOUT,), jnp.float32)}
    _L1_xattn_all = _L1_xattn_setup()
    _L1_xattn_in = {k: v for k, v in _L1_xattn_all.items() if k in ('Wq', 'bq', 'Wk', 'bk', 'Wv', 'bv', 'Wo', 'bo')}
    del _L1_xattn_all

    def _L1_ffn_setup():
        import jax, jax.numpy as jnp
        import numpy as np
        EPS = 1e-05

        def _ln(x, g, b):
            mu = jnp.mean(x, axis=-1, keepdims=True)
            var = jnp.mean(jnp.square(x - mu), axis=-1, keepdims=True)
            return (x - mu) * jax.lax.rsqrt(var + EPS) * g + b

        def _forward(x, index_b, index_t, sw1, sb1, sw2, sb2, sw3, sb3, s_ln_g, s_ln_b, sg_w, sg_b, eg_w, eg_b, exp_bias, ew1, eb1, ew2, eb2, ew3, eb3, sel_ln_g, sel_ln_b):
            x1 = jnp.einsum('btd,hd->bth', x, sw1) + sb1
            x2 = jnp.einsum('btd,hd->bth', x, sw2) + sb2
            sh = _ln(jax.nn.silu(x1) * x2, s_ln_g, s_ln_b)
            shared_out = jnp.einsum('bth,dh->btd', sh, sw3) + sb3
            x_moe = x[index_b, index_t]
            shared_scores = jax.nn.sigmoid(x_moe @ sg_w.T + sg_b)
            expert_scores = jax.nn.sigmoid(x_moe @ eg_w.T + eg_b)
            top1_idx = jnp.argmax(expert_scores + exp_bias, axis=-1)
            top1_score = jnp.take_along_axis(expert_scores, top1_idx[:, None], axis=-1)
            weights = jax.nn.softmax(jnp.concatenate([shared_scores, top1_score], axis=-1), axis=-1)
            shared_w, expert_w = (weights[:, 0], weights[:, 1])
            shared_moe_out = shared_out[index_b, index_t] * shared_w[:, None]
            h1 = jnp.einsum('md,ehd->meh', x_moe, ew1) + eb1
            h2 = jnp.einsum('md,ehd->meh', x_moe, ew2) + eb2
            z = _ln(jax.nn.silu(h1) * h2, sel_ln_g, sel_ln_b)
            out_all = jnp.einsum('meh,edh->med', z, ew3) + eb3
            expert_out = jnp.take_along_axis(out_all, top1_idx[:, None, None], axis=1)[:, 0]
            expert_moe_out = expert_out * expert_w[:, None]
            final_out = shared_out.at[index_b, index_t].set(shared_moe_out + expert_moe_out)
            return final_out
        B, T, D, E, H, M = (2, 512, 256, 8, 128, 512)
        key = jax.random.key(seed)
        ks = jax.random.split(key, 24)
        s = 0.02
        inp = {}
        inp['x'] = jax.random.normal(ks[0], (B, T, D), jnp.float32)
        flat = jnp.arange(M, dtype=jnp.int32) * 2
        inp['index_b'] = flat // T
        inp['index_t'] = flat % T
        inp['sw1'] = jax.random.normal(ks[1], (H, D), jnp.float32) * s
        inp['sb1'] = jnp.zeros((H,), jnp.float32)
        inp['sw2'] = jax.random.normal(ks[2], (H, D), jnp.float32) * s
        inp['sb2'] = jnp.zeros((H,), jnp.float32)
        inp['sw3'] = jax.random.normal(ks[3], (D, H), jnp.float32) * s
        inp['sb3'] = jnp.zeros((D,), jnp.float32)
        inp['s_ln_g'] = jnp.ones((H,), jnp.float32)
        inp['s_ln_b'] = jnp.zeros((H,), jnp.float32)
        inp['sg_w'] = jax.random.normal(ks[4], (1, D), jnp.float32) * s
        inp['sg_b'] = jnp.zeros((1,), jnp.float32)
        inp['eg_w'] = jax.random.normal(ks[5], (E, D), jnp.float32) * s
        inp['eg_b'] = jnp.zeros((E,), jnp.float32)
        inp['exp_bias'] = jnp.zeros((E,), jnp.float32)
        inp['ew1'] = jax.random.normal(ks[6], (E, H, D), jnp.float32) * s
        inp['eb1'] = jnp.zeros((E, H), jnp.float32)
        inp['ew2'] = jax.random.normal(ks[7], (E, H, D), jnp.float32) * s
        inp['eb2'] = jnp.zeros((E, H), jnp.float32)
        inp['ew3'] = jax.random.normal(ks[8], (E, D, H), jnp.float32) * s
        inp['eb3'] = jnp.zeros((E, D), jnp.float32)
        inp['sel_ln_g'] = jnp.ones((H,), jnp.float32)
        inp['sel_ln_b'] = jnp.zeros((H,), jnp.float32)
        return inp
    _L1_ffn_all = _L1_ffn_setup()
    _L1_ffn_in = {k: v for k, v in _L1_ffn_all.items() if k in ('index_b', 'index_t', 'sw1', 'sb1', 'sw2', 'sb2', 'sw3', 'sb3', 's_ln_g', 's_ln_b', 'sg_w', 'sg_b', 'eg_w', 'eg_b', 'exp_bias', 'ew1', 'eb1', 'ew2', 'eb2', 'ew3', 'eb3', 'sel_ln_g', 'sel_ln_b')}
    del _L1_ffn_all
    return {'x': x, 'ctx_1024': ctx_1024, 'mask_Bx1xS2_ik0': mask_Bx1xS2_ik0, 'L0_attn_basis_q': _L0_attn_in['basis_q'], 'L0_attn_phase_q': _L0_attn_in['phase_q'], 'L0_attn_amp_q': _L0_attn_in['amp_q'], 'L0_attn_basis_k': _L0_attn_in['basis_k'], 'L0_attn_phase_k': _L0_attn_in['phase_k'], 'L0_attn_amp_k': _L0_attn_in['amp_k'], 'L0_attn_basis_v': _L0_attn_in['basis_v'], 'L0_attn_phase_v': _L0_attn_in['phase_v'], 'L0_attn_amp_v': _L0_attn_in['amp_v'], 'L0_attn_basis_o': _L0_attn_in['basis_o'], 'L0_attn_phase_o': _L0_attn_in['phase_o'], 'L0_attn_amp_o': _L0_attn_in['amp_o'], 'L0_xattn_Wq': _L0_xattn_in['Wq'], 'L0_xattn_Wk': _L0_xattn_in['Wk'], 'L0_xattn_Wv': _L0_xattn_in['Wv'], 'L0_xattn_Wo': _L0_xattn_in['Wo'], 'L0_ffn_w1_w': _L0_ffn_in['w1_w'], 'L0_ffn_w1_s': _L0_ffn_in['w1_s'], 'L0_ffn_w2_w': _L0_ffn_in['w2_w'], 'L0_ffn_w2_s': _L0_ffn_in['w2_s'], 'L0_ffn_h1_w': _L0_ffn_in['h1_w'], 'L0_ffn_h1_s': _L0_ffn_in['h1_s'], 'L0_ffn_h2_w': _L0_ffn_in['h2_w'], 'L0_ffn_h2_s': _L0_ffn_in['h2_s'], 'L0_ffn_w3_w': _L0_ffn_in['w3_w'], 'L0_ffn_w3_s': _L0_ffn_in['w3_s'], 'L1_attn_Wk': _L1_attn_in['Wk'], 'L1_attn_bk': _L1_attn_in['bk'], 'L1_attn_Wv': _L1_attn_in['Wv'], 'L1_attn_bv': _L1_attn_in['bv'], 'L1_attn_Wq': _L1_attn_in['Wq'], 'L1_attn_bq': _L1_attn_in['bq'], 'L1_attn_Wkp': _L1_attn_in['Wkp'], 'L1_attn_bkp': _L1_attn_in['bkp'], 'L1_attn_Wqp': _L1_attn_in['Wqp'], 'L1_attn_bqp': _L1_attn_in['bqp'], 'L1_attn_phase_scale': _L1_attn_in['phase_scale'], 'L1_attn_ln_g': _L1_attn_in['ln_g'], 'L1_attn_ln_b': _L1_attn_in['ln_b'], 'L1_attn_Wo': _L1_attn_in['Wo'], 'L1_attn_bo': _L1_attn_in['bo'], 'L1_xattn_Wq': _L1_xattn_in['Wq'], 'L1_xattn_bq': _L1_xattn_in['bq'], 'L1_xattn_Wk': _L1_xattn_in['Wk'], 'L1_xattn_bk': _L1_xattn_in['bk'], 'L1_xattn_Wv': _L1_xattn_in['Wv'], 'L1_xattn_bv': _L1_xattn_in['bv'], 'L1_xattn_Wo': _L1_xattn_in['Wo'], 'L1_xattn_bo': _L1_xattn_in['bo'], 'L1_ffn_index_b': _L1_ffn_in['index_b'], 'L1_ffn_index_t': _L1_ffn_in['index_t'], 'L1_ffn_sw1': _L1_ffn_in['sw1'], 'L1_ffn_sb1': _L1_ffn_in['sb1'], 'L1_ffn_sw2': _L1_ffn_in['sw2'], 'L1_ffn_sb2': _L1_ffn_in['sb2'], 'L1_ffn_sw3': _L1_ffn_in['sw3'], 'L1_ffn_sb3': _L1_ffn_in['sb3'], 'L1_ffn_s_ln_g': _L1_ffn_in['s_ln_g'], 'L1_ffn_s_ln_b': _L1_ffn_in['s_ln_b'], 'L1_ffn_sg_w': _L1_ffn_in['sg_w'], 'L1_ffn_sg_b': _L1_ffn_in['sg_b'], 'L1_ffn_eg_w': _L1_ffn_in['eg_w'], 'L1_ffn_eg_b': _L1_ffn_in['eg_b'], 'L1_ffn_exp_bias': _L1_ffn_in['exp_bias'], 'L1_ffn_ew1': _L1_ffn_in['ew1'], 'L1_ffn_eb1': _L1_ffn_in['eb1'], 'L1_ffn_ew2': _L1_ffn_in['ew2'], 'L1_ffn_eb2': _L1_ffn_in['eb2'], 'L1_ffn_ew3': _L1_ffn_in['ew3'], 'L1_ffn_eb3': _L1_ffn_in['eb3'], 'L1_ffn_sel_ln_g': _L1_ffn_in['sel_ln_g'], 'L1_ffn_sel_ln_b': _L1_ffn_in['sel_ln_b']}

def reference(x, ctx_1024, mask_Bx1xS2_ik0, L0_attn_basis_q, L0_attn_phase_q, L0_attn_amp_q, L0_attn_basis_k, L0_attn_phase_k, L0_attn_amp_k, L0_attn_basis_v, L0_attn_phase_v, L0_attn_amp_v, L0_attn_basis_o, L0_attn_phase_o, L0_attn_amp_o, L0_xattn_Wq, L0_xattn_Wk, L0_xattn_Wv, L0_xattn_Wo, L0_ffn_w1_w, L0_ffn_w1_s, L0_ffn_w2_w, L0_ffn_w2_s, L0_ffn_h1_w, L0_ffn_h1_s, L0_ffn_h2_w, L0_ffn_h2_s, L0_ffn_w3_w, L0_ffn_w3_s, L1_attn_Wk, L1_attn_bk, L1_attn_Wv, L1_attn_bv, L1_attn_Wq, L1_attn_bq, L1_attn_Wkp, L1_attn_bkp, L1_attn_Wqp, L1_attn_bqp, L1_attn_phase_scale, L1_attn_ln_g, L1_attn_ln_b, L1_attn_Wo, L1_attn_bo, L1_xattn_Wq, L1_xattn_bq, L1_xattn_Wk, L1_xattn_bk, L1_xattn_Wv, L1_xattn_bv, L1_xattn_Wo, L1_xattn_bo, L1_ffn_index_b, L1_ffn_index_t, L1_ffn_sw1, L1_ffn_sb1, L1_ffn_sw2, L1_ffn_sb2, L1_ffn_sw3, L1_ffn_sb3, L1_ffn_s_ln_g, L1_ffn_s_ln_b, L1_ffn_sg_w, L1_ffn_sg_b, L1_ffn_eg_w, L1_ffn_eg_b, L1_ffn_exp_bias, L1_ffn_ew1, L1_ffn_eb1, L1_ffn_ew2, L1_ffn_eb2, L1_ffn_ew3, L1_ffn_eb3, L1_ffn_sel_ln_g, L1_ffn_sel_ln_b):
    import jax
    import jax.numpy as jnp

    def _L0_attn_ref(x, basis_q, phase_q, amp_q, basis_k, phase_k, amp_k, basis_v, phase_v, amp_v, basis_o, phase_o, amp_o):
        import jax, jax.numpy as jnp
        import numpy as np
        NUM_HEADS = 16
        DIM = 256
        HARMONICS = 32
        B, L = (2, 512)

        def holo_linear(x, basis, phase, amp):
            resonance = jnp.einsum('bli,hi->blh', x, basis)
            w = amp * jnp.cos(phase)
            return jnp.einsum('blh,oh->blo', resonance, w)
        Bsz, Ls, C = x.shape
        head_dim = C // NUM_HEADS
        scale = head_dim ** (-0.5)

        def split_heads(t):
            return t.reshape(Bsz, Ls, NUM_HEADS, head_dim).transpose(0, 2, 1, 3)
        q = split_heads(holo_linear(x, basis_q, phase_q, amp_q))
        k = split_heads(holo_linear(x, basis_k, phase_k, amp_k))
        v = split_heads(holo_linear(x, basis_v, phase_v, amp_v))
        attn = jnp.einsum('bhqd,bhkd->bhqk', q, k) * scale
        attn = jax.nn.softmax(attn, axis=-1)
        out = jnp.einsum('bhqk,bhkd->bhqd', attn, v)
        out = out.transpose(0, 2, 1, 3).reshape(Bsz, Ls, C)
        return holo_linear(out, basis_o, phase_o, amp_o)

    def _L0_xattn_ref(q, k, v, Wq, Wk, Wv, Wo):
        import jax, jax.numpy as jnp
        import numpy as np
        B, N, L, D, H = (8, 128, 1024, 256, 16)
        Bq, Nq, Dm = q.shape
        Lk = k.shape[1]
        Hh = H
        Dh = Dm // Hh
        scale = Dm ** (-0.5)
        qh = (q @ Wq.T).reshape(Bq, Nq, Hh, Dh).transpose(0, 2, 1, 3)
        kh = (k @ Wk.T).reshape(Bq, Lk, Hh, Dh).transpose(0, 2, 1, 3)
        vh = (v @ Wv.T).reshape(Bq, Lk, Hh, Dh).transpose(0, 2, 1, 3)
        attn = jnp.einsum('bhnc,bhlc->bhnl', qh * scale, kh)
        attn = jax.nn.softmax(attn, axis=2)
        attn = attn / jnp.sum(attn, axis=-1, keepdims=True)
        out = jnp.einsum('bhnl,bhlc->bhnc', attn, vh)
        out = out.transpose(0, 2, 1, 3).reshape(Bq, Nq, Dm)
        return out @ Wo.T

    def _L0_ffn_ref(x, w1_w, w1_s, w2_w, w2_s, h1_w, h1_s, h2_w, h2_s, w3_w, w3_s):
        import jax, jax.numpy as jnp
        import numpy as np
        D_IN, D_HID = (256, 1024)

        def _ternary(key, shape):
            return jax.random.randint(key, shape, -1, 2).astype(jnp.float32)

        def _tlin(x, w, s):
            return jnp.einsum('bsi,oi->bso', x, w) * s
        h = jax.nn.silu(_tlin(x, w1_w, w1_s)) * _tlin(x, w2_w, w2_s)
        h = jax.nn.gelu(_tlin(h, h1_w, h1_s), approximate=False)
        h = jax.nn.gelu(_tlin(h, h2_w, h2_s), approximate=False)
        return _tlin(h, w3_w, w3_s)

    def _L1_attn_ref(x, Wk, bk, Wv, bv, Wq, bq, Wkp, bkp, Wqp, bqp, phase_scale, ln_g, ln_b, Wo, bo):
        import jax, jax.numpy as jnp
        import numpy as np
        import math
        D = 256
        CHUNK = 64
        B = 4
        S = 1024

        def _layernorm(x, g, b, eps=1e-05):
            mu = jnp.mean(x, axis=-1, keepdims=True)
            var = jnp.mean((x - mu) ** 2, axis=-1, keepdims=True)
            return (x - mu) * jax.lax.rsqrt(var + eps) * g + b
        batch, seq_len, dim = x.shape
        key = jnp.einsum('bsd,ed->bse', x, Wk) + bk
        value = jnp.einsum('bsd,ed->bse', x, Wv) + bv
        query = jnp.einsum('bsd,ed->bse', x, Wq) + bq
        key_phase = jnp.tanh(jnp.einsum('bsd,ed->bse', key, Wkp) + bkp) * phase_scale
        query_phase = jnp.tanh(jnp.einsum('bsd,ed->bse', query, Wqp) + bqp) * phase_scale
        bound_real = value * jnp.cos(key_phase)
        bound_imag = value * jnp.sin(key_phase)
        pad_len = -seq_len % CHUNK
        if pad_len > 0:
            pad = ((0, 0), (0, pad_len), (0, 0))
            bound_real = jnp.pad(bound_real, pad)
            bound_imag = jnp.pad(bound_imag, pad)
            query_phase = jnp.pad(query_phase, pad)
        padded_len = seq_len + pad_len
        nc = padded_len // CHUNK
        br = bound_real.reshape(batch, nc, CHUNK, dim)
        bi = bound_imag.reshape(batch, nc, CHUNK, dim)
        qp = query_phase.reshape(batch, nc, CHUNK, dim)
        mem_real = jnp.cumsum(br, axis=2)
        mem_imag = jnp.cumsum(bi, axis=2)
        retrieved = mem_real * jnp.cos(qp) + mem_imag * jnp.sin(qp)
        retrieved = retrieved.reshape(batch, padded_len, dim)[:, :seq_len]
        retrieved = retrieved / math.sqrt(dim)
        out = jnp.einsum('bsd,ed->bse', _layernorm(retrieved, ln_g, ln_b), Wo) + bo
        return x + out

    def _L1_xattn_ref(Q, K, V, mask, Wq, bq, Wk, bk, Wv, bv, Wo, bo):
        import jax, jax.numpy as jnp
        import numpy as np
        B, SQ, SK = (2, 512, 512)
        DQ = DK = DV = DM = DOUT = 256
        H = 16
        DHEAD = DM // H
        b, sq, _ = Q.shape
        q = (Q @ Wq + bq).reshape(b, sq, H, DHEAD).transpose(0, 2, 1, 3)
        k = (K @ Wk + bk).reshape(b, -1, H, DHEAD).transpose(0, 2, 1, 3)
        v = (V @ Wv + bv).reshape(b, -1, H, DHEAD).transpose(0, 2, 1, 3)
        scores = jnp.einsum('bhqd,bhkd->bhqk', q, k) / np.sqrt(DHEAD).astype(np.float32)
        m = mask[:, None]
        scores = jnp.where(m == 0, -jnp.inf, scores)
        attn = jax.nn.softmax(scores, axis=-1)
        out = jnp.einsum('bhqk,bhkd->bhqd', attn, v)
        out = out.transpose(0, 2, 1, 3).reshape(b, sq, DM)
        return out @ Wo + bo

    def _L1_ffn_ref(x, index_b, index_t, sw1, sb1, sw2, sb2, sw3, sb3, s_ln_g, s_ln_b, sg_w, sg_b, eg_w, eg_b, exp_bias, ew1, eb1, ew2, eb2, ew3, eb3, sel_ln_g, sel_ln_b):
        import jax, jax.numpy as jnp
        import numpy as np
        EPS = 1e-05

        def _ln(x, g, b):
            mu = jnp.mean(x, axis=-1, keepdims=True)
            var = jnp.mean(jnp.square(x - mu), axis=-1, keepdims=True)
            return (x - mu) * jax.lax.rsqrt(var + EPS) * g + b

        def _forward(x, index_b, index_t, sw1, sb1, sw2, sb2, sw3, sb3, s_ln_g, s_ln_b, sg_w, sg_b, eg_w, eg_b, exp_bias, ew1, eb1, ew2, eb2, ew3, eb3, sel_ln_g, sel_ln_b):
            x1 = jnp.einsum('btd,hd->bth', x, sw1) + sb1
            x2 = jnp.einsum('btd,hd->bth', x, sw2) + sb2
            sh = _ln(jax.nn.silu(x1) * x2, s_ln_g, s_ln_b)
            shared_out = jnp.einsum('bth,dh->btd', sh, sw3) + sb3
            x_moe = x[index_b, index_t]
            shared_scores = jax.nn.sigmoid(x_moe @ sg_w.T + sg_b)
            expert_scores = jax.nn.sigmoid(x_moe @ eg_w.T + eg_b)
            top1_idx = jnp.argmax(expert_scores + exp_bias, axis=-1)
            top1_score = jnp.take_along_axis(expert_scores, top1_idx[:, None], axis=-1)
            weights = jax.nn.softmax(jnp.concatenate([shared_scores, top1_score], axis=-1), axis=-1)
            shared_w, expert_w = (weights[:, 0], weights[:, 1])
            shared_moe_out = shared_out[index_b, index_t] * shared_w[:, None]
            h1 = jnp.einsum('md,ehd->meh', x_moe, ew1) + eb1
            h2 = jnp.einsum('md,ehd->meh', x_moe, ew2) + eb2
            z = _ln(jax.nn.silu(h1) * h2, sel_ln_g, sel_ln_b)
            out_all = jnp.einsum('meh,edh->med', z, ew3) + eb3
            expert_out = jnp.take_along_axis(out_all, top1_idx[:, None, None], axis=1)[:, 0]
            expert_moe_out = expert_out * expert_w[:, None]
            final_out = shared_out.at[index_b, index_t].set(shared_moe_out + expert_moe_out)
            return final_out
        return _forward(x, index_b, index_t, sw1, sb1, sw2, sb2, sw3, sb3, s_ln_g, s_ln_b, sg_w, sg_b, eg_w, eg_b, exp_bias, ew1, eb1, ew2, eb2, ew3, eb3, sel_ln_g, sel_ln_b)
    x = _layernorm(x + _L0_attn_ref(x, L0_attn_basis_q, L0_attn_phase_q, L0_attn_amp_q, L0_attn_basis_k, L0_attn_phase_k, L0_attn_amp_k, L0_attn_basis_v, L0_attn_phase_v, L0_attn_amp_v, L0_attn_basis_o, L0_attn_phase_o, L0_attn_amp_o), axis=-1)
    x = _layernorm(x + _L0_xattn_ref(x, ctx_1024, ctx_1024, L0_xattn_Wq, L0_xattn_Wk, L0_xattn_Wv, L0_xattn_Wo), axis=-1)
    x = _layernorm(x + _L0_ffn_ref(x, L0_ffn_w1_w, L0_ffn_w1_s, L0_ffn_w2_w, L0_ffn_w2_s, L0_ffn_h1_w, L0_ffn_h1_s, L0_ffn_h2_w, L0_ffn_h2_s, L0_ffn_w3_w, L0_ffn_w3_s), axis=-1)
    x = _layernorm(x + _L1_attn_ref(x, L1_attn_Wk, L1_attn_bk, L1_attn_Wv, L1_attn_bv, L1_attn_Wq, L1_attn_bq, L1_attn_Wkp, L1_attn_bkp, L1_attn_Wqp, L1_attn_bqp, L1_attn_phase_scale, L1_attn_ln_g, L1_attn_ln_b, L1_attn_Wo, L1_attn_bo), axis=-1)
    x = _layernorm(x + _L1_xattn_ref(x, ctx_1024, ctx_1024, mask_Bx1xS2_ik0, L1_xattn_Wq, L1_xattn_bq, L1_xattn_Wk, L1_xattn_bk, L1_xattn_Wv, L1_xattn_bv, L1_xattn_Wo, L1_xattn_bo), axis=-1)
    x = _layernorm(x + _L1_ffn_ref(x, L1_ffn_index_b, L1_ffn_index_t, L1_ffn_sw1, L1_ffn_sb1, L1_ffn_sw2, L1_ffn_sb2, L1_ffn_sw3, L1_ffn_sb3, L1_ffn_s_ln_g, L1_ffn_s_ln_b, L1_ffn_sg_w, L1_ffn_sg_b, L1_ffn_eg_w, L1_ffn_eg_b, L1_ffn_exp_bias, L1_ffn_ew1, L1_ffn_eb1, L1_ffn_ew2, L1_ffn_eb2, L1_ffn_ew3, L1_ffn_eb3, L1_ffn_sel_ln_g, L1_ffn_sel_ln_b), axis=-1)
    return x

_drawn_inputs = setup_inputs


def setup_inputs(seed=0):
    import zlib

    import numpy as np

    out = dict(_drawn_inputs(seed))
    spreads = {'L0_attn_amp_q': (0.03125, 0.6),
     'L0_attn_amp_k': (0.03125, 0.6),
     'L0_attn_amp_v': (0.03125, 0.6),
     'L0_attn_amp_o': (0.03125, 0.6),
     'L1_attn_bk': (0.0, 0.8),
     'L1_attn_bv': (0.0, 0.1),
     'L1_attn_bq': (0.0, 0.8),
     'L1_attn_bkp': (0.0, 0.277),
     'L1_attn_bqp': (0.0, 0.273),
     'L1_attn_phase_scale': (3.1415927410125732, 0.6),
     'L1_attn_ln_g': (1.0, 0.2),
     'L1_attn_ln_b': (0.0, 0.495),
     'L1_attn_bo': (0.0, 0.1),
     'L1_xattn_bq': (0.0, 0.8),
     'L1_xattn_bk': (0.0, 2.0),
     'L1_xattn_bv': (0.0, 0.1),
     'L1_xattn_bo': (0.0, 0.1),
     'L1_ffn_sb1': (0.0, 0.1),
     'L1_ffn_sb2': (0.0, 0.1),
     'L1_ffn_sb3': (0.0, 0.1),
     'L1_ffn_s_ln_g': (1.0, 0.2),
     'L1_ffn_s_ln_b': (0.0, 0.45),
     'L1_ffn_eg_b': (0.0, 2.0),
     'L1_ffn_exp_bias': (0.0, 0.275),
     'L1_ffn_eb1': (0.0, 0.416),
     'L1_ffn_eb2': (0.0, 0.46),
     'L1_ffn_eb3': (0.0, 0.324),
     'L1_ffn_sel_ln_g': (1.0, 0.6),
     'L1_ffn_sel_ln_b': (0.0, 2.0)}
    factors = {'L0_attn_basis_q': 8.0,
     'L0_attn_phase_q': 8.0,
     'L0_attn_basis_k': 8.0,
     'L0_attn_phase_k': 8.0,
     'L0_attn_basis_v': 8.0,
     'L0_attn_phase_v': 8.0,
     'L0_attn_basis_o': 8.0,
     'L0_attn_phase_o': 8.0,
     'L0_ffn_w1_w': 8.0,
     'L0_ffn_w1_s': 8.0,
     'L0_ffn_w2_w': 8.0,
     'L0_ffn_w2_s': 8.0,
     'L0_ffn_h1_w': 8.0,
     'L0_ffn_h1_s': 8.0,
     'L0_ffn_h2_w': 8.0,
     'L0_ffn_h2_s': 8.0,
     'L0_ffn_w3_w': 8.0,
     'L0_ffn_w3_s': 8.0,
     'L1_attn_Wk': 2.761,
     'L1_xattn_Wq': 8.0,
     'L1_xattn_Wk': 8.0,
     'L1_ffn_sg_w': 200.0,
     'L1_ffn_eg_w': 8.0}
    for name, (base, spread) in spreads.items():
        noise = np.random.default_rng([zlib.crc32(name.encode()), seed]).standard_normal(out[name].shape)
        drawn = base * np.exp(spread * noise) if base else spread * noise
        out[name] = jnp.asarray(drawn.astype(out[name].dtype))
    for name, factor in factors.items():
        out[name] = (out[name] * factor).astype(out[name].dtype)
    return out
```

```python
from contextlib import ExitStack

import numpy as np
import concourse.bass as bass
from concourse import mybir

ALU = mybir.AluOpType
ACT = mybir.ActivationFunctionType
AX_X = mybir.AxisListType.X
F32 = mybir.dt.float32
F32R = mybir.dt.float32r
BF16 = mybir.dt.bfloat16
I32 = mybir.dt.int32
U32 = mybir.dt.uint32

P = 128
B = 2
S = 1024
D = 256
SK = 154
TOK = B * S
TILES = TOK // P
TPB = S // P
HEADS = 16
DH = D // HEADS
SLOTS = B * HEADS
CH = 512
CHUNKS = TOK // CH
HARM = 32
HID = 1024
EPS = 1e-5
NMOE = 512
MT = NMOE // P
XT = TILES + MT
NEXP = 8
EH = 128
SCAN = 64
PROD = 6 * DH
MASKROW = PROD
MAXROW = PROD + 1
KROWS = PROD + 3
Q_PART = [(0, 2), (1, 2), (0, 1), (2, 1)]
K_PART = [(0, 1), (1, 1), (0, 1), (1, 1), (2, 1), (0, 1)]
VW = 32
RSQRT_MAGIC = float(0x5F3759DF)
ROUND = 12582912.0
TWO_PI = 2.0 * np.pi
C1 = 6.28125
C2 = float((np.float32(TWO_PI - C1).view(np.uint32) & np.uint32(0xFFFFF000)).view(np.float32))
C3 = float(np.float32(TWO_PI - C1 - C2))
PI_IN = 3.1415925

M_X0Q, M_X0K, M_X0V, M_X0O, M_LK, M_LV, M_LQ, M_LKP, M_LQP, M_LO, M_X1Q, M_X1K, M_X1V, M_X1O = range(14)
V_LBK, V_LBV, V_LBQ, V_LBKP, V_LBQP, V_PS, V_LG, V_LB, V_X1BQ, V_X1BK = range(10)
R_LBO, R_X1BV, R_X1BO, R_W3S, R_SB3, R_SB12, NROWS = range(7)


USED = []


def clear_used(nc):
    nc.clear_and_free_semaphores(USED)
    USED.clear()
    nc.all_engine_barrier()


def makers(nc, st, stage):
    def semaphore(name):
        USED.append(nc.alloc_semaphore(f"{stage}_{name}"))
        return USED[-1]
    return (semaphore,
            lambda name, shape, dt: st.enter_context(nc.sbuf_tensor(f"{stage}_{name}", shape, dt)),
            lambda name, shape, dt: st.enter_context(nc.psum_tensor(f"{stage}_{name}", shape, dt)))


def linker(eng, sem):
    count = [0]

    def link(ins):
        count[0] += 1
        ins.then_inc(sem, 1)
        eng.wait_ge(sem, count[0])
    return link


def stage_setup(nc, I, G):
    with ExitStack() as st:
        sem, sb, psum = makers(nc, st, "setup")
        loaded, zeroed = sem("loaded"), sem("zeroed")
        block = st.enter_context(nc.Block())

        @block.sync
        def _(sp):
            loads = [
                (G.xT[:, :, 0:TOK], I["x_fm"].rearrange("k p t -> p k t")),
                (G.basis[:], I["basis"].rearrange("k p h -> p k h")),
                (G.holo[0:96, 0, 0, :], I["phase_qkv"]), (G.holo[0:96, 1, 0, :], I["amp_qkv"]),
                (G.holo[0:HARM, 0, 1, :], I["phase_o"]), (G.holo[0:HARM, 1, 1, :], I["amp_o"]),
                (G.X[:, 0:TILES, :], I["x_tm"].rearrange("t p d -> p t d")),
                (G.ctxT[:], I["ctx_fm"].rearrange("k p t -> p k t")),
                (G.wmat[:], I["wmat"]), (G.fvec[:], I["fvec"]), (G.ffn_s[:], I["ffn_s"]),
                (G.evec[:], I["evec"]), (G.grow[:], I["grow"].rearrange("(o r) -> o r", o=1).broadcast_to([P, 17])),
                (G.rvec[:], I["rvec"].rearrange("(o r) d -> o r d", o=1).broadcast_to([P, NROWS, D])),
            ]
            for dst, src in loads:
                sp.dma_start(dst, src).then_inc(loaded, 16)
            sp.wait_ge(loaded, 16 * len(loads))

        @block.gpsimd
        def _(pool):
            pool.memset(G.ident[:], 0.0).then_inc(zeroed, 1)
            pool.wait_ge(zeroed, 1)
            pool.affine_select(out=G.ident[:], in_=G.ident[:], compare_op=ALU.not_equal, fill=1.0, base=0,
                               pattern=[[-1, P]], channel_multiplier=1).then_inc(zeroed, 1)
            pool.memset(G.halfpi[:], float(np.pi / 2)).then_inc(zeroed, 1)
            pool.wait_ge(zeroed, 3)


class Job:

    def __init__(self, products, cols, scale, bias, stores):
        self.products, self.cols, self.scale, self.bias, self.stores = products, cols, scale, bias, stores


def split_products(pe, jobs, ps, made, read):
    for j, job in enumerate(jobs):
        if j >= 2:
            pe.wait_ge(read, 3 * (j - 1))
        for n, (lhsT, rhs) in enumerate(job.products):
            mm = pe.matmul(ps[:, j % 2, 0:job.cols], lhsT, rhs, start=(n == 0), stop=(n == len(job.products) - 1))
        mm.then_inc(made, 1)


def split_read(act, jobs, ps, full, parts, made, read, split, stored):
    for j, job in enumerate(jobs):
        act.wait_ge(made, j + 1)
        if j >= 2:
            act.wait_ge(split, j - 1)
            act.wait_ge(stored[j % 2], 16 * len(job.stores) * (j // 2))
        c = job.cols
        for out in (full[:, j % 2, 0:c], parts[:, j % 2, 0, 0:c]):
            act.activation(out, ps[:, j % 2, 0:c], ACT.Identity, bias=job.bias if job.bias is not None else 0.0,
                           scale=job.scale).then_inc(read, 1)
        act.wait_ge(read, 3 * j + 2)
        act.sem_inc(read, 1)


def split_rest(dve, jobs, full, parts, read, rest, split):
    for j, job in enumerate(jobs):
        c = job.cols
        f, p1, p2, p3 = full[:, j % 2, 0:c], *(parts[:, j % 2, n, 0:c] for n in range(3))
        dve.wait_ge(read, 3 * j + 3)
        dve.tensor_tensor(f, f, p1, ALU.subtract).then_inc(rest, 1)
        dve.wait_ge(rest, 2 * j + 1)
        dve.tensor_copy(p2, f).then_inc(rest, 1)
        dve.wait_ge(rest, 2 * j + 2)
        dve.tensor_tensor(p3, f, p2, ALU.subtract).then_inc(split, 1)


def split_store(sp, jobs, parts, split, stored):
    for j, job in enumerate(jobs):
        sp.wait_ge(split, j + 1)
        for a, b, dst in job.stores:
            sp.dma_start(dst, parts[:, j % 2, :, a:b]).then_inc(stored[j % 2], 16)
    for par in range(2):
        n = sum(len(j.stores) for j in jobs[par::2])
        sp.wait_ge(stored[par], 16 * n)


def parts_view(dram, b, blk, a, n):
    return dram[:, b, blk * P:(blk + 1) * P, a:a + n].rearrange("t p c -> p t c")


def stage_project_self(nc, G):
    with ExitStack() as st:
        sem, sb, psum = makers(nc, st, "ps")
        resT = sb("resT", [96, TOK], F32)
        full = sb("split_full", [P, 2, CH], F32)
        parts = sb("split_parts", [P, 2, 3, CH], BF16)
        tmp = sb("cos_tmp", [96, 2, D], F32)
        ps = psum("ps_split", [P, 2, CH], F32)
        ps_res = psum("ps_res", [P, 2, CH], F32)
        ps_v = psum("ps_v", [P, 2, CH], F32)
        res_made, res_read, w_made, w_step, cos_done = sem("res_made"), sem("res_read"), sem("w_made"), sem("w_step"), sem("cos")
        made, read, rest, split = sem("made"), sem("read"), sem("rest"), sem("split")
        stored = [sem("stored0"), sem("stored1")]
        v_made, v_read = sem("v_made"), sem("v_read")
        jobs = []
        for which, dram, scale in ((0, G.q_dram, DH ** -0.5), (1, G.k_dram, 1.0)):
            for c in range(CHUNKS):
                for blk in range(2):
                    r = slice(HARM * which, HARM * which + HARM)
                    jobs.append(Job([(G.holo[r, 0, 0, blk * P:(blk + 1) * P], resT[r, c * CH:(c + 1) * CH])], CH, scale,
                                    None, [(0, CH, parts_view(dram, c // 2, blk, (c % 2) * CH, CH))]))
        block = st.enter_context(nc.Block())

        @block.tensor
        def _(pe):
            for c in range(CHUNKS):
                if c >= 2:
                    pe.wait_ge(res_read, c - 1)
                for k in range(2):
                    mm = pe.matmul(ps_res[0:96, c % 2, :], G.basis[:, k, 0:96], G.xT[:, k, c * CH:(c + 1) * CH],
                                   start=(k == 0), stop=(k == 1))
                mm.then_inc(res_made, 1)
            pe.wait_ge(w_made, 1)
            pe.wait_ge(res_read, CHUNKS)
            split_products(pe, jobs, ps, made, read)
            for t in range(TILES):
                if t >= 2:
                    pe.wait_ge(v_read, t - 1)
                pe.matmul(ps_v[:, t % 2, 0:D], resT[64:96, t * P:(t + 1) * P], G.holo[64:96, 0, 0, :],
                          start=True, stop=True).then_inc(v_made, 1)

        @block.vector
        def _(dve):
            link = linker(dve, w_step)
            for rows, o in ((96, 0), (HARM, 1)):
                ph, k = G.holo[0:rows, 0, o, :], tmp[0:rows, o, :]
                link(dve.tensor_scalar(k, ph, 1.0 / TWO_PI, 0.25, ALU.mult, ALU.add))
                link(dve.tensor_scalar(k, k, ROUND, None, ALU.add))
                link(dve.tensor_scalar(k, k, -ROUND, None, ALU.add))
                for cst in (C1, C2, C3):
                    link(dve.scalar_tensor_tensor(ph, k, -cst, ph, ALU.mult, ALU.add))
                link(dve.tensor_scalar(ph, ph, float(np.pi / 2), PI_IN, ALU.add, ALU.min))
                link(dve.tensor_scalar(ph, ph, -PI_IN, None, ALU.max))
            dve.wait_ge(cos_done, 2)
            link(dve.tensor_tensor(G.holo[0:HARM, 0, 1, :], G.holo[0:HARM, 0, 1, :], G.holo[0:HARM, 1, 1, :], ALU.mult))
            dve.tensor_tensor(G.holo[0:96, 0, 0, :], G.holo[0:96, 0, 0, :], G.holo[0:96, 1, 0, :],
                              ALU.mult).then_inc(w_made, 1)
            split_rest(dve, jobs, full, parts, read, rest, split)

        @block.scalar
        def _(act):
            for c in range(CHUNKS):
                act.wait_ge(res_made, c + 1)
                act.activation(resT[:, c * CH:(c + 1) * CH], ps_res[0:96, c % 2, :], ACT.Copy).then_inc(res_read, 1)
            act.wait_ge(w_step, 16)
            act.activation(G.holo[0:96, 0, 0, :], G.holo[0:96, 0, 0, :], ACT.Sin).then_inc(cos_done, 1)
            act.activation(G.holo[0:HARM, 0, 1, :], G.holo[0:HARM, 0, 1, :], ACT.Sin).then_inc(cos_done, 1)
            split_read(act, jobs, ps, full, parts, made, read, split, stored)
            for t in range(TILES):
                act.wait_ge(v_made, t + 1)
                b, tau = t // TPB, t % TPB
                act.activation(G.V[:, b * HEADS:(b + 1) * HEADS, tau, :],
                               ps_v[:, t % 2, 0:D].rearrange("p (h d) -> p h d", d=DH), ACT.Copy).then_inc(v_read, 1)

        @block.sync
        def _(sp):
            split_store(sp, jobs, parts, split, stored)


def stage_project_cross(nc, G, tag, mq, mk, mv, scale, bq, bk, bv_row):
    with ExitStack() as st:
        sem, sb, psum = makers(nc, st, tag)
        full = sb("split_full", [P, 2, CH], F32)
        parts = sb("split_parts", [P, 2, 3, CH], BF16)
        qb = sb("q_bias", [P, 2], F32)
        ps = psum("ps_split", [P, 2, CH], F32)
        ps_v = psum("ps_v", [P, 2, CH], F32)
        made, read, rest, split = sem("made"), sem("read"), sem("rest"), sem("split")
        stored = [sem("stored0"), sem("stored1")]
        v_made, v_read, qb_made = sem("v_made"), sem("v_read"), sem("qb_made")
        jobs = []
        for blk in range(2):
            cols = slice(blk * P, (blk + 1) * P)
            jobs.append(Job([(G.wmat[:, mk, k, cols], G.ctxT[:, k, :]) for k in range(2)], B * SK, 1.0,
                            None if bk is None else G.fvec[:, bk, blk:blk + 1],
                            [(b * SK, (b + 1) * SK, parts_view(G.kx_dram, b, blk, 0, SK)) for b in range(B)]))
        for c in range(CHUNKS):
            for blk in range(2):
                cols = slice(blk * P, (blk + 1) * P)
                half = [(h * CH // 2, (h + 1) * CH // 2) for h in range(2)]
                jobs.append(Job([(G.wmat[:, mq, k, cols], G.xT[:, k, c * CH:(c + 1) * CH]) for k in range(2)], CH, scale,
                                None if bq is None else qb[:, blk:blk + 1],
                                [(a, z, parts_view(G.qx_dram, c // 2, blk, (c % 2) * CH + a, z - a)) for a, z in half]))
        block = st.enter_context(nc.Block())
        vt = [(b, kt, a, n) for b in range(B) for kt, (a, n) in enumerate(((0, P), (P, SK - P)))]

        @block.tensor
        def _(pe):
            split_products(pe, jobs, ps, made, read)
            for j, (b, kt, a, n) in enumerate(vt):
                if j >= 2:
                    pe.wait_ge(v_read, j - 1)
                for k in range(2):
                    mm = pe.matmul(ps_v[0:n, j % 2, 0:D], G.ctxT[:, k, b * SK + a:b * SK + a + n], G.wmat[:, mv, k, :],
                                   start=(k == 0), stop=(k == 1))
                mm.then_inc(v_made, 1)

        @block.vector
        def _(dve):
            if bq is not None:
                dve.tensor_scalar(qb[:], G.fvec[:, bq, :], scale, None, ALU.mult).then_inc(qb_made, 1)
            split_rest(dve, jobs, full, parts, read, rest, split)
            for j, (b, kt, a, n) in enumerate(vt):
                dve.wait_ge(v_made, j + 1)
                out = G.Vx[0:n, b * HEADS:(b + 1) * HEADS, kt, :]
                src = ps_v[0:n, j % 2, 0:D].rearrange("p (h d) -> p h d", d=DH)
                if bv_row is None:
                    dve.tensor_copy(out, src).then_inc(v_read, 1)
                else:
                    dve.tensor_tensor(out, src, G.rvec[0:n, bv_row, :].rearrange("p (h d) -> p h d", d=DH),
                                      ALU.add).then_inc(v_read, 1)

        @block.scalar
        def _(act):
            if bq is not None:
                act.wait_ge(qb_made, 1)
            split_read(act, jobs, ps, full, parts, made, read, split, stored)

        @block.sync
        def _(sp):
            split_store(sp, jobs, parts, split, stored)


class Slot:

    def __init__(self, i, c):
        self.i, self.c = i, c

    def __add__(self, k):
        return Slot(self.i, self.c + k)

    def ring(self, n=4):
        return self.c % n

    def times(self, m, more=0):
        return self.i * (4 * m) + (self.c * m + more)

    def turn(self, m, more=0):
        return self.i * m + (self.c // 4 * m + more)


def head_cols(s):
    return bass.ds(s.times(DH), DH) if not isinstance(s.i, int) else slice(s.times(DH), s.times(DH) + DH)


def run_slots(eng, first, last, loop_from, loop_last, emit):
    for s in range(first, loop_from):
        emit(Slot(0, s))
    turns = (loop_last - loop_from + 1) // 4
    with eng.Fori(0, turns) as i:
        for u in range(4):
            emit(Slot(i, loop_from + u))
    for s in range(loop_from + 4 * turns, last + 1):
        emit(Slot(0, s))


def load_stacks(sp, n, q_stack, k_stack, q_dram, k_dram, cols, ready):
    r = n.ring()
    qd = q_dram.rearrange("t b (h d) c -> t (b h) d c", d=DH)
    kd = k_dram.rearrange("t b (h d) c -> t (b h) d c", d=DH)
    for dram, stack, table, w in ((qd, q_stack, Q_PART, S), (kd, k_stack, K_PART, cols)):
        row = 0
        for part, times in table:
            for _ in range(times):
                sp.dma_start(stack[row:row + DH, r, 0:w], dram[part, n.times(1)]).then_inc(ready[r], 16)
                row += DH
LOADS = sum(t for _, t in Q_PART) + sum(t for _, t in K_PART)


def stage_attention(nc, G, tag, self_attn, mask):
    keys = S if self_attn else SK
    ktiles = [(a, min(P, keys - a)) for a in range(0, keys, P)]
    NKT = len(ktiles)
    EB = 4 if self_attn else 2
    CONSTS = 5 if self_attn else 6
    UNITS = TPB if self_attn else 2
    QPU = TPB // UNITS
    STEP_O, STEP_M = min(2, NKT - 1), min(4, NKT - 1)
    q_dram, k_dram, V = (G.q_dram, G.k_dram, G.V) if self_attn else (G.qx_dram, G.kx_dram, G.Vx)
    with ExitStack() as st:
        sem, sb, psum = makers(nc, st, tag)
        q_stack = sb("q_stack", [P, 4, S], BF16)
        k_stack = sb("k_stack", [P, 4, keys], BF16)
        values = sb("values", [P, 4, NKT, VW], F32)
        probs = sb("probs", [P, EB, S], F32)
        neg_max = sb("neg_max", [P, 4, TPB], F32)
        max_rows = sb("max_rows", [TPB, 4, 2, P], BF16)
        out_raw = sb("out_raw", [P, 2, 2 * P], F32)
        inv_sum = sb("inv_sum", [P, 2, 2, 4], F32)
        mrow = sb("mrow", [1, B, 2, SK], F32)
        mrow_i = sb("mrow_i", [1, B, SK], I32)
        mrow_b = sb("mrow_b", [1, B, SK], BF16)
        pm = psum("ps_max", [P, 2, 2 * CH], F32)
        pscore = psum("ps_score", [P, 2, CH], F32)
        po = psum("ps_out", [P, CH], F32)
        pmisc = psum("ps_misc", [P, CH], F32)
        ready = [sem(f"stack{r}") for r in range(4)]
        rows_in = [sem(f"rows{r}") for r in range(4)]
        const, mask_in, mask_step = sem("const"), sem("mask_in"), sem("mask_step")
        max_made, max_done = sem("max_made"), sem("max_done")
        misc_made, misc_done = sem("misc_made"), sem("misc_done")
        row_hi, row_done = sem("row_hi"), sem("row_done")
        score_made, exp_done, pv_done = sem("score"), sem("exp"), sem("pv")
        out_read, recip, values_in = sem("out_read"), sem("recip"), sem("values_in")
        block = st.enter_context(nc.Block())

        def pos(x, n):
            return x.times(*n) if not isinstance(x.i, int) or x.times(*n) > 0 else None

        def wait(eng, s, v):
            if v is not None:
                eng.wait_ge(s, v)

        @block.sync
        def _(sp):
            sp.wait_ge(const, CONSTS)
            if mask:
                sp.dma_start(mrow_i[:], G.mask.rearrange("(o b) s -> o b s", o=1)).then_inc(mask_in, 16)
                sp.wait_ge(mask_step, 2)
                for r in range(4):
                    sp.dma_start(k_stack[MASKROW:MASKROW + 1, r, :], mrow_b[:, 0, :]).then_inc(mask_in, 16)
                sp.wait_ge(mask_in, 80)

            def rows(n):
                r = n.ring()
                sp.wait_ge(row_done, n.times(1, 1))
                for part in range(2):
                    sp.dma_start(q_stack[MAXROW + part:MAXROW + part + 1, r, :],
                                 max_rows[:, r, part, :]).then_inc(rows_in[r], 16)

            def slot(s):
                if s.c + 1 < SLOTS or not isinstance(s.i, int):
                    rows(s + 1)
                if s.c + 4 < SLOTS or not isinstance(s.i, int):
                    sp.wait_ge(pv_done, s.times(NKT, NKT))
                    if mask and isinstance(s.i, int) and HEADS <= s.c + 4 < HEADS + 4:
                        sp.dma_start(k_stack[MASKROW:MASKROW + 1, s.ring(), :], mrow_b[:, 1, :]).then_inc(mask_in, 16)
                        sp.wait_ge(mask_in, 96 + 16 * (s.c + 4 - HEADS))
                    load_stacks(sp, s + 4, q_stack, k_stack, q_dram, k_dram, keys, ready)

            for n in range(4):
                load_stacks(sp, Slot(0, n), q_stack, k_stack, q_dram, k_dram, keys, ready)
            rows(Slot(0, 0))
            if mask:
                run_slots(sp, 0, 11, 0, 11, slot)
                for s in range(12, 16):
                    slot(Slot(0, s))
                run_slots(sp, 16, SLOTS - 1, 16, SLOTS - 5, slot)
            else:
                run_slots(sp, 0, SLOTS - 1, 0, SLOTS - 5, slot)

        @block.gpsimd
        def _(pool):
            link = linker(pool, const)
            link(pool.memset(values[:], 0.0))
            link(pool.memset(q_stack[PROD:KROWS, :, :], 1.0))
            link(pool.memset(k_stack[PROD:KROWS, :, :], 1.0))
            if self_attn:
                link(pool.memset(k_stack[MASKROW:MASKROW + 1, :, :], 0.0))
                link(pool.memset(values[:, :, :, DH:DH + 1], 1.0))
            else:
                link(pool.memset(probs[:], 0.0))
                for kt, (a, n) in enumerate(ktiles):
                    link(pool.memset(values[0:n, :, kt, DH:DH + 1], 1.0))

            def copy_values(n):
                r = n.ring()
                if not isinstance(n.i, int) or n.c >= 4:
                    pool.wait_ge(pv_done, n.times(NKT, -3 * NKT))
                for kt, (a, m) in enumerate(ktiles) if not self_attn else ((0, (0, P)),):
                    src = V[0:m, n.times(1), kt:kt + 1, :] if not self_attn else V[:, n.times(1), :, :]
                    dst = values[0:m, r, kt:kt + 1, 0:DH] if not self_attn else values[:, r, :, 0:DH]
                    pool.tensor_copy(dst, src).then_inc(values_in, 1)
            run_slots(pool, 0, SLOTS - 1, 4, SLOTS - 1, copy_values)

        VCOP = 1 if self_attn else 2

        @block.tensor
        def _(pe):
            def max_unit(n, m):
                r, buf = n.ring(), (n.c * UNITS + m) % 2
                if m == 0:
                    pe.wait_ge(ready[r], n.turn(16 * LOADS, 16 * LOADS))
                wait(pe, max_done, pos(n, (UNITS, m - 1)))
                rows = PROD if self_attn else PROD + 1
                if self_attn:
                    for h in range(2):
                        mm = pe.matmul(pm[:, buf, h * CH:(h + 1) * CH], q_stack[0:rows, r, m * P:(m + 1) * P],
                                       k_stack[0:rows, r, h * CH:(h + 1) * CH], start=True, stop=True)
                else:
                    view = pm[:, buf, :].rearrange("p (q c) -> p q c", q=QPU)
                    for q in range(QPU):
                        t = m * QPU + q
                        mm = pe.matmul(view[:, q, 0:SK], q_stack[0:rows, r, t * P:(t + 1) * P], k_stack[0:rows, r, :],
                                       start=True, stop=True)
                mm.then_inc(max_made, 1)

            def max_turn(n, index):
                pe.wait_ge(max_done, n.times(UNITS, UNITS))
                if index is not None:
                    pe.wait_ge(misc_done, index)
                pe.transpose(pmisc[0:TPB, 0:P], neg_max[:, n.ring(), :], G.ident[:]).then_inc(misc_made, 1)

            def score(s, t, h):
                r, (a, m) = s.ring(), ktiles[t]
                g = 2 * t + h
                if g == 0:
                    pe.wait_ge(rows_in[r], s.turn(32, 32))
                wait(pe, exp_done, pos(s, (2 * NKT, g - 1)))
                pe.matmul(pscore[0:m, h, :], k_stack[0:KROWS, r, a:a + m], q_stack[0:KROWS, r, h * CH:(h + 1) * CH],
                          start=True, stop=True).then_inc(score_made, 1)

            def pv(s, t):
                if t == 0:
                    pe.wait_ge(values_in, s.times(VCOP, VCOP))
                    wait(pe, out_read, pos(s, (1, 0)))
                pe.wait_ge(exp_done, s.times(2 * NKT, 2 * t + 2))
                e = (s.c * NKT + t) % EB
                for j in range(4):
                    mm = pe.matmul(po[j * VW:(j + 1) * VW, 0:2 * P], values[:, s.ring(), t, :],
                                   probs[:, e, j * 2 * P:(j + 1) * 2 * P], start=(t == 0), stop=(t == NKT - 1))
                mm.then_inc(pv_done, 1)

            def out_turn(s, index):
                pe.wait_ge(out_read, s.times(1, 1))
                pe.wait_ge(misc_done, index)
                for h in range(2):
                    mm = pe.transpose(pmisc[:, h * P:(h + 1) * P], out_raw[:, s.ring(2), h * P:(h + 1) * P], G.ident[:])
                mm.then_inc(misc_made, 1)

            def slot(s):
                known = isinstance(s.i, int)
                first = known and s.c == 0
                for t in range(NKT):
                    score(s, t, 0)
                    score(s, t, 1)
                    if t == 0 and not first:
                        pv(s + -1, NKT - 1)
                    if t >= 1:
                        pv(s, t - 1)
                    if not known or s.c + 2 < SLOTS:
                        max_unit(s + 2, t)
                    if t == STEP_O and not first:
                        out_turn(s + -1, s.times(2, 0))
                    if t == STEP_M and (not known or s.c + 1 < SLOTS):
                        max_turn(s + 1, s.times(2, 1))

            pe.wait_ge(const, CONSTS)
            for n in range(2):
                for m in range(UNITS):
                    max_unit(Slot(0, n), m)
            max_turn(Slot(0, 0), None)
            run_slots(pe, 0, SLOTS - 1, 1, SLOTS - 4, slot)
            pv(Slot(0, SLOTS - 1), NKT - 1)
            out_turn(Slot(0, SLOTS - 1), 2 * SLOTS - 1)

        @block.scalar
        def _(act):
            def slot(s):
                for t, (a, m) in enumerate(ktiles):
                    e = (s.c * NKT + t) % EB
                    for h in range(2):
                        act.wait_ge(score_made, s.times(2 * NKT, 2 * t + h + 1))
                        if h == 0:
                            wait(act, pv_done, pos(s, (NKT, t + 1 - EB)))
                        act.activation(probs[0:m, e, h * CH:(h + 1) * CH], pscore[0:m, h, :],
                                       ACT.Exp).then_inc(exp_done, 1)
                    if t == 0 and not (isinstance(s.i, int) and s.c == 0):
                        read_out(s + -1)

            def read_out(s):
                act.wait_ge(pv_done, s.times(NKT, NKT))
                act.activation(out_raw[:, s.ring(2), :], po[:, 0:2 * P], ACT.Copy).then_inc(out_read, 1)

            if not self_attn:
                act.wait_ge(const, 4)
            run_slots(act, 0, SLOTS - 1, 1, SLOTS - 4, slot)
            read_out(Slot(0, SLOTS - 1))

        @block.vector
        def _(dve):
            if mask:
                dve.wait_ge(mask_in, 16)
                dve.tensor_copy(mrow[:, :, 0, :], mrow_i[:]).then_inc(mask_step, 1)
                dve.wait_ge(mask_step, 1)
                dve.tensor_scalar(mrow_b[:], mrow[:, :, 0, :], 0.0, -1e30, ALU.is_equal, ALU.mult).then_inc(mask_step, 1)

            def max_unit(n, m):
                buf = (n.c * UNITS + m) % 2
                dve.wait_ge(max_made, n.times(UNITS, m + 1))
                if self_attn:
                    src = pm[:, buf, :].rearrange("p (q c) -> p q c", q=1)
                else:
                    src = pm[:, buf, :].rearrange("p (q c) -> p q c", q=QPU)[:, :, 0:SK]
                dve.tensor_reduce(neg_max[:, n.ring(), m * QPU:(m + 1) * QPU], src, AX_X, ALU.max,
                                  negate=True).then_inc(max_done, 1)

            def max_row(n, index):
                r = n.ring()
                dve.wait_ge(misc_made, index)
                dve.tensor_copy(max_rows[:, r, 0, :], pmisc[0:TPB, 0:P]).then_inc(row_hi, 1)
                dve.wait_ge(row_hi, n.times(1, 1))
                dve.tensor_tensor(max_rows[:, r, 1, :], pmisc[0:TPB, 0:P], max_rows[:, r, 0, :],
                                  ALU.subtract).then_inc(row_done, 1)
                dve.wait_ge(row_done, n.times(1, 1))
                dve.sem_inc(misc_done, 1)

            def normalise(s, index):
                par = s.ring(2)
                dve.wait_ge(misc_made, index)
                sums = pmisc[:, 0:2 * P].rearrange("p (h j c) -> p h j c", h=2, j=4)
                dve.reciprocal(inv_sum[:, par], sums[:, :, :, DH:DH + 1]).then_inc(recip, 1)
                dve.wait_ge(recip, s.times(1, 1))
                dst = G.A[:, :, head_cols(s)].rearrange("p (j h) d -> p h j d", h=2)
                dve.tensor_tensor(dst, sums[:, :, :, 0:DH],
                                  inv_sum[:, par].rearrange("p h (j o) -> p h j o", o=1).broadcast_to([P, 2, 4, DH]),
                                  ALU.mult).then_inc(misc_done, 1)

            def slot(s):
                known = isinstance(s.i, int)
                for t in range(NKT):
                    if not known or s.c + 2 < SLOTS:
                        max_unit(s + 2, t)
                    if t == STEP_O and not (known and s.c == 0):
                        normalise(s + -1, s.times(2, 1))
                    if t == STEP_M and (not known or s.c + 1 < SLOTS):
                        max_row(s + 1, s.times(2, 2))

            for n in range(2):
                for m in range(UNITS):
                    max_unit(Slot(0, n), m)
            max_row(Slot(0, 0), 1)
            run_slots(dve, 0, SLOTS - 1, 1, SLOTS - 4, slot)
            normalise(Slot(0, SLOTS - 1), 2 * SLOTS)


def stage_attention_over_queries(nc, G):
    ktiles = [(0, P), (P, SK - P)]
    NKT = 2
    with ExitStack() as st:
        sem, sb, psum = makers(nc, st, "x0")
        q_stack = sb("q_stack", [P, 4, S], BF16)
        k_stack = sb("k_stack", [P, 4, SK], BF16)
        values = sb("values", [P, 4, NKT, VW], F32)
        probs = sb("probs", [P, 4, S], F32)
        neg_max = sb("neg_max", [P, 4, NKT], F32)
        row_sum = sb("row_sum", [P, 4, NKT], F32)
        inv_row = sb("inv_row", [P, 4, NKT], F32)
        out_raw = sb("out_raw", [P, 2, 2 * P], F32)
        inv_sum = sb("inv_sum", [P, 2, 2, 4], F32)
        pscore = psum("ps_score", [P, 2, 2 * CH], F32)
        po = psum("ps_out", [P, CH], F32)
        pt = psum("ps_turn", [P, CH], F32)
        ready = [sem(f"stack{r}") for r in range(4)]
        const = sem("const")
        score_made, max_done, exp_done, inv_done = sem("score"), sem("max"), sem("exp"), sem("inv")
        values_in, pv_done, out_read, turned, recip, filed = (sem("values_in"), sem("pv"), sem("out_read"),
                                                              sem("turned"), sem("recip"), sem("filed"))
        block = st.enter_context(nc.Block())

        @block.sync
        def _(sp):
            def slot(s):
                sp.wait_ge(score_made, s.times(NKT, NKT))
                load_stacks(sp, s + 4, q_stack, k_stack, G.qx_dram, G.kx_dram, SK, ready)
            for n in range(4):
                load_stacks(sp, Slot(0, n), q_stack, k_stack, G.qx_dram, G.kx_dram, SK, ready)
            run_slots(sp, 0, SLOTS - 5, 0, SLOTS - 5, slot)

        @block.gpsimd
        def _(pool):
            link = linker(pool, const)
            link(pool.memset(values[:], 0.0))
            link(pool.memset(probs[:], 0.0))

            def scale_values(n):
                r = n.ring()
                for kt, (a, m) in enumerate(ktiles):
                    pool.wait_ge(inv_done, n.times(NKT, kt + 1))
                    pool.tensor_tensor(values[0:m, r, kt, 0:DH], G.Vx[0:m, n.times(1), kt, :],
                                       inv_row[0:m, r, kt:kt + 1].broadcast_to([m, DH]), ALU.mult).then_inc(values_in, 1)
                    pool.tensor_copy(values[0:m, r, kt, DH:DH + 1], inv_row[0:m, r, kt:kt + 1]).then_inc(values_in, 1)
            run_slots(pool, 0, SLOTS - 1, 0, SLOTS - 1, scale_values)

        @block.tensor
        def _(pe):
            def scores(s):
                r = s.ring()
                pe.wait_ge(ready[r], s.turn(16 * LOADS, 16 * LOADS))
                for t, (a, m) in enumerate(ktiles):
                    if not isinstance(s.i, int) or s.c > 0:
                        pe.wait_ge(exp_done, s.times(NKT, t - 1))
                    for h in range(2):
                        mm = pe.matmul(pscore[0:m, t, h * CH:(h + 1) * CH], k_stack[0:PROD, r, a:a + m],
                                       q_stack[0:PROD, r, h * CH:(h + 1) * CH], start=True, stop=True)
                    mm.then_inc(score_made, 1)

            def products(s):
                if not isinstance(s.i, int) or s.c > 0:
                    pe.wait_ge(out_read, s.times(1))
                for t in range(NKT):
                    pe.wait_ge(values_in, s.times(2 * NKT, 2 * t + 2))
                    e = (s.c * NKT + t) % 4
                    for j in range(4):
                        mm = pe.matmul(po[j * VW:(j + 1) * VW, 0:2 * P], values[:, s.ring(), t, :],
                                       probs[:, e, j * 2 * P:(j + 1) * 2 * P], start=(t == 0), stop=(t == NKT - 1))
                mm.then_inc(pv_done, 1)

            def turn(s):
                pe.wait_ge(out_read, s.times(1, 1))
                if not isinstance(s.i, int) or s.c > 0:
                    pe.wait_ge(filed, s.times(1))
                for h in range(2):
                    mm = pe.transpose(pt[:, h * P:(h + 1) * P], out_raw[:, s.ring(2), h * P:(h + 1) * P], G.ident[:])
                mm.then_inc(turned, 1)

            def slot(s):
                scores(s)
                turn(s + -2)
                products(s + -1)
            pe.wait_ge(const, 2)
            scores(Slot(0, 0))
            scores(Slot(0, 1))
            products(Slot(0, 0))
            run_slots(pe, 2, SLOTS - 1, 2, SLOTS - 1, slot)
            turn(Slot(0, SLOTS - 2))
            products(Slot(0, SLOTS - 1))
            turn(Slot(0, SLOTS - 1))

        @block.scalar
        def _(act):
            def slot(s):
                for t, (a, m) in enumerate(ktiles):
                    act.wait_ge(max_done, s.times(NKT, t + 1))
                    if not isinstance(s.i, int) or s.c >= 2:
                        act.wait_ge(pv_done, s.times(1, -1))
                    act.activation(probs[0:m, (s.c * NKT + t) % 4, :], pscore[0:m, t, :], ACT.Exp,
                                   bias=neg_max[0:m, s.ring(), t:t + 1],
                                   accum_out=row_sum[0:m, s.ring(), t:t + 1]).then_inc(exp_done, 1)
                if not (isinstance(s.i, int) and s.c == 0):
                    read_out(s + -1)

            def read_out(s):
                act.wait_ge(pv_done, s.times(1, 1))
                act.activation(out_raw[:, s.ring(2), :], po[:, 0:2 * P], ACT.Copy).then_inc(out_read, 1)
            act.wait_ge(const, 2)
            run_slots(act, 0, SLOTS - 1, 2, SLOTS - 1, slot)
            read_out(Slot(0, SLOTS - 1))

        @block.vector
        def _(dve):
            def maxima(s):
                for t, (a, m) in enumerate(ktiles):
                    dve.wait_ge(score_made, s.times(NKT, t + 1))
                    dve.tensor_reduce(neg_max[0:m, s.ring(), t:t + 1], pscore[0:m, t, :], AX_X, ALU.max,
                                      negate=True).then_inc(max_done, 1)

            def invert(s):
                for t, (a, m) in enumerate(ktiles):
                    dve.wait_ge(exp_done, s.times(NKT, t + 1))
                    dve.reciprocal(inv_row[0:m, s.ring(), t:t + 1], row_sum[0:m, s.ring(), t:t + 1]).then_inc(inv_done, 1)

            def normalise(s):
                par = s.ring(2)
                dve.wait_ge(turned, s.times(1, 1))
                sums = pt[:, 0:2 * P].rearrange("p (h j c) -> p h j c", h=2, j=4)
                dve.reciprocal(inv_sum[:, par], sums[:, :, :, DH:DH + 1]).then_inc(recip, 1)
                dve.wait_ge(recip, s.times(1, 1))
                dst = G.A[:, :, head_cols(s)].rearrange("p (j h) d -> p h j d", h=2)
                dve.tensor_tensor(dst, sums[:, :, :, 0:DH],
                                  inv_sum[:, par].rearrange("p h (j o) -> p h j o", o=1).broadcast_to([P, 2, 4, DH]),
                                  ALU.mult).then_inc(filed, 1)

            def slot(s):
                maxima(s)
                invert(s)
                normalise(s + -2)
            for n in range(2):
                maxima(Slot(0, n))
                invert(Slot(0, n))
            run_slots(dve, 2, SLOTS - 1, 2, SLOTS - 1, slot)
            normalise(Slot(0, SLOTS - 2))
            normalise(Slot(0, SLOTS - 1))


def newton_rsqrt(dve, link, y, v, t):
    link(dve.tensor_scalar(v, v, EPS, None, ALU.add))
    link(dve.tensor_scalar(y.bitcast(I32), v.bitcast(I32), 1, None, ALU.logical_shift_right))
    link(dve.tensor_scalar(y.bitcast(I32), y.bitcast(I32), -1.0, RSQRT_MAGIC, ALU.mult, ALU.add))
    link(dve.tensor_scalar(v, v, -0.5, None, ALU.mult))
    for _ in range(3):
        link(dve.tensor_tensor(t, y, y, ALU.mult))
        link(dve.tensor_tensor(t, t, v, ALU.mult))
        link(dve.scalar_tensor_tensor(y, t, 1.5, y, ALU.add, ALU.mult))


def stage_turn(nc, G, tag):
    with ExitStack() as st:
        sem, sb, psum = makers(nc, st, tag)
        ps = psum("ps_turn", [P, 4, CH], F32)
        turned, read = sem("turned"), sem("read")
        block = st.enter_context(nc.Block())
        groups = [(c, blk) for c in range(CHUNKS) for blk in range(2)]

        @block.tensor
        def _(pe):
            for n, (c, blk) in enumerate(groups):
                if n >= 4:
                    pe.wait_ge(read, n - 3)
                for q in range(4):
                    t = 4 * c + q
                    b, tau = t // TPB, t % TPB
                    src = G.A[:, tau, b * D + blk * P:b * D + (blk + 1) * P]
                    mm = pe.transpose(ps[:, n % 4, q * P:(q + 1) * P], src, G.ident[:])
                mm.then_inc(turned, 1)

        @block.scalar
        def _(act):
            for n, (c, blk) in enumerate(groups):
                act.wait_ge(turned, n + 1)
                act.activation(G.AT[:, blk, c * CH:(c + 1) * CH], ps[:, n % 4, :], ACT.Copy).then_inc(read, 1)


def stage_out(nc, G, tag, products, row, keep=1.0, tiles=TILES):
    with ExitStack() as st:
        sem, sb, psum = makers(nc, st, tag)
        ps = psum("ps_y", [P, 4, CH], F32)
        made, added, biased, kept = sem("made"), sem("added"), sem("biased"), sem("kept")
        block = st.enter_context(nc.Block())

        @block.tensor
        def _(pe):
            for t in range(tiles):
                if t >= 4:
                    pe.wait_ge(added, t - 3)
                ops = products(t)
                for n, (lhsT, rhs) in enumerate(ops):
                    mm = pe.matmul(ps[:, t % 4, 0:D], lhsT, rhs, start=(n == 0), stop=(n == len(ops) - 1))
                mm.then_inc(made, 1)

        @block.gpsimd
        def _(pool):
            if row is not None:
                for t in range(tiles):
                    x = G.X[:, t, :]
                    if keep != 1.0:
                        pool.tensor_scalar(x, x, keep, None, ALU.mult).then_inc(kept, 1)
                        pool.wait_ge(kept, t + 1)
                    pool.tensor_tensor(x, x, G.rvec[:, row, :], ALU.add).then_inc(biased, 1)

        @block.vector
        def _(dve):
            for t in range(tiles):
                dve.wait_ge(made, t + 1)
                if row is not None:
                    dve.wait_ge(biased, t + 1)
                dve.tensor_tensor(G.X[:, t, :], ps[:, t % 4, 0:D], G.X[:, t, :], ALU.add).then_inc(added, 1)


def stage_resonance_out(nc, G):
    with ExitStack() as st:
        sem, sb, psum = makers(nc, st, "ro")
        ps = psum("ps_ro", [P, CHUNKS, CH], F32)
        made, read = sem("made"), sem("read")
        block = st.enter_context(nc.Block())

        @block.tensor
        def _(pe):
            for c in range(CHUNKS):
                for k in range(2):
                    mm = pe.matmul(ps[0:HARM, c, :], G.basis[:, k, 96:128], G.AT[:, k, c * CH:(c + 1) * CH],
                                   start=(k == 0), stop=(k == 1))
                mm.then_inc(made, 1)

        @block.scalar
        def _(act):
            for c in range(CHUNKS):
                act.wait_ge(made, c + 1)
                act.activation(G.ro[:, c * CH:(c + 1) * CH], ps[0:HARM, c, :], ACT.Copy).then_inc(read, 1)
            act.wait_ge(read, CHUNKS)


def stage_norm(nc, G, tag, src, tiles, width, dst, gain=None, shift=None, out=None, scratch=None):
    blks = width // P
    with ExitStack() as st:
        sem, sb, psum = makers(nc, st, tag)
        stats = sb("stats", [P, tiles, 6], F32)
        mv = sb("mean_var", [P, 2, tiles], F32)
        rstd = sb("rstd", [P, 2, tiles], F32)
        ps = psum("ps_turn", [P, 4, CH], F32)
        step, normed, turned, read, stored = sem("step"), sem("normed"), sem("turned"), sem("read"), sem("stored")
        block = st.enter_context(nc.Block())
        groups = [(g, blk) for g in range(tiles // 4) for blk in range(blks)]

        @block.vector
        def _(dve):
            link = linker(dve, step)
            for t in range(tiles):
                ins = dve.bn_stats(stats[:, t, :], src[:, t, 0:width])
                if t == tiles - 1:
                    link(ins)
            for t in range(tiles):
                ins = dve.bn_aggr(mv[:, :, t], stats[:, t, :])
                if t == tiles - 1:
                    link(ins)
            newton_rsqrt(dve, link, rstd[:, 0, :], mv[:, 1, :], rstd[:, 1, :])
            for t in range(tiles):
                dve.tensor_scalar(src[:, t, 0:width], src[:, t, 0:width], mv[:, 0, t:t + 1], rstd[:, 0, t:t + 1],
                                  ALU.subtract, ALU.mult).then_inc(normed, 1)

        if dst is not None:
            @block.tensor
            def _(pe):
                for n, (g, blk) in enumerate(groups):
                    pe.wait_ge(normed, 4 * g + 4)
                    if n >= 4:
                        pe.wait_ge(read, n - 3)
                    for q in range(4):
                        mm = pe.transpose(ps[:, n % 4, q * P:(q + 1) * P],
                                          src[:, 4 * g + q, blk * P:(blk + 1) * P], G.ident[:])
                    mm.then_inc(turned, 1)

            @block.scalar
            def _(act):
                for n, (g, blk) in enumerate(groups):
                    act.wait_ge(turned, n + 1)
                    out_ap = dst[:, blk, g * CH:(g + 1) * CH]
                    if gain is None:
                        act.activation(out_ap, ps[:, n % 4, :], ACT.Copy).then_inc(read, 1)
                    else:
                        act.activation(out_ap, ps[:, n % 4, :], ACT.Identity, bias=shift(blk, g),
                                       scale=gain(blk, g)).then_inc(read, 1)

        if scratch is not None or out is not None:
            @block.sync
            def _(sp):
                n = 0
                for t in range(0, TILES, 4):
                    sp.wait_ge(normed, t + 4)
                    for dram in (scratch, out):
                        if dram is not None:
                            sp.dma_start(dram[t:t + 4].rearrange("t p d -> p t d"), src[:, t:t + 4, :]).then_inc(stored, 16)
                            n += 16
                sp.wait_ge(stored, n)
                if out is not None:
                    sp.wait_ge(normed, tiles)


UNITS_A, UNITS_BC, UNITS_D = 4, 8, 2
UNITS = UNITS_A + 2 * UNITS_BC + UNITS_D
MB = HID // P


def stage_ffn0(nc, G):
    with ExitStack() as st:
        sem, sb, psum = makers(nc, st, "f0")
        raw = sb("w_raw", [P, 2, 1024], F32)
        w_hi, w_lo = sb("w_hi", [P, 2, 1024], F32R), sb("w_lo", [P, 2, 1024], F32R)
        x_hi, x_lo = sb("x_hi", [P, 2, CH], F32R), sb("x_lo", [P, 2, CH], F32R)
        h_hi, h_lo = sb("h_hi", [P, 2, MB, CH], F32R), sb("h_lo", [P, 2, MB, CH], F32R)
        full = sb("h_full", [P, 2, CH], F32)
        gate = sb("gate", [P, 2, CH], F32)
        y_tmp = sb("y_tmp", [P, 2, D], F32)
        pp = psum("ps_h", [P, 4, CH], F32)
        pd = psum("ps_y", [P, 4, CH], F32)
        w_in = [sem("w_in0"), sem("w_in1")]
        w_hi_done, w_lo_done = sem("w_hi"), sem("w_lo")
        x_hi_done, x_lo_done = sem("x_hi"), sem("x_lo")
        made, gate_done, full_done, hi_done, lo_done = sem("made"), sem("gate"), sem("full"), sem("hi"), sem("lo")
        y_made, y_done = sem("y_made"), sem("y_done")
        block = st.enter_context(nc.Block())
        TUR = 24
        units = G.ffn_units

        def each_chunk(eng, chunk):
            with eng.Fori(0, CHUNKS - 1) as c:
                chunk(c, False)
            chunk(CHUNKS - 1, True)

        @block.sync
        def _(sp):
            for u in range(2):
                sp.dma_start(raw[:, u, :], units[u]).then_inc(w_in[u], 16)

            def chunk(c, last):
                for u in range(UNITS - 2 * last):
                    sp.wait_ge(w_lo_done, c * UNITS + (u + 1))
                    sp.dma_start(raw[:, u % 2, :], units[(u + 2) % UNITS]).then_inc(w_in[u % 2], 16)
            each_chunk(sp, chunk)

        def split_hi(act, c, u):
            act.wait_ge(w_in[u % 2], c * (8 * UNITS) + 16 * (u // 2 + 1))
            act.activation(w_hi[:, u % 2, :], raw[:, u % 2, :], ACT.Copy).then_inc(w_hi_done, 1)

        def split_lo(dve, c, u):
            dve.wait_ge(w_hi_done, c * UNITS + (u + 1))
            dve.tensor_tensor(w_lo[:, u % 2, :], raw[:, u % 2, :], w_hi[:, u % 2, :].bitcast(F32),
                              ALU.subtract).then_inc(w_lo_done, 1)

        @block.tensor
        def _(pe):
            def three(out, wcols, slot, hi, lo, first, last):
                for n, (w, x) in enumerate(((w_hi, hi), (w_hi, lo), (w_lo, hi))):
                    mm = pe.matmul(out, w[:, slot, wcols], x, start=(first and n == 0), stop=(last and n == 2))
                return mm

            def chunk(c, last):
                for u in range(UNITS_A):
                    pe.wait_ge(w_lo_done, c * UNITS + (u + 1))
                    if u == 0:
                        pe.wait_ge(x_lo_done, c + 1)
                    for m in (2 * u, 2 * u + 1):
                        for w in range(2):
                            bank = 2 * m + w
                            if m >= 2:
                                pe.wait_ge(gate_done if w == 0 else full_done, c * 8 + (m - 1))
                            for k in range(2):
                                off = (m % 2) * 512 + w * 256 + k * P
                                mm = three(pp[:, bank % 4, :], slice(off, off + P), u % 2, x_hi[:, k, :], x_lo[:, k, :],
                                           k == 0, k == 1)
                            mm.then_inc(made, 1)
                for layer in range(2):
                    for m in range(MB):
                        u = UNITS_A + layer * UNITS_BC + m
                        tile = 8 + layer * 8 + m
                        pe.wait_ge(w_lo_done, c * UNITS + (u + 1))
                        if layer == 0 and m < 4:
                            pe.wait_ge(gate_done if m % 2 == 0 else full_done, c * 8 + (7 + m // 2))
                        else:
                            pe.wait_ge(hi_done, c * TUR + (tile - 3))
                        for k in range(MB):
                            if m == 0:
                                pe.wait_ge(lo_done, c * TUR + (layer * 8 + k + 1))
                            mm = three(pp[:, m % 4, :], slice(k * P, (k + 1) * P), u % 2, h_hi[:, layer, k, :],
                                       h_lo[:, layer, k, :], k == 0, k == MB - 1)
                        mm.then_inc(made, 1)
                for v in range(UNITS_D):
                    u = UNITS_A + 2 * UNITS_BC + v
                    pe.wait_ge(w_lo_done, c * UNITS + (u + 1))
                    for kk in range(4):
                        k = 4 * v + kk
                        pe.wait_ge(lo_done, c * TUR + (16 + k + 1))
                        for q in range(4):
                            for n, (h, w) in enumerate(((h_hi, w_hi), (h_hi, w_lo), (h_lo, w_hi))):
                                mm = pe.matmul(pd[:, q, 0:D], h[:, 0, k, q * P:(q + 1) * P],
                                               w[:, u % 2, kk * D:(kk + 1) * D], start=(k == 0 and n == 0),
                                               stop=(k == MB - 1 and n == 2))
                    mm.then_inc(y_made, 1)
            each_chunk(pe, chunk)

        MADE = 32

        @block.scalar
        def _(act):
            def free_hi(c, u, last):
                if last and u + 2 >= UNITS:
                    return
                if u < UNITS_A + 2 * UNITS_BC:
                    act.wait_ge(made, c * MADE + (4 * (u + 1) if u < UNITS_A else 16 + u - UNITS_A + 1))
                else:
                    act.wait_ge(y_made, c * 2 + (u - UNITS_A - 2 * UNITS_BC + 1))
                split_hi(act, c, u + 2)

            def chunk(c, last):
                act.activation(x_hi[:], G.xT[:, :, bass.ds(c * CH, CH)], ACT.Copy).then_inc(x_hi_done, 1)
                for u in range(UNITS_A):
                    for m in (2 * u, 2 * u + 1):
                        act.wait_ge(made, c * MADE + (2 * m + 1))
                        act.activation(gate[:, m % 2, :], pp[:, (2 * m) % 4, :], ACT.Silu,
                                       scale=G.ffn_s[:, 0, m:m + 1]).then_inc(gate_done, 1)
                        act.wait_ge(full_done, c * 8 + (m + 1))
                        act.activation(h_hi[:, 0, m, :], full[:, m % 2, :], ACT.Copy).then_inc(hi_done, 1)
                    free_hi(c, u, last)
                for layer in range(2):
                    for m in range(MB):
                        n = 8 + 8 * layer + m
                        act.wait_ge(made, c * MADE + (16 + 8 * layer + m + 1))
                        act.wait_ge(lo_done, c * TUR + (n - 1))
                        act.activation(full[:, m % 2, :], pp[:, m % 4, :], ACT.Gelu,
                                       scale=G.ffn_s[:, 2 + layer, m:m + 1])
                        act.activation(h_hi[:, 1 - layer, m, :], pp[:, m % 4, :], ACT.Gelu,
                                       scale=G.ffn_s[:, 2 + layer, m:m + 1]).then_inc(hi_done, 1)
                        free_hi(c, UNITS_A + layer * UNITS_BC + m, last)
                for v in range(UNITS_D):
                    free_hi(c, UNITS_A + 2 * UNITS_BC + v, last)
            for u in range(2):
                split_hi(act, 0, u)
            each_chunk(act, chunk)

        @block.vector
        def _(dve):
            def chunk(c, last):
                def next_lo(u):
                    if not (last and u + 2 >= UNITS):
                        split_lo(dve, c, u + 2)
                dve.wait_ge(x_hi_done, c + 1)
                dve.tensor_tensor(x_lo[:], G.xT[:, :, bass.ds(c * CH, CH)], x_hi[:].bitcast(F32),
                                  ALU.subtract).then_inc(x_lo_done, 1)
                for u in range(UNITS_A):
                    for m in (2 * u, 2 * u + 1):
                        dve.wait_ge(made, c * MADE + (2 * m + 2))
                        dve.wait_ge(gate_done, c * 8 + (m + 1))
                        dve.scalar_tensor_tensor(full[:, m % 2, :], pp[:, (2 * m + 1) % 4, :], G.ffn_s[:, 1, m:m + 1],
                                                 gate[:, m % 2, :], ALU.mult, ALU.mult).then_inc(full_done, 1)
                        dve.wait_ge(hi_done, c * TUR + (m + 1))
                        dve.tensor_tensor(h_lo[:, 0, m, :], full[:, m % 2, :], h_hi[:, 0, m, :].bitcast(F32),
                                          ALU.subtract).then_inc(lo_done, 1)
                    next_lo(u)
                for layer in range(2):
                    for m in range(MB):
                        dve.wait_ge(hi_done, c * TUR + (8 + 8 * layer + m + 1))
                        dve.tensor_tensor(h_lo[:, 1 - layer, m, :], full[:, m % 2, :],
                                          h_hi[:, 1 - layer, m, :].bitcast(F32), ALU.subtract).then_inc(lo_done, 1)
                        next_lo(UNITS_A + layer * UNITS_BC + m)
                next_lo(UNITS - 2)
                dve.wait_ge(y_made, c * 2 + 2)
                for q in range(4):
                    dve.tensor_tensor(y_tmp[:, q % 2, :], pd[:, q, 0:D], G.rvec[:, R_W3S, :], ALU.mult).then_inc(y_done, 1)
                    dve.wait_ge(y_done, c * 8 + (2 * q + 1))
                    dve.tensor_tensor(G.X[:, c * 4 + q, :], y_tmp[:, q % 2, :], G.X[:, c * 4 + q, :],
                                      ALU.add).then_inc(y_done, 1)
                next_lo(UNITS - 1)
            for u in range(2):
                split_lo(dve, 0, u)
            each_chunk(dve, chunk)


def stage_holographic(nc, G):
    with ExitStack() as st:
        sem, sb, psum = makers(nc, st, "lo")
        kq = sb("key_query", [P, 2, 2, CH], F32)
        val = sb("value", [P, 2, 2, CH], F32)
        th = sb("tanh", [P, 2, 2, 2, CH], F32)
        ph, turns = sb("phase", [P, 2, 2, CH], F32), sb("turns", [P, 2, 2, CH], F32)
        sn, cs = sb("sine", [P, 2, 2, CH], F32), sb("cosine", [P, 2, 2, CH], F32)
        bound, mem = sb("bound", [P, 2, 2, CH], F32), sb("memory", [P, 2, 2, CH], F32)
        keep = sb("keep", [P, CH], F32)
        vb = sb("value_bias", [P, 2], F32)
        ps = psum("ps_lo", [P, 8, CH], F32)
        const, made, read = sem("const"), sem("made"), sem("read")
        step, reduced, trig, magnitude = sem("step"), sem("reduced"), sem("trig"), sem("magnitude")
        bound_done, scanned, mixed, filed = sem("bound"), sem("scanned"), sem("mixed"), sem("filed")
        block = st.enter_context(nc.Block())
        TILES_C = 10
        units = [(c, blk) for c in range(CHUNKS) for blk in range(2)]

        @block.gpsimd
        def _(pool):
            pool.memset(keep[:], 1.0).then_inc(const, 1)
            pool.wait_ge(const, 1)
            pool.memset(keep[:].rearrange("p (g t) -> p g t", t=SCAN)[:, :, 0:1], 0.0).then_inc(const, 1)
            pool.tensor_scalar(vb[:], G.fvec[:, V_LBV, :], 1.0 / 16, None, ALU.mult).then_inc(const, 1)

            def bind(n):
                c, blk = units[n]
                pool.wait_ge(trig, 2 * n + 2)
                for part, src in enumerate((cs, sn)):
                    pool.tensor_tensor(bound[:, n % 2, part, :], val[:, c % 2, blk, :], src[:, n % 2, 0, :],
                                       ALU.mult).then_inc(bound_done, 1)

            def retrieve(n):
                pool.wait_ge(scanned, 2 * n + 2)
                for part, src in enumerate((cs, sn)):
                    pool.tensor_tensor(mem[:, n % 2, part, :], mem[:, n % 2, part, :], src[:, n % 2, 1, :],
                                       ALU.mult).then_inc(mixed, 1)
            for n in range(len(units)):
                bind(n)
                retrieve(n)

        @block.tensor
        def _(pe):
            n = 0
            for c in range(CHUNKS):
                for which, mat in enumerate((M_LK, M_LQ, M_LV, M_LKP, M_LQP)):
                    for blk in range(2):
                        if n >= 8:
                            pe.wait_ge(read, n - 7)
                        if which >= 3:
                            pe.wait_ge(read, c * TILES_C + (2 if which == 3 else 4))
                        for k in range(2):
                            rhs = kq[:, which - 3, k, :] if which >= 3 else G.xT[:, k, c * CH:(c + 1) * CH]
                            mm = pe.matmul(ps[:, n % 8, :], G.wmat[:, mat, k, blk * P:(blk + 1) * P], rhs,
                                           start=(k == 0), stop=(k == 1))
                        mm.then_inc(made, 1)
                        n += 1

        @block.scalar
        def _(act):
            act.wait_ge(const, 3)

            def trigonometry(n):
                act.wait_ge(reduced, n + 1)
                if n >= 2:
                    act.wait_ge(mixed, 2 * n - 2)
                act.activation(turns[:, n % 2], ph[:, n % 2], ACT.Abs).then_inc(magnitude, 1)
                act.activation(sn[:, n % 2], ph[:, n % 2], ACT.Sin).then_inc(trig, 1)
                act.wait_ge(magnitude, n + 1)
                act.activation(cs[:, n % 2], turns[:, n % 2], ACT.Sin, bias=G.halfpi[:, 0:1],
                               scale=-1.0).then_inc(trig, 1)
            n = 0
            for c in range(CHUNKS):
                for which, vec in enumerate((V_LBK, V_LBQ, V_LBV, V_LBKP, V_LBQP)):
                    for blk in range(2):
                        act.wait_ge(made, n + 1)
                        src = ps[:, n % 8, :]
                        if which < 2:
                            act.activation(kq[:, which, blk, :], src, ACT.Identity,
                                           bias=G.fvec[:, vec, blk:blk + 1]).then_inc(read, 1)
                        elif which == 2:
                            if c >= 2:
                                act.wait_ge(bound_done, 4 * (c - 1))
                            act.activation(val[:, c % 2, blk, :], src, ACT.Identity, bias=vb[:, blk:blk + 1],
                                           scale=1.0 / 16).then_inc(read, 1)
                        else:
                            if c >= 2:
                                act.wait_ge(reduced, 2 * (c - 1))
                            act.activation(th[:, c % 2, which - 3, blk, :], src, ACT.Tanh,
                                           bias=G.fvec[:, vec, blk:blk + 1]).then_inc(read, 1)
                        n += 1
                if c >= 1:
                    trigonometry(2 * c - 2)
                    trigonometry(2 * c - 1)
            trigonometry(2 * CHUNKS - 2)
            trigonometry(2 * CHUNKS - 1)

        @block.vector
        def _(dve):
            link = linker(dve, step)

            def reduce_phase(n):
                c, blk = units[n]
                dve.wait_ge(read, (c + 1) * TILES_C - (1 - blk))
                if n >= 2:
                    dve.wait_ge(trig, 2 * n - 2)
                p, k = ph[:, n % 2], turns[:, n % 2]
                link(dve.tensor_scalar(p, th[:, c % 2, :, blk, :], G.fvec[:, V_PS, blk:blk + 1], None, ALU.mult))
                link(dve.tensor_scalar(k, p, 1.0 / TWO_PI, ROUND, ALU.mult, ALU.add))
                link(dve.tensor_scalar(k, k, -ROUND, None, ALU.add))
                for cst in (C1, C2, C3):
                    link(dve.scalar_tensor_tensor(p, k, -cst, p, ALU.mult, ALU.add))
                dve.tensor_scalar(p, p, PI_IN, -PI_IN, ALU.min, ALU.max).then_inc(reduced, 1)

            def scan(n):
                dve.wait_ge(bound_done, 2 * n + 2)
                if n >= 2:
                    dve.wait_ge(filed, n - 1)
                for part in range(2):
                    dve.tensor_tensor_scan(mem[:, n % 2, part, :], keep[:], bound[:, n % 2, part, :], 0.0,
                                           ALU.mult, ALU.add).then_inc(scanned, 1)

            def file(n):
                c, blk = units[n]
                dve.wait_ge(mixed, 2 * n + 2)
                dve.tensor_tensor(G.AT[:, blk, c * CH:(c + 1) * CH], mem[:, n % 2, 0, :], mem[:, n % 2, 1, :],
                                  ALU.add).then_inc(filed, 1)
            N = len(units)
            dve.wait_ge(const, 3)
            for n in range(N + 2):
                if n < N:
                    reduce_phase(n)
                if 1 <= n <= N:
                    scan(n - 1)
                if n >= 2:
                    file(n - 2)


def stage_turn_back(nc, G, tag, src, tiles, dst):
    with ExitStack() as st:
        sem, sb, psum = makers(nc, st, tag)
        ps = psum("ps_back", [P, 4, CH], F32)
        turned, read = sem("turned"), sem("read")
        block = st.enter_context(nc.Block())

        @block.tensor
        def _(pe):
            for n in range(tiles // 2):
                if n >= 4:
                    pe.wait_ge(read, n - 3)
                for q in range(2):
                    for k in range(2):
                        t = 2 * n + q
                        mm = pe.transpose(ps[:, n % 4, q * D + k * P:q * D + (k + 1) * P], src[:, k, t * P:(t + 1) * P],
                                          G.ident[:])
                mm.then_inc(turned, 1)

        @block.scalar
        def _(act):
            for n in range(tiles // 2):
                act.wait_ge(turned, n + 1)
                act.activation(dst[:, 2 * n:2 * n + 2, :].rearrange("p t d -> p (t d)"), ps[:, n % 4, :],
                               ACT.Copy).then_inc(read, 1)


def stage_gather(nc, I, G):
    with ExitStack() as st:
        sem, sb, psum = makers(nc, st, "ga")
        col_i = sb("col_i", [P, 2, MT], I32)
        row_i = sb("row_i", [P, 2, NMOE], I32)
        col_f, row_f = sb("col_f", [P, 2, MT], F32), sb("row_f", [P, 2, NMOE], F32)
        rows = sb("row_token", [P, NMOE], F32)
        same = sb("same", [P, MT, NMOE], F32)
        dup = sb("dup", [P, MT], F32)
        loaded, gathered = sem("loaded"), sem("gathered")
        step, same_done, kept, turned, read = sem("step"), sem("same"), sem("kept"), sem("turned"), sem("read")
        tok_done = sem("tok")
        ps = psum("ps_ga", [P, 2, CH], F32)
        block = st.enter_context(nc.Block())

        @block.sync
        def _(sp):
            for n, name in enumerate(("index_b", "index_t")):
                with nc.allow_non_contiguous_dma(reason="512 indices"):
                    sp.dma_start(col_i[:, n, :], I[name].rearrange("(q p) -> p q", p=P)).then_inc(loaded, 16)
                sp.dma_start(row_i[:, n, :], I[name].rearrange("(o m) -> o m", o=1).broadcast_to([P, NMOE])).then_inc(loaded, 16)
            for k in range(2):
                sp.dma_start(G.ew1[:, k, :], I["ew1"][k]).then_inc(loaded, 16)
                sp.dma_start(G.ew2[:, k, :], I["ew2"][k]).then_inc(loaded, 16)
            sp.dma_start(G.ew3[:], I["ew3"]).then_inc(loaded, 16)
            sp.dma_start(G.sw12[:], I["sw12"].rearrange("k p c -> p k c")).then_inc(loaded, 16)
            sp.dma_start(G.sw3[:], I["sw3"]).then_inc(loaded, 16)
            sp.dma_start(G.gw[:], I["gw"].rearrange("k p c -> p k c")).then_inc(loaded, 16)
            sp.dma_start(G.eb[:], I["eb"]).then_inc(loaded, 16)
            sp.wait_ge(loaded, 16 * 13)

        @block.vector
        def _(dve):
            link = linker(dve, step)
            dve.wait_ge(loaded, 16 * 13)
            link(dve.tensor_copy(col_f[:], col_i[:]))
            link(dve.tensor_copy(row_f[:], row_i[:]))
            link(dve.scalar_tensor_tensor(G.tok_f[:], col_f[:, 0, :], float(S), col_f[:, 1, :], ALU.mult, ALU.add))
            dve.tensor_copy(G.tok[:], G.tok_f[:]).then_inc(tok_done, 1)
            link(dve.scalar_tensor_tensor(rows[:], row_f[:, 0, :], float(S), row_f[:, 1, :], ALU.mult, ALU.add))
            for q in range(MT):
                dve.tensor_scalar(same[:, q, :], rows[:], G.tok_f[:, q:q + 1], None, ALU.is_equal).then_inc(same_done, 1)
            dve.wait_ge(kept, MT)
            link(dve.tensor_reduce(dup[:], same[:], AX_X, ALU.max))
            link(dve.scalar_tensor_tensor(G.tok_f[:], dup[:], float(2 * TOK), G.tok_f[:], ALU.mult, ALU.add))
            link(dve.tensor_copy(G.tok_once[:], G.tok_f[:]))

        @block.gpsimd
        def _(pool):
            pool.wait_ge(tok_done, 1)
            for q in range(MT):
                pool.indirect_dma_start(G.X[:, TILES + q, :], None, G.x_dram.rearrange("t p d -> (t p) d"),
                                        bass.IndirectOffsetOnAxis(ap=G.tok[:, q:q + 1], axis=0)).then_inc(gathered, 16)
            for q in range(MT):
                pool.wait_ge(same_done, q + 1)
                pool.affine_select(out=same[:, q, :], in_=same[:, q, :], compare_op=ALU.is_gt, fill=0.0, base=q * P,
                                   pattern=[[-1, NMOE]], channel_multiplier=1).then_inc(kept, 1)

        @block.tensor
        def _(pe):
            pe.wait_ge(gathered, 16 * MT)
            for blk in range(2):
                for q in range(MT):
                    mm = pe.transpose(ps[:, blk, q * P:(q + 1) * P], G.X[:, TILES + q, blk * P:(blk + 1) * P], G.ident[:])
                mm.then_inc(turned, 1)

        @block.scalar
        def _(act):
            for blk in range(2):
                act.wait_ge(turned, blk + 1)
                act.activation(G.xT[:, blk, TOK:TOK + NMOE], ps[:, blk, :], ACT.Copy).then_inc(read, 1)


def stage_shared_hidden(nc, G):
    with ExitStack() as st:
        sem, sb, psum = makers(nc, st, "sh")
        h = sb("sh_h", [P, 4, D], F32)
        ps = psum("ps_sh", [P, 4, CH], F32)
        made, biased, silu, z_done = sem("made"), sem("biased"), sem("silu"), sem("z")
        block = st.enter_context(nc.Block())

        @block.tensor
        def _(pe):
            for t in range(XT):
                if t >= 4:
                    pe.wait_ge(biased, t - 3)
                for k in range(2):
                    mm = pe.matmul(ps[:, t % 4, 0:D], G.xT[:, k, t * P:(t + 1) * P], G.sw12[:, k, :],
                                   start=(k == 0), stop=(k == 1))
                mm.then_inc(made, 1)

        @block.vector
        def _(dve):
            for t in range(XT):
                dve.wait_ge(made, t + 1)
                if t >= 4:
                    dve.wait_ge(z_done, t - 3)
                dve.tensor_tensor(h[:, t % 4, :], ps[:, t % 4, 0:D], G.rvec[:, R_SB12, :], ALU.add).then_inc(biased, 1)

        @block.scalar
        def _(act):
            for t in range(XT):
                act.wait_ge(biased, t + 1)
                act.activation(G.Z[:, t, :], h[:, t % 4, 0:EH], ACT.Silu).then_inc(silu, 1)

        @block.gpsimd
        def _(pool):
            for t in range(XT):
                pool.wait_ge(silu, t + 1)
                pool.tensor_tensor(G.Z[:, t, :], G.Z[:, t, :], h[:, t % 4, EH:D], ALU.mult).then_inc(z_done, 1)


def stage_shared_out(nc, G):
    with ExitStack() as st:
        sem, sb, psum = makers(nc, st, "so")
        ps = psum("ps_so", [P, 4, CH], F32)
        made, added, biased = sem("made"), sem("added"), sem("biased")
        block = st.enter_context(nc.Block())

        @block.tensor
        def _(pe):
            for t in range(XT):
                if t >= 4:
                    pe.wait_ge(added, t - 3)
                pe.matmul(ps[:, t % 4, 0:D], G.ZT[:, 0, t * P:(t + 1) * P], G.sw3[:], start=True, stop=True).then_inc(made, 1)

        @block.gpsimd
        def _(pool):
            for t in range(TILES):
                pool.tensor_tensor(G.X[:, t, :], G.X[:, t, :], G.rvec[:, R_SB3, :], ALU.add).then_inc(biased, 1)

        @block.vector
        def _(dve):
            for t in range(XT):
                dve.wait_ge(made, t + 1)
                if t < TILES:
                    dve.wait_ge(biased, t + 1)
                    dve.tensor_tensor(G.X[:, t, :], ps[:, t % 4, 0:D], G.X[:, t, :], ALU.add).then_inc(added, 1)
                else:
                    dve.tensor_tensor(G.shared_g[:, t - TILES, :], ps[:, t % 4, 0:D], G.rvec[:, R_SB3, :],
                                      ALU.add).then_inc(added, 1)


def stage_experts(nc, G):
    with ExitStack() as st:
        sem, sb, psum = makers(nc, st, "ex")
        logits, scores = sb("logits", [P, MT, 9], F32), sb("scores", [P, MT, 9], F32)
        choice, best = sb("choice", [P, MT, NEXP], F32), sb("best", [P, MT, NEXP], F32)
        best_i = sb("best_i", [P, MT, NEXP], U32)
        best_f = sb("best_f", [P, MT], F32)
        lane_i, lane = sb("lane_i", [P, NEXP], I32), sb("lane", [P, NEXP], F32)
        onehot = sb("onehot", [P, MT, NEXP], F32)
        onehotT = sb("onehotT", [NEXP, MT, P], F32)
        pair, top = sb("pair", [P, MT, 2], F32), sb("top", [P, MT, NEXP], F32)
        pmax, psums = sb("pmax", [P, MT], F32), sb("psums", [P, MT], F32)
        bias = sb("bias", [P, MT, 2 * D], F32)
        hsel = sb("hsel", [P, MT, 2, EH], F32)
        ze = sb("ze", [P, MT, EH], F32)
        zeT = sb("zeT", [P, NMOE], F32)
        yexp = sb("yexp", [P, MT, D], F32)
        stats, mv, rstd = sb("stats", [P, MT, 6], F32), sb("mv", [P, 2, MT], F32), sb("rstd", [P, 2, MT], F32)
        ph = psum("ps_h", [P, 4, CH], F32)
        pg = psum("ps_g", [P, CH], F32)
        pt = psum("ps_t", [P, CH], F32)
        pb = psum("ps_b", [P, CH], F32)
        step, gates_made, logit_done, score_done, hot_done = sem("step"), sem("gates"), sem("logit"), sem("score"), sem("hot")
        hotT_made, hotT_read, bias_made, bias_read = sem("hotT"), sem("hotTr"), sem("biasm"), sem("biasr")
        h_made, h_read, silu, z_normed, zT_made, zT_read = sem("h"), sem("hr"), sem("silu"), sem("zn"), sem("zT"), sem("zTr")
        y_made, y_read, lanes, pmax_done, pair_done = sem("y"), sem("yr"), sem("lanes"), sem("pmax"), sem("pair")
        block = st.enter_context(nc.Block())

        @block.gpsimd
        def _(pool):
            pool.iota(lane_i[:], pattern=[[1, NEXP]], base=0, channel_multiplier=0).then_inc(lanes, 1)

        @block.tensor
        def _(pe):
            for q in range(MT):
                for k in range(2):
                    mm = pe.matmul(pg[:, q * 16:q * 16 + 9], G.xT[:, k, TOK + q * P:TOK + (q + 1) * P], G.gw[:, k, :],
                                   start=(k == 0), stop=(k == 1))
            mm.then_inc(gates_made, 1)
            for q in range(MT):
                if q >= 1:
                    pe.wait_ge(h_read, q)
                for w, wt in enumerate((G.ew1, G.ew2)):
                    for h in range(2):
                        for k in range(2):
                            mm = pe.matmul(ph[:, 2 * w + h, :], G.xT[:, k, TOK + q * P:TOK + (q + 1) * P],
                                           wt[:, k, h * CH:(h + 1) * CH], start=(k == 0), stop=(k == 1))
                mm.then_inc(h_made, 1)
                if q == 0:
                    pe.wait_ge(hot_done, 1)
                    for p in range(MT):
                        mm2 = pe.transpose(pt[0:NEXP, p * P:(p + 1) * P], onehot[:, p, :], G.ident[:])
                    mm2.then_inc(hotT_made, 1)
                    pe.wait_ge(hotT_read, 1)
                if q >= 1:
                    pe.wait_ge(bias_read, q)
                pe.matmul(pb[:], onehotT[:, q, :], G.eb[:], start=True, stop=True).then_inc(bias_made, 1)
            for q in range(MT):
                pe.wait_ge(z_normed, q + 1)
                pe.transpose(pt[:, q * P:(q + 1) * P], ze[:, q, :], G.ident[:]).then_inc(zT_made, 1)
            pe.wait_ge(h_read, MT)
            pe.wait_ge(zT_read, 1)
            for q in range(MT):
                if q >= 1:
                    pe.wait_ge(y_read, q)
                for h in range(4):
                    mm = pe.matmul(ph[:, h, :], zeT[:, q * P:(q + 1) * P], G.ew3[:, h * CH:(h + 1) * CH], start=True, stop=True)
                mm.then_inc(y_made, 1)

        @block.scalar
        def _(act):
            act.wait_ge(logit_done, 1)
            act.activation(scores[:], logits[:], ACT.Sigmoid).then_inc(score_done, 1)
            act.wait_ge(hotT_made, 1)
            act.activation(onehotT[:], pt[0:NEXP, :].rearrange("e (q p) -> e q p", q=MT), ACT.Copy).then_inc(hotT_read, 1)
            for q in range(MT):
                act.wait_ge(bias_made, q + 1)
                act.activation(bias[:, q, :], pb[:], ACT.Copy).then_inc(bias_read, 1)
                act.wait_ge(h_read, q + 1)
                act.activation(ze[:, q, :], hsel[:, q, 0, :], ACT.Silu).then_inc(silu, 1)
            act.wait_ge(pmax_done, 1)
            for q in range(MT):
                act.activation(pair[:, q, :], pair[:, q, :], ACT.Exp, bias=pmax[:, q:q + 1],
                               accum_out=psums[:, q:q + 1]).then_inc(pair_done, 1)
            act.wait_ge(zT_made, MT)
            act.activation(zeT[:], pt[:], ACT.Identity, bias=G.evec[:, 3:4], scale=G.evec[:, 2:3]).then_inc(zT_read, 1)

        @block.vector
        def _(dve):
            link = linker(dve, step)
            link(dve.memset(pair[:], 0.0))
            dve.wait_ge(lanes, 1)
            link(dve.tensor_copy(lane[:], lane_i[:]))
            dve.wait_ge(gates_made, 1)
            dve.tensor_tensor(logits[:], pg[:, 0:16 * MT].rearrange("p (q c) -> p q c", q=MT)[:, :, 0:9],
                              G.grow[:, 0:9].rearrange("p (o c) -> p o c", o=1).broadcast_to([P, MT, 9]),
                              ALU.add).then_inc(logit_done, 1)
            dve.wait_ge(score_done, 1)
            link(dve.tensor_tensor(choice[:], scores[:, :, 1:9],
                                   G.grow[:, 9:17].rearrange("p (o c) -> p o c", o=1).broadcast_to([P, MT, NEXP]), ALU.add))
            for q in range(MT):
                link(dve.max(best[:, q, :], choice[:, q, :]))
                link(dve.max_index(best_i[:, q, :], best[:, q, :], choice[:, q, :]))
            link(dve.tensor_copy(best_f[:], best_i[:, :, 0]))
            for q in range(MT):
                link(dve.tensor_scalar(onehot[:, q, :], lane[:], best_f[:, q:q + 1], None, ALU.is_equal))
            dve.sem_inc(hot_done, 1)
            link(dve.tensor_tensor(top[:], scores[:, :, 1:9], onehot[:], ALU.mult))
            link(dve.tensor_copy(pair[:, :, 0:1], scores[:, :, 0:1]))
            link(dve.tensor_reduce(pair[:, :, 1:2], top[:], AX_X, ALU.add))
            dve.tensor_reduce(pmax[:], pair[:], AX_X, ALU.max, negate=True).then_inc(pmax_done, 1)
            for q in range(MT):
                dve.wait_ge(h_made, q + 1)
                dve.wait_ge(bias_read, q + 1)
                for w in range(2):
                    out = hsel[:, q, w, :]
                    for e in range(NEXP):
                        src = ph[:, 2 * w + e // 4, (e % 4) * EH:(e % 4 + 1) * EH]
                        prev = bias[:, q, w * EH:(w + 1) * EH] if e == 0 else out
                        link(dve.scalar_tensor_tensor(out, src, onehot[:, q, e:e + 1], prev, ALU.mult, ALU.add))
                dve.sem_inc(h_read, 1)
                dve.wait_ge(silu, q + 1)
                link(dve.tensor_tensor(ze[:, q, :], ze[:, q, :], hsel[:, q, 1, :], ALU.mult))
                link(dve.bn_stats(stats[:, q, :], ze[:, q, :]))
                link(dve.bn_aggr(mv[:, :, q], stats[:, q, :]))
            newton_rsqrt(dve, link, rstd[:, 0, :], mv[:, 1, :], rstd[:, 1, :])
            for q in range(MT):
                dve.tensor_scalar(ze[:, q, :], ze[:, q, :], mv[:, 0, q:q + 1], rstd[:, 0, q:q + 1],
                                  ALU.subtract, ALU.mult).then_inc(z_normed, 1)
            dve.wait_ge(pair_done, MT)
            link(dve.reciprocal(psums[:], psums[:]))
            link(dve.tensor_tensor(pair[:], pair[:], psums[:].rearrange("p (q o) -> p q o", o=1).broadcast_to([P, MT, 2]),
                                   ALU.mult))
            for q in range(MT):
                dve.wait_ge(y_made, q + 1)
                for e in range(NEXP):
                    src = ph[:, e // 2, (e % 2) * D:(e % 2 + 1) * D]
                    prev = bias[:, q, D:2 * D] if e == 0 else yexp[:, q, :]
                    link(dve.scalar_tensor_tensor(yexp[:, q, :], src, onehot[:, q, e:e + 1], prev, ALU.mult, ALU.add))
                dve.sem_inc(y_read, 1)
                x = G.X[:, TILES + q, :]
                link(dve.scalar_tensor_tensor(x, G.shared_g[:, q, :], pair[:, q, 0:1], x, ALU.mult, ALU.add))
                link(dve.scalar_tensor_tensor(x, yexp[:, q, :], pair[:, q, 1:2], x, ALU.mult, ALU.add))


def stage_scatter(nc, G, out):
    with ExitStack() as st:
        done = st.enter_context(nc.semaphore("sc_done"))
        block = st.enter_context(nc.Block())

        @block.gpsimd
        def _(pool):
            for q in range(MT):
                pool.indirect_dma_start(out.rearrange("t p d -> (t p) d"),
                                        bass.IndirectOffsetOnAxis(ap=G.tok_once[:, q:q + 1], axis=0),
                                        G.X[:, TILES + q, :], None, bounds_check=TOK - 1, oob_is_err=False).then_inc(done, 16)
            pool.wait_ge(done, 16 * MT)


class Shared:

    def __init__(self, nc, st):
        sb = lambda *a: st.enter_context(nc.sbuf_tensor(*a))
        self.X = sb("X", [P, XT, D], F32)
        self.xT = sb("xT", [P, 2, TOK + NMOE], F32)
        self.ident = sb("ident", [P, P], F32)
        self.halfpi = sb("halfpi", [P, 1], F32)
        self.wmat = sb("wmat", [P, 14, 2, D], F32)
        self.fvec, self.evec = sb("fvec", [P, 10, 2], F32), sb("evec", [P, 4], F32)
        self.rvec, self.grow = sb("rvec", [P, NROWS, D], F32), sb("grow", [P, 17], F32)
        self.ffn_s = sb("ffn_s", [P, 4, MB], F32)
        self.tok, self.tok_once, self.tok_f = sb("tok", [P, MT], U32), sb("tok_once", [P, MT], U32), sb("tok_f", [P, MT], F32)
        dram = lambda name, shape, dt: nc.dram_tensor(name, shape, dt).ap()
        self.q_dram = dram("q_parts", [3, B, D, S], BF16)
        self.k_dram = dram("k_parts", [3, B, D, S], BF16)
        self.qx_dram = dram("qx_parts", [3, B, D, S], BF16)
        self.kx_dram = dram("kx_parts", [3, B, D, SK], BF16)
        self.x_dram = dram("x_rows", [TILES, P, D], F32)


def decoder_kernel(nc, I, out):
    with ExitStack() as st:
        G = Shared(nc, st)
        G.ffn_units, G.mask = I["ffn_units"], I["mask"]
        tile = lambda t: slice(t * P, (t + 1) * P)

        def out_products(mat):
            return lambda t: [(G.AT[:, k, tile(t)], G.wmat[:, mat, k, :]) for k in range(2)]

        def norm_x(tag, **kw):
            stage_norm(nc, G, tag, G.X, TILES, D, G.xT, **kw)

        with ExitStack() as st0:
            sb = lambda *a: st0.enter_context(nc.sbuf_tensor(*a))
            G.basis, G.holo = sb("basis", [P, 2, P], F32), sb("holo", [96, 2, 2, D], F32)
            G.V = sb("V", [P, SLOTS, TPB, DH], F32)
            G.ctxT, G.Vx = sb("ctxT", [P, 2, B * SK], F32), sb("Vx", [P, SLOTS, 2, DH], F32)
            G.ro = sb("ro", [HARM, TOK], F32)
            G.A, G.AT = sb("A", [P, TPB, B * D], F32), sb("AT", [P, 2, TOK], F32)
            stage_setup(nc, I, G)
            stage_project_self(nc, G)
            stage_attention(nc, G, "a0", True, False)
            stage_turn(nc, G, "t0")
            stage_resonance_out(nc, G)
            stage_out(nc, G, "o0", lambda t: [(G.ro[:, tile(t)], G.holo[0:HARM, 0, 1, :])], None)
            norm_x("n0")
            clear_used(nc)
            stage_project_cross(nc, G, "p1", M_X0Q, M_X0K, M_X0V, 1.0 / 16, None, None, None)
            stage_attention_over_queries(nc, G)
            stage_turn(nc, G, "t1")
            stage_out(nc, G, "o1", out_products(M_X0O), None)
            norm_x("n1")
        stage_ffn0(nc, G)
        norm_x("n2")
        clear_used(nc)
        sb = lambda *a: st.enter_context(nc.sbuf_tensor(*a))
        G.A, G.AT = sb("A_l1", [P, TPB, B * D], F32), sb("AT_l1", [P, 2, TOK], F32)
        stage_holographic(nc, G)
        az = G.A[:].rearrange("p t (b d) -> p (t b) d", d=D)
        stage_turn_back(nc, G, "b3", G.AT, TILES, az)
        stage_norm(nc, G, "m3", az, TILES, D, G.AT, gain=lambda k, g: G.fvec[:, V_LG, k:k + 1],
                   shift=lambda k, g: G.fvec[:, V_LB, k:k + 1])
        stage_out(nc, G, "o3", out_products(M_LO), R_LBO, keep=2.0)
        norm_x("n3")
        with ExitStack() as st0:
            sb = lambda *a: st0.enter_context(nc.sbuf_tensor(*a))
            G.ctxT, G.Vx = sb("ctxT2", [P, 2, B * SK], F32), sb("Vx2", [P, SLOTS, 2, DH], F32)
            stage_reload_context(nc, I, G)
            stage_project_cross(nc, G, "p4", M_X1Q, M_X1K, M_X1V, DH ** -0.5, V_X1BQ, V_X1BK, R_X1BV)
            stage_attention(nc, G, "a4", False, True)
            stage_turn(nc, G, "t4")
            stage_out(nc, G, "o4", out_products(M_X1O), R_X1BO)
        norm_x("n4", scratch=G.x_dram)
        clear_used(nc)
        sb = lambda *a: st.enter_context(nc.sbuf_tensor(*a))
        G.ew1, G.ew2 = sb("ew1", [P, 2, NEXP * EH], F32), sb("ew2", [P, 2, NEXP * EH], F32)
        G.ew3, G.sw12, G.sw3 = sb("ew3", [P, NEXP * D], F32), sb("sw12", [P, 2, D], F32), sb("sw3", [P, D], F32)
        G.gw, G.eb = sb("gw", [P, 2, 9], F32), sb("eb", [NEXP, 2 * D], F32)
        G.Z, G.ZT = sb("Z", [P, XT, EH], F32), sb("ZT", [P, 1, TOK + NMOE], F32)
        G.shared_g = sb("shared_g", [P, MT, D], F32)
        stage_gather(nc, I, G)
        stage_shared_hidden(nc, G)
        stage_norm(nc, G, "m5", G.Z, XT, EH, G.ZT, gain=lambda k, g: G.evec[:, 0:1], shift=lambda k, g: G.evec[:, 1:2])
        stage_shared_out(nc, G)
        stage_experts(nc, G)
        stage_norm(nc, G, "n5", G.X, XT, D, None, out=out)
        stage_scatter(nc, G, out)


def stage_reload_context(nc, I, G):
    with ExitStack() as st:
        loaded = st.enter_context(nc.semaphore("ctx_loaded"))
        block = st.enter_context(nc.Block())

        @block.sync
        def _(sp):
            sp.dma_start(G.ctxT[:], I["ctx_fm"].rearrange("k p t -> p k t")).then_inc(loaded, 16)
            sp.wait_ge(loaded, 16)


def kernel(**inputs):
    import numpy as _np
    import concourse.bacc as _bacc
    from concourse import mybir as _mybir
    from concourse.bass_utils import run_bass_kernel_spmd as _run

    a = {k: _np.asarray(v) for k, v in inputs.items()}

    def fm(w):
        return w.reshape(w.shape[0] // 128, 128, -1).transpose(1, 0, 2)

    def col(v):
        return v.reshape(-1, 128).T

    x = a["x"].reshape(2048, 256)
    mats = [a["L0_xattn_Wq"].T, a["L0_xattn_Wk"].T, a["L0_xattn_Wv"].T, a["L0_xattn_Wo"].T,
            a["L1_attn_Wk"].T, a["L1_attn_Wv"].T, a["L1_attn_Wq"].T, a["L1_attn_Wkp"].T, a["L1_attn_Wqp"].T,
            a["L1_attn_Wo"].T, a["L1_xattn_Wq"], a["L1_xattn_Wk"], a["L1_xattn_Wv"], a["L1_xattn_Wo"]]
    w1, w2 = fm(a["L0_ffn_w1_w"].T), fm(a["L0_ffn_w2_w"].T)
    h1, h2, w3 = fm(a["L0_ffn_h1_w"].T), fm(a["L0_ffn_h2_w"].T), fm(a["L0_ffn_w3_w"].T)
    units = [_np.concatenate([w[:, k, m * 128:(m + 1) * 128] for m in (2 * u, 2 * u + 1) for w in (w1, w2)
                              for k in range(2)], axis=1) for u in range(4)]
    units += [h[:, :, m * 128:(m + 1) * 128].reshape(128, 1024) for h in (h1, h2) for m in range(8)]
    units += [w3[:, 4 * v:4 * v + 4, :].reshape(128, 1024) for v in range(2)]
    experts = lambda w: w.transpose(2, 0, 1).reshape(w.shape[2], -1)
    arrays = {
        "x_tm": x.reshape(16, 128, 256),
        "x_fm": x.T.reshape(2, 128, 2048),
        "ctx_fm": a["ctx_1024"].reshape(308, 256).T.reshape(2, 128, 308),
        "mask": a["mask_Bx1xS2_ik0"].reshape(2, 154),
        "basis": _np.concatenate([a["L0_attn_basis_" + c] for c in "qkvo"]).T.reshape(2, 128, 128),
        "phase_qkv": _np.concatenate([a["L0_attn_phase_" + c].T for c in "qkv"]),
        "amp_qkv": _np.concatenate([a["L0_attn_amp_" + c].T for c in "qkv"]),
        "phase_o": a["L0_attn_phase_o"].T, "amp_o": a["L0_attn_amp_o"].T,
        "wmat": _np.stack([fm(m) for m in mats], axis=1),
        "fvec": _np.stack([col(a[n]) for n in ("L1_attn_bk", "L1_attn_bv", "L1_attn_bq", "L1_attn_bkp", "L1_attn_bqp",
                                               "L1_attn_phase_scale", "L1_attn_ln_g", "L1_attn_ln_b",
                                               "L1_xattn_bq", "L1_xattn_bk")], axis=1),
        "evec": _np.stack([a["L1_ffn_" + n] for n in ("s_ln_g", "s_ln_b", "sel_ln_g", "sel_ln_b")], axis=1),
        "rvec": _np.stack([a["L1_attn_bo"], a["L1_xattn_bv"], a["L1_xattn_bo"], a["L0_ffn_w3_s"], a["L1_ffn_sb3"],
                           _np.concatenate([a["L1_ffn_sb1"], a["L1_ffn_sb2"]])]),
        "grow": _np.concatenate([a["L1_ffn_sg_b"], a["L1_ffn_eg_b"], a["L1_ffn_exp_bias"]]),
        "ffn_s": _np.stack([col(a["L0_ffn_" + n]) for n in ("w1_s", "w2_s", "h1_s", "h2_s")], axis=1),
        "ffn_units": _np.stack(units),
        "index_b": a["L1_ffn_index_b"], "index_t": a["L1_ffn_index_t"],
        "sw12": _np.concatenate([a["L1_ffn_sw1"], a["L1_ffn_sw2"]]).T.reshape(2, 128, 256),
        "sw3": a["L1_ffn_sw3"].T,
        "gw": _np.concatenate([a["L1_ffn_sg_w"], a["L1_ffn_eg_w"]]).T.reshape(2, 128, 9),
        "ew1": experts(a["L1_ffn_ew1"]).reshape(2, 128, 1024), "ew2": experts(a["L1_ffn_ew2"]).reshape(2, 128, 1024),
        "ew3": experts(a["L1_ffn_ew3"]),
        "eb": _np.concatenate([a["L1_ffn_eb1"], a["L1_ffn_eb2"], a["L1_ffn_eb3"]], axis=1),
    }
    arrays = {k: _np.ascontiguousarray(v) for k, v in arrays.items()}
    nc = _bacc.Bacc("TRN2", target_bir_lowering=False, num_devices=1)
    I = {k: nc.dram_tensor("in_" + k, v.shape, _mybir.dt.from_np(v.dtype), kind="ExternalInput").ap()
         for k, v in arrays.items()}
    out = nc.dram_tensor("out_x", (16, 128, 256), _mybir.dt.float32, kind="ExternalOutput").ap()
    decoder_kernel(nc, I, out)
    r = _run(nc, [{"in_" + k: v for k, v in arrays.items()}], core_ids=[0])
    return r.results[0]["out_x"].reshape(2, 1024, 256)
```

```python
from contextlib import ExitStack

import numpy as np
import concourse.bass as bass
from concourse import mybir

ALU = mybir.AluOpType
ACT = mybir.ActivationFunctionType
AX_X = mybir.AxisListType.X
F32 = mybir.dt.float32
F32R = mybir.dt.float32r
BF16 = mybir.dt.bfloat16
I32 = mybir.dt.int32
U32 = mybir.dt.uint32

P = 128
B = 2
S = 1024
D = 256
SK = 154
TOK = B * S
TILES = TOK // P
TPB = S // P
HEADS = 16
DH = D // HEADS
SLOTS = B * HEADS
CH = 512
CHUNKS = TOK // CH
HARM = 32
HID = 1024
EPS = 1e-5
NMOE = 512
MT = NMOE // P
XT = TILES + MT
NEXP = 8
EH = 128
SCAN = 64
PROD = 6 * DH
MASKROW = PROD
MAXROW = PROD + 1
KROWS = PROD + 3
VW = 32
RSQRT_MAGIC = float(0x5F3759DF)
ROUND = 12582912.0
TWO_PI = 2.0 * np.pi
C1 = 6.28125
C2 = float((np.float32(TWO_PI - C1).view(np.uint32) & np.uint32(0xFFFFF000)).view(np.float32))
C3 = float(np.float32(TWO_PI - C1 - C2))
PI_IN = 3.1415925

M_X0Q, M_X0K, M_X0V, M_X0O, M_LK, M_LV, M_LQ, M_LKP, M_LQP, M_LO, M_X1Q, M_X1K, M_X1V, M_X1O = range(14)
V_LBK, V_LBV, V_LBQ, V_LBKP, V_LBQP, V_PS, V_LG, V_LB, V_X1BQ, V_X1BK = range(10)
R_LBO, R_X1BV, R_X1BO, R_W3S, R_SB3, R_SB12, NROWS = range(7)


USED = []


def clear_used(nc):
    nc.clear_and_free_semaphores(USED)
    USED.clear()
    nc.all_engine_barrier()


def makers(nc, st, stage):
    def semaphore(name):
        USED.append(nc.alloc_semaphore(f"{stage}_{name}"))
        return USED[-1]
    return (semaphore,
            lambda name, shape, dt: st.enter_context(nc.sbuf_tensor(f"{stage}_{name}", shape, dt)),
            lambda name, shape, dt: st.enter_context(nc.psum_tensor(f"{stage}_{name}", shape, dt)))


def linker(eng, sem):
    count = [0]

    def link(ins):
        count[0] += 1
        ins.then_inc(sem, 1)
        eng.wait_ge(sem, count[0])
    return link


def stage_setup(nc, I, G):
    with ExitStack() as st:
        sem, sb, psum = makers(nc, st, "setup")
        loaded, zeroed = sem("loaded"), sem("zeroed")
        block = st.enter_context(nc.Block())

        @block.sync
        def _(sp):
            loads = [
                (G.xT[:, :, 0:TOK], I["x_fm"].rearrange("k p t -> p k t")),
                (G.basis[:], I["basis"].rearrange("k p h -> p k h")),
                (G.holo[0:96, 0, 0, :], I["phase_qkv"]), (G.holo[0:96, 1, 0, :], I["amp_qkv"]),
                (G.holo[0:HARM, 0, 1, :], I["phase_o"]), (G.holo[0:HARM, 1, 1, :], I["amp_o"]),
                (G.X[:, 0:TILES, :], I["x_tm"].rearrange("t p d -> p t d")),
                (G.ctxT[:], I["ctx_fm"].rearrange("k p t -> p k t")),
                (G.wmat[:], I["wmat"]), (G.fvec[:], I["fvec"]), (G.ffn_s[:], I["ffn_s"]),
                (G.evec[:], I["evec"]), (G.grow[:], I["grow"].rearrange("(o r) -> o r", o=1).broadcast_to([P, 17])),
                (G.rvec[:], I["rvec"].rearrange("(o r) d -> o r d", o=1).broadcast_to([P, NROWS, D])),
            ]
            for dst, src in loads:
                sp.dma_start(dst, src).then_inc(loaded, 16)
            sp.wait_ge(loaded, 16 * len(loads))

        @block.gpsimd
        def _(pool):
            pool.memset(G.ident[:], 0.0).then_inc(zeroed, 1)
            pool.wait_ge(zeroed, 1)
            pool.affine_select(out=G.ident[:], in_=G.ident[:], compare_op=ALU.not_equal, fill=1.0, base=0,
                               pattern=[[-1, P]], channel_multiplier=1).then_inc(zeroed, 1)
            pool.memset(G.halfpi[:], float(np.pi / 2)).then_inc(zeroed, 1)
            pool.wait_ge(zeroed, 3)


class Job:

    def __init__(self, products, cols, scale, bias, stores):
        self.products, self.cols, self.scale, self.bias, self.stores = products, cols, scale, bias, stores


def split_products(pe, jobs, ps, made, read):
    for j, job in enumerate(jobs):
        if j >= 2:
            pe.wait_ge(read, 3 * (j - 1))
        for n, (lhsT, rhs) in enumerate(job.products):
            mm = pe.matmul(ps[:, j % 2, 0:job.cols], lhsT, rhs, start=(n == 0), stop=(n == len(job.products) - 1))
        mm.then_inc(made, 1)


def split_read(act, jobs, ps, full, parts, made, read, split, stored):
    for j, job in enumerate(jobs):
        act.wait_ge(made, j + 1)
        if j >= 2:
            act.wait_ge(split, j - 1)
            act.wait_ge(stored[j % 2], 16 * len(job.stores) * (j // 2))
        c = job.cols
        for out in (full[:, j % 2, 0:c], parts[:, j % 2, 0, 0:c]):
            act.activation(out, ps[:, j % 2, 0:c], ACT.Identity, bias=job.bias if job.bias is not None else 0.0,
                           scale=job.scale).then_inc(read, 1)
        act.wait_ge(read, 3 * j + 2)
        act.sem_inc(read, 1)


def split_rest(dve, jobs, full, parts, read, rest, split):
    for j, job in enumerate(jobs):
        c = job.cols
        f, p1, p2, p3 = full[:, j % 2, 0:c], *(parts[:, j % 2, n, 0:c] for n in range(3))
        dve.wait_ge(read, 3 * j + 3)
        dve.tensor_tensor(f, f, p1, ALU.subtract).then_inc(rest, 1)
        dve.wait_ge(rest, 2 * j + 1)
        dve.tensor_copy(p2, f).then_inc(rest, 1)
        dve.wait_ge(rest, 2 * j + 2)
        dve.tensor_tensor(p3, f, p2, ALU.subtract).then_inc(split, 1)


def split_store(sp, jobs, parts, split, stored):
    for j, job in enumerate(jobs):
        sp.wait_ge(split, j + 1)
        for a, b, dst in job.stores:
            sp.dma_start(dst, parts[:, j % 2, :, a:b]).then_inc(stored[j % 2], 16)
    for par in range(2):
        n = sum(len(j.stores) for j in jobs[par::2])
        sp.wait_ge(stored[par], 16 * n)


def parts_view(dram, b, blk, a, n):
    return dram[:, b, blk * P:(blk + 1) * P, a:a + n].rearrange("t p c -> p t c")


def stage_project_self(nc, G):
    with ExitStack() as st:
        sem, sb, psum = makers(nc, st, "ps")
        resT = sb("resT", [96, TOK], F32)
        full = sb("split_full", [P, 2, CH], F32)
        parts = sb("split_parts", [P, 2, 3, CH], BF16)
        tmp = sb("cos_tmp", [96, 2, D], F32)
        ps = psum("ps_split", [P, 2, CH], F32)
        ps_res = psum("ps_res", [P, 2, CH], F32)
        ps_v = psum("ps_v", [P, 2, CH], F32)
        res_made, res_read, w_made, w_step, cos_done = sem("res_made"), sem("res_read"), sem("w_made"), sem("w_step"), sem("cos")
        made, read, rest, split = sem("made"), sem("read"), sem("rest"), sem("split")
        stored = [sem("stored0"), sem("stored1")]
        v_made, v_read = sem("v_made"), sem("v_read")
        jobs = []
        for which, dram, scale in ((0, G.q_dram, DH ** -0.5), (1, G.k_dram, 1.0)):
            for c in range(CHUNKS):
                for blk in range(2):
                    r = slice(HARM * which, HARM * which + HARM)
                    jobs.append(Job([(G.holo[r, 0, 0, blk * P:(blk + 1) * P], resT[r, c * CH:(c + 1) * CH])], CH, scale,
                                    None, [(0, CH, parts_view(dram, c // 2, blk, (c % 2) * CH, CH))]))
        block = st.enter_context(nc.Block())

        @block.tensor
        def _(pe):
            for c in range(CHUNKS):
                if c >= 2:
                    pe.wait_ge(res_read, c - 1)
                for k in range(2):
                    mm = pe.matmul(ps_res[0:96, c % 2, :], G.basis[:, k, 0:96], G.xT[:, k, c * CH:(c + 1) * CH],
                                   start=(k == 0), stop=(k == 1))
                mm.then_inc(res_made, 1)
            pe.wait_ge(w_made, 1)
            pe.wait_ge(res_read, CHUNKS)
            split_products(pe, jobs, ps, made, read)
            for t in range(TILES):
                if t >= 2:
                    pe.wait_ge(v_read, t - 1)
                pe.matmul(ps_v[:, t % 2, 0:D], resT[64:96, t * P:(t + 1) * P], G.holo[64:96, 0, 0, :],
                          start=True, stop=True).then_inc(v_made, 1)

        @block.vector
        def _(dve):
            link = linker(dve, w_step)
            for rows, o in ((96, 0), (HARM, 1)):
                ph, k = G.holo[0:rows, 0, o, :], tmp[0:rows, o, :]
                link(dve.tensor_scalar(k, ph, 1.0 / TWO_PI, 0.25, ALU.mult, ALU.add))
                link(dve.tensor_scalar(k, k, ROUND, None, ALU.add))
                link(dve.tensor_scalar(k, k, -ROUND, None, ALU.add))
                for cst in (C1, C2, C3):
                    link(dve.scalar_tensor_tensor(ph, k, -cst, ph, ALU.mult, ALU.add))
                link(dve.tensor_scalar(ph, ph, float(np.pi / 2), PI_IN, ALU.add, ALU.min))
                link(dve.tensor_scalar(ph, ph, -PI_IN, None, ALU.max))
            dve.wait_ge(cos_done, 2)
            link(dve.tensor_tensor(G.holo[0:HARM, 0, 1, :], G.holo[0:HARM, 0, 1, :], G.holo[0:HARM, 1, 1, :], ALU.mult))
            dve.tensor_tensor(G.holo[0:96, 0, 0, :], G.holo[0:96, 0, 0, :], G.holo[0:96, 1, 0, :],
                              ALU.mult).then_inc(w_made, 1)
            split_rest(dve, jobs, full, parts, read, rest, split)

        @block.scalar
        def _(act):
            for c in range(CHUNKS):
                act.wait_ge(res_made, c + 1)
                act.activation(resT[:, c * CH:(c + 1) * CH], ps_res[0:96, c % 2, :], ACT.Copy).then_inc(res_read, 1)
            act.wait_ge(w_step, 16)
            act.activation(G.holo[0:96, 0, 0, :], G.holo[0:96, 0, 0, :], ACT.Sin).then_inc(cos_done, 1)
            act.activation(G.holo[0:HARM, 0, 1, :], G.holo[0:HARM, 0, 1, :], ACT.Sin).then_inc(cos_done, 1)
            split_read(act, jobs, ps, full, parts, made, read, split, stored)
            for t in range(TILES):
                act.wait_ge(v_made, t + 1)
                b, tau = t // TPB, t % TPB
                act.activation(G.V[:, b * HEADS:(b + 1) * HEADS, tau, :],
                               ps_v[:, t % 2, 0:D].rearrange("p (h d) -> p h d", d=DH), ACT.Copy).then_inc(v_read, 1)

        @block.sync
        def _(sp):
            split_store(sp, jobs, parts, split, stored)


def stage_project_cross(nc, G, tag, mq, mk, mv, scale, bq, bk, bv_row):
    with ExitStack() as st:
        sem, sb, psum = makers(nc, st, tag)
        full = sb("split_full", [P, 2, CH], F32)
        parts = sb("split_parts", [P, 2, 3, CH], BF16)
        qb = sb("q_bias", [P, 2], F32)
        ps = psum("ps_split", [P, 2, CH], F32)
        ps_v = psum("ps_v", [P, 2, CH], F32)
        made, read, rest, split = sem("made"), sem("read"), sem("rest"), sem("split")
        stored = [sem("stored0"), sem("stored1")]
        v_made, v_read, qb_made = sem("v_made"), sem("v_read"), sem("qb_made")
        jobs = []
        for blk in range(2):
            cols = slice(blk * P, (blk + 1) * P)
            jobs.append(Job([(G.wmat[:, mk, k, cols], G.ctxT[:, k, :]) for k in range(2)], B * SK, 1.0,
                            None if bk is None else G.fvec[:, bk, blk:blk + 1],
                            [(b * SK, (b + 1) * SK, parts_view(G.kx_dram, b, blk, 0, SK)) for b in range(B)]))
        for c in range(CHUNKS):
            for blk in range(2):
                cols = slice(blk * P, (blk + 1) * P)
                half = [(h * CH // 2, (h + 1) * CH // 2) for h in range(2)]
                jobs.append(Job([(G.wmat[:, mq, k, cols], G.xT[:, k, c * CH:(c + 1) * CH]) for k in range(2)], CH, scale,
                                None if bq is None else qb[:, blk:blk + 1],
                                [(a, z, parts_view(G.qx_dram, c // 2, blk, (c % 2) * CH + a, z - a)) for a, z in half]))
        block = st.enter_context(nc.Block())
        vt = [(b, kt, a, n) for b in range(B) for kt, (a, n) in enumerate(((0, P), (P, SK - P)))]

        @block.tensor
        def _(pe):
            split_products(pe, jobs, ps, made, read)
            for j, (b, kt, a, n) in enumerate(vt):
                if j >= 2:
                    pe.wait_ge(v_read, j - 1)
                for k in range(2):
                    mm = pe.matmul(ps_v[0:n, j % 2, 0:D], G.ctxT[:, k, b * SK + a:b * SK + a + n], G.wmat[:, mv, k, :],
                                   start=(k == 0), stop=(k == 1))
                mm.then_inc(v_made, 1)

        @block.vector
        def _(dve):
            if bq is not None:
                dve.tensor_scalar(qb[:], G.fvec[:, bq, :], scale, None, ALU.mult).then_inc(qb_made, 1)
            split_rest(dve, jobs, full, parts, read, rest, split)
            for j, (b, kt, a, n) in enumerate(vt):
                dve.wait_ge(v_made, j + 1)
                out = G.Vx[0:n, b * HEADS:(b + 1) * HEADS, kt, :]
                src = ps_v[0:n, j % 2, 0:D].rearrange("p (h d) -> p h d", d=DH)
                if bv_row is None:
                    dve.tensor_copy(out, src).then_inc(v_read, 1)
                else:
                    dve.tensor_tensor(out, src, G.rvec[0:n, bv_row, :].rearrange("p (h d) -> p h d", d=DH),
                                      ALU.add).then_inc(v_read, 1)

        @block.scalar
        def _(act):
            if bq is not None:
                act.wait_ge(qb_made, 1)
            split_read(act, jobs, ps, full, parts, made, read, split, stored)

        @block.sync
        def _(sp):
            split_store(sp, jobs, parts, split, stored)


class Slot:

    def __init__(self, i, c, u=4):
        self.i, self.c, self.u = i, c, u

    def __add__(self, k):
        return Slot(self.i, self.c + k, self.u)

    def known(self):
        return isinstance(self.i, int)

    def ring(self, n=4):
        return self.c % n

    def times(self, m, more=0):
        return self.i * (self.u * m) + (self.c * m + more)

    def turn(self, m, more=0, ring=4):
        return self.i * (self.u // ring * m) + (self.c // ring * m + more)


def head_cols(s):
    return bass.ds(s.times(DH), DH) if not s.known() else slice(s.times(DH), s.times(DH) + DH)


def run_slots(eng, first, last, loop_from, loop_last, emit, u=4):
    for s in range(first, loop_from):
        emit(Slot(0, s, u))
    turns = (loop_last - loop_from + 1) // u
    with eng.Fori(0, turns) as i:
        for n in range(u):
            emit(Slot(i, loop_from + n, u))
    for s in range(loop_from + u * turns, last + 1):
        emit(Slot(0, s, u))


RUNS = [(0, 3 * DH, slice(0, 3), 0), (3 * DH, 2 * DH, slice(0, 2), 1), (5 * DH, DH, slice(0, 1), 2)]
LOADS = len(RUNS)


def load_queries(sp, n, stack, dram, ready):
    src = dram.rearrange("t b (h d) c -> t (b h) d c", d=DH)
    for row, rows, qp, kp in RUNS:
        sp.dma_start(stack[row:row + rows], src[qp, n.times(1)]).then_inc(ready, 16)


def load_keys(sp, n, stack, dram, ready):
    src = dram.rearrange("t b (h d) c -> t (b h) d c", d=DH)
    for row, rows, qp, kp in RUNS:
        one = src[kp:kp + 1, n.times(1)]
        sp.dma_start(stack[row:row + rows], one.broadcast_to([rows // DH, DH, one.shape[-1]])).then_inc(ready, 16)


def load_all_keys(sp, stack, dram, ready):
    src = dram.rearrange("t b (h d) c -> t d (b h) c", d=DH)
    for row, rows, qp, kp in RUNS:
        for r in range(row, row + rows, DH):
            sp.dma_start(stack[r:r + DH], src[kp]).then_inc(ready, 16)


def stage_attention(nc, G, tag):
    NKT = S // P
    EB = 4
    CONSTS = 5
    STEP_O, STEP_M = 2, 4
    with ExitStack() as st:
        sem, sb, psum = makers(nc, st, tag)
        q_stack = sb("q_stack", [P, 4, S], BF16)
        k_stack = sb("k_stack", [P, 4, S], BF16)
        values = sb("values", [P, 4, NKT, VW], F32)
        probs = sb("probs", [P, EB, S], F32)
        neg_max = sb("neg_max", [P, 4, TPB], F32)
        max_rows = sb("max_rows", [TPB, 4, 2, P], BF16)
        out_raw = sb("out_raw", [P, 2, 2 * P], F32)
        inv_sum = sb("inv_sum", [P, 2, 2, 4], F32)
        pm = psum("ps_max", [P, 2, 2 * CH], F32)
        pscore = psum("ps_score", [P, 2, CH], F32)
        po = psum("ps_out", [P, CH], F32)
        pmisc = psum("ps_misc", [P, CH], F32)
        ready = [sem(f"stack{r}") for r in range(4)]
        rows_in = [sem(f"rows{r}") for r in range(4)]
        const = sem("const")
        max_made, max_done = sem("max_made"), sem("max_done")
        misc_made, misc_done = sem("misc_made"), sem("misc_done")
        row_hi, row_done = sem("row_hi"), sem("row_done")
        score_made, exp_done, pv_done = sem("score"), sem("exp"), sem("pv")
        out_read, recip, values_in = sem("out_read"), sem("recip"), sem("values_in")
        block = st.enter_context(nc.Block())

        def pos(x, n):
            return x.times(*n) if not x.known() or x.times(*n) > 0 else None

        def wait(eng, s, v):
            if v is not None:
                eng.wait_ge(s, v)

        @block.sync
        def _(sp):
            sp.wait_ge(const, CONSTS)

            def rows(n):
                r = n.ring()
                sp.wait_ge(row_done, n.times(1, 1))
                for part in range(2):
                    sp.dma_start(q_stack[MAXROW + part:MAXROW + part + 1, r, :],
                                 max_rows[:, r, part, :]).then_inc(rows_in[r], 16)

            def slot(s):
                if s.c + 1 < SLOTS or not s.known():
                    rows(s + 1)
                if s.c + 4 < SLOTS or not s.known():
                    sp.wait_ge(pv_done, s.times(NKT, NKT))
                    load(s + 4)

            def load(n):
                r = n.ring()
                load_queries(sp, n, q_stack[:, r, :], G.q_dram, ready[r])
                load_keys(sp, n, k_stack[:, r, :], G.k_dram, ready[r])

            for n in range(4):
                load(Slot(0, n))
            rows(Slot(0, 0))
            run_slots(sp, 0, SLOTS - 1, 0, SLOTS - 5, slot)

        @block.gpsimd
        def _(pool):
            link = linker(pool, const)
            link(pool.memset(values[:], 0.0))
            link(pool.memset(q_stack[PROD:KROWS, :, :], 1.0))
            link(pool.memset(k_stack[PROD:KROWS, :, :], 1.0))
            link(pool.memset(k_stack[MASKROW:MASKROW + 1, :, :], 0.0))
            link(pool.memset(values[:, :, :, DH:DH + 1], 1.0))

            def copy_values(n):
                if not n.known() or n.c >= 4:
                    pool.wait_ge(pv_done, n.times(NKT, -3 * NKT))
                pool.tensor_copy(values[:, n.ring(), :, 0:DH], G.V[:, n.times(1), :, :]).then_inc(values_in, 1)
            run_slots(pool, 0, SLOTS - 1, 4, SLOTS - 1, copy_values)

        @block.tensor
        def _(pe):
            def max_unit(n, m):
                r = n.ring()
                if m == 0:
                    pe.wait_ge(ready[r], n.turn(32 * LOADS, 32 * LOADS))
                wait(pe, max_done, pos(n, (NKT, m - 1)))
                for h in range(2):
                    mm = pe.matmul(pm[:, m % 2, h * CH:(h + 1) * CH], q_stack[0:PROD, r, m * P:(m + 1) * P],
                                   k_stack[0:PROD, r, h * CH:(h + 1) * CH], start=True, stop=True)
                mm.then_inc(max_made, 1)

            def max_turn(n, index):
                pe.wait_ge(max_done, n.times(NKT, NKT))
                if index is not None:
                    pe.wait_ge(misc_done, index)
                pe.transpose(pmisc[0:TPB, 0:P], neg_max[:, n.ring(), :], G.ident[:]).then_inc(misc_made, 1)

            def score(s, t, h):
                r = s.ring()
                g = 2 * t + h
                if g == 0:
                    pe.wait_ge(rows_in[r], s.turn(32, 32))
                wait(pe, exp_done, pos(s, (2 * NKT, g - 1)))
                pe.matmul(pscore[:, h, :], k_stack[0:KROWS, r, t * P:(t + 1) * P], q_stack[0:KROWS, r, h * CH:(h + 1) * CH],
                          start=True, stop=True).then_inc(score_made, 1)

            def pv(s, t):
                if t == 0:
                    pe.wait_ge(values_in, s.times(1, 1))
                    wait(pe, out_read, pos(s, (1, 0)))
                pe.wait_ge(exp_done, s.times(2 * NKT, 2 * t + 2))
                e = (s.c * NKT + t) % EB
                for j in range(4):
                    mm = pe.matmul(po[j * VW:(j + 1) * VW, 0:2 * P], values[:, s.ring(), t, :],
                                   probs[:, e, j * 2 * P:(j + 1) * 2 * P], start=(t == 0), stop=(t == NKT - 1))
                mm.then_inc(pv_done, 1)

            def out_turn(s, index):
                pe.wait_ge(out_read, s.times(1, 1))
                pe.wait_ge(misc_done, index)
                for h in range(2):
                    mm = pe.transpose(pmisc[:, h * P:(h + 1) * P], out_raw[:, s.ring(2), h * P:(h + 1) * P], G.ident[:])
                mm.then_inc(misc_made, 1)

            def slot(s):
                known = s.known()
                first = known and s.c == 0
                for t in range(NKT):
                    score(s, t, 0)
                    score(s, t, 1)
                    if t == 0 and not first:
                        pv(s + -1, NKT - 1)
                    if t >= 1:
                        pv(s, t - 1)
                    if not known or s.c + 2 < SLOTS:
                        max_unit(s + 2, t)
                    if t == STEP_O and not first:
                        out_turn(s + -1, s.times(2, 0))
                    if t == STEP_M and (not known or s.c + 1 < SLOTS):
                        max_turn(s + 1, s.times(2, 1))

            pe.wait_ge(const, CONSTS)
            for n in range(2):
                for m in range(NKT):
                    max_unit(Slot(0, n), m)
            max_turn(Slot(0, 0), None)
            run_slots(pe, 0, SLOTS - 1, 1, SLOTS - 4, slot)
            pv(Slot(0, SLOTS - 1), NKT - 1)
            out_turn(Slot(0, SLOTS - 1), 2 * SLOTS - 1)

        @block.scalar
        def _(act):
            def slot(s):
                for t in range(NKT):
                    e = (s.c * NKT + t) % EB
                    for h in range(2):
                        act.wait_ge(score_made, s.times(2 * NKT, 2 * t + h + 1))
                        if h == 0:
                            wait(act, pv_done, pos(s, (NKT, t + 1 - EB)))
                        act.activation(probs[:, e, h * CH:(h + 1) * CH], pscore[:, h, :],
                                       ACT.Exp).then_inc(exp_done, 1)
                    if t == 0 and not (s.known() and s.c == 0):
                        read_out(s + -1)

            def read_out(s):
                act.wait_ge(pv_done, s.times(NKT, NKT))
                act.activation(out_raw[:, s.ring(2), :], po[:, 0:2 * P], ACT.Copy).then_inc(out_read, 1)

            run_slots(act, 0, SLOTS - 1, 1, SLOTS - 4, slot)
            read_out(Slot(0, SLOTS - 1))

        @block.vector
        def _(dve):
            def max_unit(n, m):
                dve.wait_ge(max_made, n.times(NKT, m + 1))
                dve.tensor_reduce(neg_max[:, n.ring(), m:m + 1], pm[:, m % 2, :], AX_X, ALU.max,
                                  negate=True).then_inc(max_done, 1)

            def max_row(n, index):
                r = n.ring()
                dve.wait_ge(misc_made, index)
                dve.tensor_copy(max_rows[:, r, 0, :], pmisc[0:TPB, 0:P]).then_inc(row_hi, 1)
                dve.wait_ge(row_hi, n.times(1, 1))
                dve.tensor_tensor(max_rows[:, r, 1, :], pmisc[0:TPB, 0:P], max_rows[:, r, 0, :],
                                  ALU.subtract).then_inc(row_done, 1)
                dve.wait_ge(row_done, n.times(1, 1))
                dve.sem_inc(misc_done, 1)

            def normalise(s, index):
                par = s.ring(2)
                dve.wait_ge(misc_made, index)
                sums = pmisc[:, 0:2 * P].rearrange("p (h j c) -> p h j c", h=2, j=4)
                dve.reciprocal(inv_sum[:, par], sums[:, :, :, DH:DH + 1]).then_inc(recip, 1)
                dve.wait_ge(recip, s.times(1, 1))
                dst = G.A[:, :, head_cols(s)].rearrange("p (j h) d -> p h j d", h=2)
                dve.tensor_tensor(dst, sums[:, :, :, 0:DH],
                                  inv_sum[:, par].rearrange("p h (j o) -> p h j o", o=1).broadcast_to([P, 2, 4, DH]),
                                  ALU.mult).then_inc(misc_done, 1)

            def slot(s):
                known = s.known()
                for t in range(NKT):
                    if not known or s.c + 2 < SLOTS:
                        max_unit(s + 2, t)
                    if t == STEP_O and not (known and s.c == 0):
                        normalise(s + -1, s.times(2, 1))
                    if t == STEP_M and (not known or s.c + 1 < SLOTS):
                        max_row(s + 1, s.times(2, 2))

            for n in range(2):
                for m in range(NKT):
                    max_unit(Slot(0, n), m)
            max_row(Slot(0, 0), 1)
            run_slots(dve, 0, SLOTS - 1, 1, SLOTS - 4, slot)
            normalise(Slot(0, SLOTS - 1), 2 * SLOTS)


def stage_attention_cross(nc, G, tag):
    ktiles = [(0, P), (P, SK - P)]
    NKT = len(ktiles)
    RING = 8
    UNITS = 4
    QPU = TPB // UNITS
    with ExitStack() as st:
        sem, sb, psum = makers(nc, st, tag)
        q_stack = sb("q_stack", [P, RING, S], BF16)
        k_stack = sb("k_stack", [P, SLOTS, SK], BF16)
        values = sb("values", [P, 4, NKT, VW], F32)
        probs = sb("probs", [P, 4, S], F32)
        neg_max = sb("neg_max", [P, RING, TPB], F32)
        max_rows = sb("max_rows", [TPB, RING, 2, P], BF16)
        out_raw = sb("out_raw", [P, 2, 2 * P], F32)
        inv_sum = sb("inv_sum", [P, 2, 2, 4], F32)
        mask_f, mask_i, mask_b = sb("mask_f", [1, B, SK], F32), sb("mask_i", [1, B, SK], I32), sb("mask_b", [1, B, SK], BF16)
        pm = psum("ps_max", [P, 2, CH], F32)
        pscore = psum("ps_score", [P, NKT, 2 * CH], F32)
        po = psum("ps_out", [P, CH], F32)
        pmisc = psum("ps_misc", [P, CH], F32)
        ready = [sem(f"stack{r}") for r in range(RING)]
        rows_in = [sem(f"rows{r}") for r in range(RING)]
        const, mask_in, mask_step, keys_in = sem("const"), sem("mask_in"), sem("mask_step"), sem("keys_in")
        max_made, max_done = sem("max_made"), sem("max_done")
        max_turned, row_hi, row_done, row_free = sem("max_turned"), sem("row_hi"), sem("row_done"), sem("row_free")
        out_turned, recip, filed = sem("out_turned"), sem("recip"), sem("filed")
        score_made, exp_done, pv_done = sem("score"), sem("exp"), sem("pv")
        out_read, values_in = sem("out_read"), sem("values_in")
        block = st.enter_context(nc.Block())

        def run(eng, first, last, loop_from, loop_last, emit):
            run_slots(eng, first, last, loop_from, loop_last, emit, RING)

        def slot0(c):
            return Slot(0, c, RING)

        @block.sync
        def _(sp):
            def load(n):
                load_queries(sp, n, q_stack[:, n.ring(RING), :], G.qx_dram, ready[n.ring(RING)])

            def rows(n):
                r = n.ring(RING)
                sp.wait_ge(row_done, n.times(1, 1))
                for part in range(2):
                    sp.dma_start(q_stack[MAXROW + part:MAXROW + part + 1, r, :],
                                 max_rows[:, r, part, :]).then_inc(rows_in[r], 16)

            def slot(s):
                if not s.known() or s.c + RING < SLOTS:
                    sp.wait_ge(score_made, s.times(NKT, NKT))
                    load(s + RING)
                if not s.known() or s.c + 3 < SLOTS:
                    rows(s + 3)

            sp.dma_start(mask_i[:], G.mask.rearrange("(o b) s -> o b s", o=1)).then_inc(mask_in, 16)
            load(slot0(0))
            load_all_keys(sp, k_stack, G.kx_dram, keys_in)
            sp.wait_ge(const, 2)
            sp.wait_ge(mask_step, 2)
            for b in range(B):
                sp.dma_start(k_stack[MASKROW:MASKROW + 1, b * HEADS:(b + 1) * HEADS, :],
                             mask_b[:, b:b + 1, :].broadcast_to([1, HEADS, SK])).then_inc(keys_in, 16)
            for n in range(1, RING):
                load(slot0(n))
            for n in range(3):
                rows(slot0(n))
            run(sp, 0, SLOTS - 1, 0, SLOTS - RING - 1, slot)

        @block.gpsimd
        def _(pool):
            link = linker(pool, const)
            link(pool.memset(q_stack[PROD:KROWS, :, :], 1.0))
            link(pool.memset(k_stack[PROD:KROWS, :, :], 1.0))
            link(pool.memset(values[:], 0.0))
            link(pool.memset(probs[:], 0.0))
            for kt, (a, m) in enumerate(ktiles):
                link(pool.memset(values[0:m, :, kt, DH:DH + 1], 1.0))

            def copy_values(n):
                if not n.known() or n.c >= 4:
                    pool.wait_ge(pv_done, n.times(1, -3))
                for kt, (a, m) in enumerate(ktiles):
                    pool.tensor_copy(values[0:m, n.ring(), kt:kt + 1, 0:DH],
                                     G.Vx[0:m, n.times(1), kt:kt + 1, :]).then_inc(values_in, 1)
            run(pool, 0, SLOTS - 1, RING, SLOTS - 1, copy_values)

        @block.tensor
        def _(pe):
            def max_unit(n, m):
                r = n.ring(RING)
                if m == 0:
                    pe.wait_ge(ready[r], n.turn(16 * LOADS, 16 * LOADS, RING))
                if not n.known() or n.c > 0 or m >= 2:
                    pe.wait_ge(max_done, n.times(UNITS, m - 1))
                for q in range(QPU):
                    t = m * QPU + q
                    mm = pe.matmul(pm[:, m % 2, q * SK:(q + 1) * SK], q_stack[0:PROD + 1, r, t * P:(t + 1) * P],
                                   k_stack[0:PROD + 1, n.times(1), :], start=True, stop=True)
                mm.then_inc(max_made, 1)

            def max_turn(n, filed_before):
                pe.wait_ge(max_done, n.times(UNITS, UNITS))
                if not n.known() or n.c > 0:
                    pe.wait_ge(row_free, n.times(1))
                if filed_before is not None:
                    pe.wait_ge(filed, filed_before)
                pe.transpose(pmisc[0:TPB, 0:P], neg_max[:, n.ring(RING), :], G.ident[:]).then_inc(max_turned, 1)

            def scores(s):
                r = s.ring(RING)
                pe.wait_ge(rows_in[r], s.turn(32, 32, RING))
                for t, (a, m) in enumerate(ktiles):
                    if not s.known() or s.c > 0:
                        pe.wait_ge(exp_done, s.times(NKT, t - 1))
                    for h in range(2):
                        mm = pe.matmul(pscore[0:m, t, h * CH:(h + 1) * CH], k_stack[0:KROWS, s.times(1), a:a + m],
                                       q_stack[0:KROWS, r, h * CH:(h + 1) * CH], start=True, stop=True)
                    mm.then_inc(score_made, 1)

            def products(s):
                pe.wait_ge(values_in, s.times(NKT, NKT))
                if not s.known() or s.c > 0:
                    pe.wait_ge(out_read, s.times(1))
                for t, (a, m) in enumerate(ktiles):
                    pe.wait_ge(exp_done, s.times(NKT, t + 1))
                    e = (s.c * NKT + t) % 4
                    for j in range(4):
                        mm = pe.matmul(po[j * VW:(j + 1) * VW, 0:2 * P], values[:, s.ring(), t, :],
                                       probs[:, e, j * 2 * P:(j + 1) * 2 * P], start=(t == 0), stop=(t == NKT - 1))
                mm.then_inc(pv_done, 1)

            def out_turn(s):
                pe.wait_ge(out_read, s.times(1, 1))
                rows_before = s + 6 if s.c + 6 <= SLOTS or not s.known() else Slot(0, SLOTS, RING)
                pe.wait_ge(row_free, rows_before.times(1))
                if not s.known() or s.c > 0:
                    pe.wait_ge(filed, s.times(1))
                for h in range(2):
                    mm = pe.transpose(pmisc[:, h * P:(h + 1) * P], out_raw[:, s.ring(2), h * P:(h + 1) * P], G.ident[:])
                mm.then_inc(out_turned, 1)

            def slot(s):
                scores(s)
                more = not s.known() or s.c + 4 < SLOTS
                if not s.known() or s.c + 3 < SLOTS:
                    max_turn(s + 3, (s + -2).times(1) if not s.known() or s.c >= 3 else None)
                if more:
                    max_unit(s + 4, 0)
                    max_unit(s + 4, 1)
                if not s.known() or s.c >= 1:
                    products(s + -1)
                if more:
                    max_unit(s + 4, 2)
                if not s.known() or s.c >= 2:
                    out_turn(s + -2)
                if more:
                    max_unit(s + 4, 3)

            pe.wait_ge(const, 6)
            pe.wait_ge(keys_in, 16 * 8)
            for n in range(4):
                for m in range(UNITS):
                    max_unit(slot0(n), m)
                if n < 3:
                    max_turn(slot0(n), None)
            run(pe, 0, SLOTS - 1, 3, SLOTS - 5, slot)
            products(slot0(SLOTS - 1))
            out_turn(slot0(SLOTS - 2))
            out_turn(slot0(SLOTS - 1))

        @block.scalar
        def _(act):
            def slot(s):
                for t, (a, m) in enumerate(ktiles):
                    act.wait_ge(score_made, s.times(NKT, t + 1))
                    if not s.known() or s.c >= 2:
                        act.wait_ge(pv_done, s.times(1, -1))
                    act.activation(probs[0:m, (s.c * NKT + t) % 4, :], pscore[0:m, t, :], ACT.Exp).then_inc(exp_done, 1)
                if not s.known() or s.c >= 1:
                    read_out(s + -1)

            def read_out(s):
                act.wait_ge(pv_done, s.times(1, 1))
                act.activation(out_raw[:, s.ring(2), :], po[:, 0:2 * P], ACT.Copy).then_inc(out_read, 1)
            act.wait_ge(const, 4)
            run(act, 0, SLOTS - 1, 2, SLOTS - 1, slot)
            read_out(slot0(SLOTS - 1))

        @block.vector
        def _(dve):
            dve.wait_ge(mask_in, 16)
            dve.tensor_copy(mask_f[:], mask_i[:]).then_inc(mask_step, 1)
            dve.wait_ge(mask_step, 1)
            dve.tensor_scalar(mask_b[:], mask_f[:], 0.0, -1e30, ALU.is_equal, ALU.mult).then_inc(mask_step, 1)

            def max_unit(n, m):
                dve.wait_ge(max_made, n.times(UNITS, m + 1))
                src = pm[:, m % 2, 0:QPU * SK].rearrange("p (q c) -> p q c", q=QPU)
                dve.tensor_reduce(neg_max[:, n.ring(RING), m * QPU:(m + 1) * QPU], src, AX_X, ALU.max,
                                  negate=True).then_inc(max_done, 1)

            def max_row(n):
                r = n.ring(RING)
                dve.wait_ge(max_turned, n.times(1, 1))
                dve.tensor_copy(max_rows[:, r, 0, :], pmisc[0:TPB, 0:P]).then_inc(row_hi, 1)
                dve.wait_ge(row_hi, n.times(1, 1))
                dve.tensor_tensor(max_rows[:, r, 1, :], pmisc[0:TPB, 0:P], max_rows[:, r, 0, :],
                                  ALU.subtract).then_inc(row_done, 1)
                dve.wait_ge(row_done, n.times(1, 1))
                dve.sem_inc(row_free, 1)

            def normalise(s):
                par = s.ring(2)
                dve.wait_ge(out_turned, s.times(1, 1))
                sums = pmisc[:, 0:2 * P].rearrange("p (h j c) -> p h j c", h=2, j=4)
                dve.reciprocal(inv_sum[:, par], sums[:, :, :, DH:DH + 1]).then_inc(recip, 1)
                dve.wait_ge(recip, s.times(1, 1))
                dst = G.A[:, :, head_cols(s)].rearrange("p (j h) d -> p h j d", h=2)
                dve.tensor_tensor(dst, sums[:, :, :, 0:DH],
                                  inv_sum[:, par].rearrange("p h (j o) -> p h j o", o=1).broadcast_to([P, 2, 4, DH]),
                                  ALU.mult).then_inc(filed, 1)

            def slot(s):
                more = not s.known() or s.c + 4 < SLOTS
                if not s.known() or s.c + 3 < SLOTS:
                    max_row(s + 3)
                if more:
                    max_unit(s + 4, 0)
                    max_unit(s + 4, 1)
                    max_unit(s + 4, 2)
                if not s.known() or s.c >= 2:
                    normalise(s + -2)
                if more:
                    max_unit(s + 4, 3)

            for n in range(4):
                for m in range(UNITS):
                    max_unit(slot0(n), m)
                if n < 3:
                    max_row(slot0(n))
            run(dve, 0, SLOTS - 1, 3, SLOTS - 5, slot)
            normalise(slot0(SLOTS - 2))
            normalise(slot0(SLOTS - 1))


def stage_attention_over_queries(nc, G):
    ktiles = [(0, P), (P, SK - P)]
    NKT = 2
    with ExitStack() as st:
        sem, sb, psum = makers(nc, st, "x0")
        q_stack = sb("q_stack", [P, 4, S], BF16)
        k_stack = sb("k_stack", [P, SLOTS, SK], BF16)
        values = sb("values", [P, 4, NKT, VW], F32)
        probs = sb("probs", [P, 4, S], F32)
        neg_max = sb("neg_max", [P, 4, NKT], F32)
        row_sum = sb("row_sum", [P, 4, NKT], F32)
        inv_row = sb("inv_row", [P, 4, NKT], F32)
        out_raw = sb("out_raw", [P, 2, 2 * P], F32)
        inv_sum = sb("inv_sum", [P, 2, 2, 4], F32)
        pscore = psum("ps_score", [P, 2, 2 * CH], F32)
        po = psum("ps_out", [P, CH], F32)
        pt = psum("ps_turn", [P, CH], F32)
        ready = [sem(f"stack{r}") for r in range(4)]
        const, keys_in = sem("const"), sem("keys_in")
        score_made, max_done, exp_done, inv_done = sem("score"), sem("max"), sem("exp"), sem("inv")
        values_in, pv_done, out_read, turned, recip, filed = (sem("values_in"), sem("pv"), sem("out_read"),
                                                              sem("turned"), sem("recip"), sem("filed"))
        block = st.enter_context(nc.Block())

        @block.sync
        def _(sp):
            def slot(s):
                sp.wait_ge(score_made, s.times(NKT, NKT))
                load(s + 4)

            def load(n):
                load_queries(sp, n, q_stack[:, n.ring(), :], G.qx_dram, ready[n.ring()])
            load(Slot(0, 0))
            load_all_keys(sp, k_stack, G.kx_dram, keys_in)
            for n in range(1, 4):
                load(Slot(0, n))
            run_slots(sp, 0, SLOTS - 5, 0, SLOTS - 5, slot)

        @block.gpsimd
        def _(pool):
            link = linker(pool, const)
            link(pool.memset(values[:], 0.0))
            link(pool.memset(probs[:], 0.0))

            def scale_values(n):
                r = n.ring()
                for kt, (a, m) in enumerate(ktiles):
                    pool.wait_ge(inv_done, n.times(NKT, kt + 1))
                    pool.tensor_tensor(values[0:m, r, kt, 0:DH], G.Vx[0:m, n.times(1), kt, :],
                                       inv_row[0:m, r, kt:kt + 1].broadcast_to([m, DH]), ALU.mult).then_inc(values_in, 1)
                    pool.tensor_copy(values[0:m, r, kt, DH:DH + 1], inv_row[0:m, r, kt:kt + 1]).then_inc(values_in, 1)
            run_slots(pool, 0, SLOTS - 1, 0, SLOTS - 1, scale_values)

        @block.tensor
        def _(pe):
            def scores(s):
                r = s.ring()
                pe.wait_ge(ready[r], s.turn(16 * LOADS, 16 * LOADS))
                for t, (a, m) in enumerate(ktiles):
                    if not s.known() or s.c > 0:
                        pe.wait_ge(exp_done, s.times(NKT, t - 1))
                    for h in range(2):
                        mm = pe.matmul(pscore[0:m, t, h * CH:(h + 1) * CH], k_stack[0:PROD, s.times(1), a:a + m],
                                       q_stack[0:PROD, r, h * CH:(h + 1) * CH], start=True, stop=True)
                    mm.then_inc(score_made, 1)

            def products(s):
                if not s.known() or s.c > 0:
                    pe.wait_ge(out_read, s.times(1))
                for t in range(NKT):
                    pe.wait_ge(values_in, s.times(2 * NKT, 2 * t + 2))
                    e = (s.c * NKT + t) % 4
                    for j in range(4):
                        mm = pe.matmul(po[j * VW:(j + 1) * VW, 0:2 * P], values[:, s.ring(), t, :],
                                       probs[:, e, j * 2 * P:(j + 1) * 2 * P], start=(t == 0), stop=(t == NKT - 1))
                mm.then_inc(pv_done, 1)

            def turn(s):
                pe.wait_ge(out_read, s.times(1, 1))
                if not s.known() or s.c > 0:
                    pe.wait_ge(filed, s.times(1))
                for h in range(2):
                    mm = pe.transpose(pt[:, h * P:(h + 1) * P], out_raw[:, s.ring(2), h * P:(h + 1) * P], G.ident[:])
                mm.then_inc(turned, 1)

            def slot(s):
                scores(s)
                turn(s + -2)
                products(s + -1)
            pe.wait_ge(const, 2)
            pe.wait_ge(keys_in, 96)
            scores(Slot(0, 0))
            scores(Slot(0, 1))
            products(Slot(0, 0))
            run_slots(pe, 2, SLOTS - 1, 3, SLOTS - 1, slot)
            turn(Slot(0, SLOTS - 2))
            products(Slot(0, SLOTS - 1))
            turn(Slot(0, SLOTS - 1))

        @block.scalar
        def _(act):
            def slot(s):
                for t, (a, m) in enumerate(ktiles):
                    act.wait_ge(max_done, s.times(NKT, t + 1))
                    if not s.known() or s.c >= 2:
                        act.wait_ge(pv_done, s.times(1, -1))
                    act.activation(probs[0:m, (s.c * NKT + t) % 4, :], pscore[0:m, t, :], ACT.Exp,
                                   bias=neg_max[0:m, s.ring(), t:t + 1],
                                   accum_out=row_sum[0:m, s.ring(), t:t + 1]).then_inc(exp_done, 1)
                if not (s.known() and s.c == 0):
                    read_out(s + -1)

            def read_out(s):
                act.wait_ge(pv_done, s.times(1, 1))
                act.activation(out_raw[:, s.ring(2), :], po[:, 0:2 * P], ACT.Copy).then_inc(out_read, 1)
            act.wait_ge(const, 2)
            run_slots(act, 0, SLOTS - 1, 2, SLOTS - 1, slot)
            read_out(Slot(0, SLOTS - 1))

        @block.vector
        def _(dve):
            def maxima(s):
                for t, (a, m) in enumerate(ktiles):
                    dve.wait_ge(score_made, s.times(NKT, t + 1))
                    dve.tensor_reduce(neg_max[0:m, s.ring(), t:t + 1], pscore[0:m, t, :], AX_X, ALU.max,
                                      negate=True).then_inc(max_done, 1)

            def invert(s):
                for t, (a, m) in enumerate(ktiles):
                    dve.wait_ge(exp_done, s.times(NKT, t + 1))
                    dve.reciprocal(inv_row[0:m, s.ring(), t:t + 1], row_sum[0:m, s.ring(), t:t + 1]).then_inc(inv_done, 1)

            def normalise(s):
                par = s.ring(2)
                dve.wait_ge(turned, s.times(1, 1))
                sums = pt[:, 0:2 * P].rearrange("p (h j c) -> p h j c", h=2, j=4)
                dve.reciprocal(inv_sum[:, par], sums[:, :, :, DH:DH + 1]).then_inc(recip, 1)
                dve.wait_ge(recip, s.times(1, 1))
                dst = G.A[:, :, head_cols(s)].rearrange("p (j h) d -> p h j d", h=2)
                dve.tensor_tensor(dst, sums[:, :, :, 0:DH],
                                  inv_sum[:, par].rearrange("p h (j o) -> p h j o", o=1).broadcast_to([P, 2, 4, DH]),
                                  ALU.mult).then_inc(filed, 1)

            def slot(s):
                maxima(s)
                invert(s)
                normalise(s + -2)
            for n in range(2):
                maxima(Slot(0, n))
                invert(Slot(0, n))
            run_slots(dve, 2, SLOTS - 1, 2, SLOTS - 1, slot)
            normalise(Slot(0, SLOTS - 2))
            normalise(Slot(0, SLOTS - 1))


def newton_rsqrt(dve, link, y, v, t):
    link(dve.tensor_scalar(v, v, EPS, None, ALU.add))
    link(dve.tensor_scalar(y.bitcast(I32), v.bitcast(I32), 1, None, ALU.logical_shift_right))
    link(dve.tensor_scalar(y.bitcast(I32), y.bitcast(I32), -1.0, RSQRT_MAGIC, ALU.mult, ALU.add))
    link(dve.tensor_scalar(v, v, -0.5, None, ALU.mult))
    for _ in range(3):
        link(dve.tensor_tensor(t, y, y, ALU.mult))
        link(dve.tensor_tensor(t, t, v, ALU.mult))
        link(dve.scalar_tensor_tensor(y, t, 1.5, y, ALU.add, ALU.mult))


def stage_turn(nc, G, tag):
    with ExitStack() as st:
        sem, sb, psum = makers(nc, st, tag)
        ps = psum("ps_turn", [P, 4, CH], F32)
        turned, read = sem("turned"), sem("read")
        block = st.enter_context(nc.Block())
        groups = [(c, blk) for c in range(CHUNKS) for blk in range(2)]

        @block.tensor
        def _(pe):
            for n, (c, blk) in enumerate(groups):
                if n >= 4:
                    pe.wait_ge(read, n - 3)
                for q in range(4):
                    t = 4 * c + q
                    b, tau = t // TPB, t % TPB
                    src = G.A[:, tau, b * D + blk * P:b * D + (blk + 1) * P]
                    mm = pe.transpose(ps[:, n % 4, q * P:(q + 1) * P], src, G.ident[:])
                mm.then_inc(turned, 1)

        @block.scalar
        def _(act):
            for n, (c, blk) in enumerate(groups):
                act.wait_ge(turned, n + 1)
                act.activation(G.AT[:, blk, c * CH:(c + 1) * CH], ps[:, n % 4, :], ACT.Copy).then_inc(read, 1)


def stage_out(nc, G, tag, products, row, keep=1.0, tiles=TILES):
    with ExitStack() as st:
        sem, sb, psum = makers(nc, st, tag)
        ps = psum("ps_y", [P, 4, CH], F32)
        made, added, biased, kept = sem("made"), sem("added"), sem("biased"), sem("kept")
        block = st.enter_context(nc.Block())

        @block.tensor
        def _(pe):
            for t in range(tiles):
                if t >= 4:
                    pe.wait_ge(added, t - 3)
                ops = products(t)
                for n, (lhsT, rhs) in enumerate(ops):
                    mm = pe.matmul(ps[:, t % 4, 0:D], lhsT, rhs, start=(n == 0), stop=(n == len(ops) - 1))
                mm.then_inc(made, 1)

        @block.gpsimd
        def _(pool):
            if row is not None:
                for t in range(tiles):
                    x = G.X[:, t, :]
                    if keep != 1.0:
                        pool.tensor_scalar(x, x, keep, None, ALU.mult).then_inc(kept, 1)
                        pool.wait_ge(kept, t + 1)
                    pool.tensor_tensor(x, x, G.rvec[:, row, :], ALU.add).then_inc(biased, 1)

        @block.vector
        def _(dve):
            for t in range(tiles):
                dve.wait_ge(made, t + 1)
                if row is not None:
                    dve.wait_ge(biased, t + 1)
                dve.tensor_tensor(G.X[:, t, :], ps[:, t % 4, 0:D], G.X[:, t, :], ALU.add).then_inc(added, 1)


def stage_resonance_out(nc, G):
    with ExitStack() as st:
        sem, sb, psum = makers(nc, st, "ro")
        ps = psum("ps_ro", [P, CHUNKS, CH], F32)
        made, read = sem("made"), sem("read")
        block = st.enter_context(nc.Block())

        @block.tensor
        def _(pe):
            for c in range(CHUNKS):
                for k in range(2):
                    mm = pe.matmul(ps[0:HARM, c, :], G.basis[:, k, 96:128], G.AT[:, k, c * CH:(c + 1) * CH],
                                   start=(k == 0), stop=(k == 1))
                mm.then_inc(made, 1)

        @block.scalar
        def _(act):
            for c in range(CHUNKS):
                act.wait_ge(made, c + 1)
                act.activation(G.ro[:, c * CH:(c + 1) * CH], ps[0:HARM, c, :], ACT.Copy).then_inc(read, 1)
            act.wait_ge(read, CHUNKS)


def stage_norm(nc, G, tag, src, tiles, width, dst, gain=None, shift=None, out=None, scratch=None):
    blks = width // P
    with ExitStack() as st:
        sem, sb, psum = makers(nc, st, tag)
        stats = sb("stats", [P, tiles, 6], F32)
        mv = sb("mean_var", [P, 2, tiles], F32)
        rstd = sb("rstd", [P, 2, tiles], F32)
        ps = psum("ps_turn", [P, 4, CH], F32)
        step, normed, turned, read, stored = sem("step"), sem("normed"), sem("turned"), sem("read"), sem("stored")
        block = st.enter_context(nc.Block())
        groups = [(g, blk) for g in range(tiles // 4) for blk in range(blks)]

        @block.vector
        def _(dve):
            link = linker(dve, step)
            for t in range(tiles):
                ins = dve.bn_stats(stats[:, t, :], src[:, t, 0:width])
                if t == tiles - 1:
                    link(ins)
            for t in range(tiles):
                ins = dve.bn_aggr(mv[:, :, t], stats[:, t, :])
                if t == tiles - 1:
                    link(ins)
            newton_rsqrt(dve, link, rstd[:, 0, :], mv[:, 1, :], rstd[:, 1, :])
            for t in range(tiles):
                dve.tensor_scalar(src[:, t, 0:width], src[:, t, 0:width], mv[:, 0, t:t + 1], rstd[:, 0, t:t + 1],
                                  ALU.subtract, ALU.mult).then_inc(normed, 1)

        if dst is not None:
            @block.tensor
            def _(pe):
                for n, (g, blk) in enumerate(groups):
                    pe.wait_ge(normed, 4 * g + 4)
                    if n >= 4:
                        pe.wait_ge(read, n - 3)
                    for q in range(4):
                        mm = pe.transpose(ps[:, n % 4, q * P:(q + 1) * P],
                                          src[:, 4 * g + q, blk * P:(blk + 1) * P], G.ident[:])
                    mm.then_inc(turned, 1)

            @block.scalar
            def _(act):
                for n, (g, blk) in enumerate(groups):
                    act.wait_ge(turned, n + 1)
                    out_ap = dst[:, blk, g * CH:(g + 1) * CH]
                    if gain is None:
                        act.activation(out_ap, ps[:, n % 4, :], ACT.Copy).then_inc(read, 1)
                    else:
                        act.activation(out_ap, ps[:, n % 4, :], ACT.Identity, bias=shift(blk, g),
                                       scale=gain(blk, g)).then_inc(read, 1)

        if scratch is not None or out is not None:
            @block.sync
            def _(sp):
                n = 0
                for t in range(0, TILES, 4):
                    sp.wait_ge(normed, t + 4)
                    for dram in (scratch, out):
                        if dram is not None:
                            sp.dma_start(dram[t:t + 4].rearrange("t p d -> p t d"), src[:, t:t + 4, :]).then_inc(stored, 16)
                            n += 16
                sp.wait_ge(stored, n)
                if out is not None:
                    sp.wait_ge(normed, tiles)


UNITS_A, UNITS_BC, UNITS_D = 4, 8, 2
UNITS = UNITS_A + 2 * UNITS_BC + UNITS_D
MB = HID // P


def stage_ffn0(nc, G):
    with ExitStack() as st:
        sem, sb, psum = makers(nc, st, "f0")
        raw = sb("w_raw", [P, 2, 1024], F32)
        w_hi, w_lo = sb("w_hi", [P, 2, 1024], F32R), sb("w_lo", [P, 2, 1024], F32R)
        x_hi, x_lo = sb("x_hi", [P, 2, CH], F32R), sb("x_lo", [P, 2, CH], F32R)
        h_hi, h_lo = sb("h_hi", [P, 2, MB, CH], F32R), sb("h_lo", [P, 2, MB, CH], F32R)
        full = sb("h_full", [P, 2, CH], F32)
        gate = sb("gate", [P, 2, CH], F32)
        y_tmp = sb("y_tmp", [P, 2, D], F32)
        pp = psum("ps_h", [P, 4, CH], F32)
        pd = psum("ps_y", [P, 4, CH], F32)
        w_in = [sem("w_in0"), sem("w_in1")]
        w_hi_done, w_lo_done = sem("w_hi"), sem("w_lo")
        x_hi_done, x_lo_done = sem("x_hi"), sem("x_lo")
        made, gate_done, full_done, hi_done, lo_done = sem("made"), sem("gate"), sem("full"), sem("hi"), sem("lo")
        y_made, y_done = sem("y_made"), sem("y_done")
        block = st.enter_context(nc.Block())
        TUR = 24
        units = G.ffn_units

        def each_chunk(eng, chunk):
            with eng.Fori(0, CHUNKS - 1) as c:
                chunk(c, False)
            chunk(CHUNKS - 1, True)

        @block.sync
        def _(sp):
            for u in range(2):
                sp.dma_start(raw[:, u, :], units[u]).then_inc(w_in[u], 16)

            def chunk(c, last):
                for u in range(UNITS - 2 * last):
                    sp.wait_ge(w_lo_done, c * UNITS + (u + 1))
                    sp.dma_start(raw[:, u % 2, :], units[(u + 2) % UNITS]).then_inc(w_in[u % 2], 16)
            each_chunk(sp, chunk)

        def split_hi(act, c, u):
            act.wait_ge(w_in[u % 2], c * (8 * UNITS) + 16 * (u // 2 + 1))
            act.activation(w_hi[:, u % 2, :], raw[:, u % 2, :], ACT.Copy).then_inc(w_hi_done, 1)

        def split_lo(dve, c, u):
            dve.wait_ge(w_hi_done, c * UNITS + (u + 1))
            dve.tensor_tensor(w_lo[:, u % 2, :], raw[:, u % 2, :], w_hi[:, u % 2, :].bitcast(F32),
                              ALU.subtract).then_inc(w_lo_done, 1)

        @block.tensor
        def _(pe):
            def three(out, wcols, slot, hi, lo, first, last):
                for n, (w, x) in enumerate(((w_hi, hi), (w_hi, lo), (w_lo, hi))):
                    mm = pe.matmul(out, w[:, slot, wcols], x, start=(first and n == 0), stop=(last and n == 2))
                return mm

            def chunk(c, last):
                for u in range(UNITS_A):
                    pe.wait_ge(w_lo_done, c * UNITS + (u + 1))
                    if u == 0:
                        pe.wait_ge(x_lo_done, c + 1)
                    for m in (2 * u, 2 * u + 1):
                        for w in range(2):
                            bank = 2 * m + w
                            if m >= 2:
                                pe.wait_ge(gate_done if w == 0 else full_done, c * 8 + (m - 1))
                            for k in range(2):
                                off = (m % 2) * 512 + w * 256 + k * P
                                mm = three(pp[:, bank % 4, :], slice(off, off + P), u % 2, x_hi[:, k, :], x_lo[:, k, :],
                                           k == 0, k == 1)
                            mm.then_inc(made, 1)
                for layer in range(2):
                    for m in range(MB):
                        u = UNITS_A + layer * UNITS_BC + m
                        tile = 8 + layer * 8 + m
                        pe.wait_ge(w_lo_done, c * UNITS + (u + 1))
                        if layer == 0 and m < 4:
                            pe.wait_ge(gate_done if m % 2 == 0 else full_done, c * 8 + (7 + m // 2))
                        else:
                            pe.wait_ge(hi_done, c * TUR + (tile - 3))
                        for k in range(MB):
                            if m == 0:
                                pe.wait_ge(lo_done, c * TUR + (layer * 8 + k + 1))
                            mm = three(pp[:, m % 4, :], slice(k * P, (k + 1) * P), u % 2, h_hi[:, layer, k, :],
                                       h_lo[:, layer, k, :], k == 0, k == MB - 1)
                        mm.then_inc(made, 1)
                for v in range(UNITS_D):
                    u = UNITS_A + 2 * UNITS_BC + v
                    pe.wait_ge(w_lo_done, c * UNITS + (u + 1))
                    for kk in range(4):
                        k = 4 * v + kk
                        pe.wait_ge(lo_done, c * TUR + (16 + k + 1))
                        for q in range(4):
                            for n, (h, w) in enumerate(((h_hi, w_hi), (h_hi, w_lo), (h_lo, w_hi))):
                                mm = pe.matmul(pd[:, q, 0:D], h[:, 0, k, q * P:(q + 1) * P],
                                               w[:, u % 2, kk * D:(kk + 1) * D], start=(k == 0 and n == 0),
                                               stop=(k == MB - 1 and n == 2))
                    mm.then_inc(y_made, 1)
            each_chunk(pe, chunk)

        MADE = 32

        @block.scalar
        def _(act):
            def free_hi(c, u, last):
                if last and u + 2 >= UNITS:
                    return
                if u < UNITS_A + 2 * UNITS_BC:
                    act.wait_ge(made, c * MADE + (4 * (u + 1) if u < UNITS_A else 16 + u - UNITS_A + 1))
                else:
                    act.wait_ge(y_made, c * 2 + (u - UNITS_A - 2 * UNITS_BC + 1))
                split_hi(act, c, u + 2)

            def chunk(c, last):
                act.activation(x_hi[:], G.xT[:, :, bass.ds(c * CH, CH)], ACT.Copy).then_inc(x_hi_done, 1)
                for u in range(UNITS_A):
                    for m in (2 * u, 2 * u + 1):
                        act.wait_ge(made, c * MADE + (2 * m + 1))
                        act.activation(gate[:, m % 2, :], pp[:, (2 * m) % 4, :], ACT.Silu,
                                       scale=G.ffn_s[:, 0, m:m + 1]).then_inc(gate_done, 1)
                        act.wait_ge(full_done, c * 8 + (m + 1))
                        act.activation(h_hi[:, 0, m, :], full[:, m % 2, :], ACT.Copy).then_inc(hi_done, 1)
                    free_hi(c, u, last)
                for layer in range(2):
                    for m in range(MB):
                        n = 8 + 8 * layer + m
                        act.wait_ge(made, c * MADE + (16 + 8 * layer + m + 1))
                        act.wait_ge(lo_done, c * TUR + (n - 1))
                        act.activation(full[:, m % 2, :], pp[:, m % 4, :], ACT.Gelu,
                                       scale=G.ffn_s[:, 2 + layer, m:m + 1])
                        act.activation(h_hi[:, 1 - layer, m, :], pp[:, m % 4, :], ACT.Gelu,
                                       scale=G.ffn_s[:, 2 + layer, m:m + 1]).then_inc(hi_done, 1)
                        free_hi(c, UNITS_A + layer * UNITS_BC + m, last)
                for v in range(UNITS_D):
                    free_hi(c, UNITS_A + 2 * UNITS_BC + v, last)
            for u in range(2):
                split_hi(act, 0, u)
            each_chunk(act, chunk)

        @block.vector
        def _(dve):
            def chunk(c, last):
                def next_lo(u):
                    if not (last and u + 2 >= UNITS):
                        split_lo(dve, c, u + 2)
                dve.wait_ge(x_hi_done, c + 1)
                dve.tensor_tensor(x_lo[:], G.xT[:, :, bass.ds(c * CH, CH)], x_hi[:].bitcast(F32),
                                  ALU.subtract).then_inc(x_lo_done, 1)
                for u in range(UNITS_A):
                    for m in (2 * u, 2 * u + 1):
                        dve.wait_ge(made, c * MADE + (2 * m + 2))
                        dve.wait_ge(gate_done, c * 8 + (m + 1))
                        dve.scalar_tensor_tensor(full[:, m % 2, :], pp[:, (2 * m + 1) % 4, :], G.ffn_s[:, 1, m:m + 1],
                                                 gate[:, m % 2, :], ALU.mult, ALU.mult).then_inc(full_done, 1)
                        dve.wait_ge(hi_done, c * TUR + (m + 1))
                        dve.tensor_tensor(h_lo[:, 0, m, :], full[:, m % 2, :], h_hi[:, 0, m, :].bitcast(F32),
                                          ALU.subtract).then_inc(lo_done, 1)
                    next_lo(u)
                for layer in range(2):
                    for m in range(MB):
                        dve.wait_ge(hi_done, c * TUR + (8 + 8 * layer + m + 1))
                        dve.tensor_tensor(h_lo[:, 1 - layer, m, :], full[:, m % 2, :],
                                          h_hi[:, 1 - layer, m, :].bitcast(F32), ALU.subtract).then_inc(lo_done, 1)
                        next_lo(UNITS_A + layer * UNITS_BC + m)
                next_lo(UNITS - 2)
                dve.wait_ge(y_made, c * 2 + 2)
                for q in range(4):
                    dve.tensor_tensor(y_tmp[:, q % 2, :], pd[:, q, 0:D], G.rvec[:, R_W3S, :], ALU.mult).then_inc(y_done, 1)
                    dve.wait_ge(y_done, c * 8 + (2 * q + 1))
                    dve.tensor_tensor(G.X[:, c * 4 + q, :], y_tmp[:, q % 2, :], G.X[:, c * 4 + q, :],
                                      ALU.add).then_inc(y_done, 1)
                next_lo(UNITS - 1)
            for u in range(2):
                split_lo(dve, 0, u)
            each_chunk(dve, chunk)


def stage_holographic(nc, G):
    with ExitStack() as st:
        sem, sb, psum = makers(nc, st, "lo")
        kq = sb("key_query", [P, 2, 2, CH], F32)
        val = sb("value", [P, 2, 2, CH], F32)
        th = sb("tanh", [P, 2, 2, 2, CH], F32)
        ph, turns = sb("phase", [P, 2, 2, CH], F32), sb("turns", [P, 2, 2, CH], F32)
        sn, cs = sb("sine", [P, 2, 2, CH], F32), sb("cosine", [P, 2, 2, CH], F32)
        bound, mem = sb("bound", [P, 2, 2, CH], F32), sb("memory", [P, 2, 2, CH], F32)
        keep = sb("keep", [P, CH], F32)
        vb = sb("value_bias", [P, 2], F32)
        ps = psum("ps_lo", [P, 8, CH], F32)
        const, made, read = sem("const"), sem("made"), sem("read")
        step, reduced, trig, magnitude = sem("step"), sem("reduced"), sem("trig"), sem("magnitude")
        bound_done, scanned, mixed, filed = sem("bound"), sem("scanned"), sem("mixed"), sem("filed")
        block = st.enter_context(nc.Block())
        TILES_C = 10
        units = [(c, blk) for c in range(CHUNKS) for blk in range(2)]

        @block.gpsimd
        def _(pool):
            pool.memset(keep[:], 1.0).then_inc(const, 1)
            pool.wait_ge(const, 1)
            pool.memset(keep[:].rearrange("p (g t) -> p g t", t=SCAN)[:, :, 0:1], 0.0).then_inc(const, 1)
            pool.tensor_scalar(vb[:], G.fvec[:, V_LBV, :], 1.0 / 16, None, ALU.mult).then_inc(const, 1)

            def bind(n):
                c, blk = units[n]
                pool.wait_ge(trig, 2 * n + 2)
                for part, src in enumerate((cs, sn)):
                    pool.tensor_tensor(bound[:, n % 2, part, :], val[:, c % 2, blk, :], src[:, n % 2, 0, :],
                                       ALU.mult).then_inc(bound_done, 1)

            def retrieve(n):
                pool.wait_ge(scanned, 2 * n + 2)
                for part, src in enumerate((cs, sn)):
                    pool.tensor_tensor(mem[:, n % 2, part, :], mem[:, n % 2, part, :], src[:, n % 2, 1, :],
                                       ALU.mult).then_inc(mixed, 1)
            for n in range(len(units)):
                bind(n)
                retrieve(n)

        @block.tensor
        def _(pe):
            n = 0
            for c in range(CHUNKS):
                for which, mat in enumerate((M_LK, M_LQ, M_LV, M_LKP, M_LQP)):
                    for blk in range(2):
                        if n >= 8:
                            pe.wait_ge(read, n - 7)
                        if which >= 3:
                            pe.wait_ge(read, c * TILES_C + (2 if which == 3 else 4))
                        for k in range(2):
                            rhs = kq[:, which - 3, k, :] if which >= 3 else G.xT[:, k, c * CH:(c + 1) * CH]
                            mm = pe.matmul(ps[:, n % 8, :], G.wmat[:, mat, k, blk * P:(blk + 1) * P], rhs,
                                           start=(k == 0), stop=(k == 1))
                        mm.then_inc(made, 1)
                        n += 1

        @block.scalar
        def _(act):
            act.wait_ge(const, 3)

            def trigonometry(n):
                act.wait_ge(reduced, n + 1)
                if n >= 2:
                    act.wait_ge(mixed, 2 * n - 2)
                act.activation(turns[:, n % 2], ph[:, n % 2], ACT.Abs).then_inc(magnitude, 1)
                act.activation(sn[:, n % 2], ph[:, n % 2], ACT.Sin).then_inc(trig, 1)
                act.wait_ge(magnitude, n + 1)
                act.activation(cs[:, n % 2], turns[:, n % 2], ACT.Sin, bias=G.halfpi[:, 0:1],
                               scale=-1.0).then_inc(trig, 1)
            n = 0
            for c in range(CHUNKS):
                for which, vec in enumerate((V_LBK, V_LBQ, V_LBV, V_LBKP, V_LBQP)):
                    for blk in range(2):
                        act.wait_ge(made, n + 1)
                        src = ps[:, n % 8, :]
                        if which < 2:
                            act.activation(kq[:, which, blk, :], src, ACT.Identity,
                                           bias=G.fvec[:, vec, blk:blk + 1]).then_inc(read, 1)
                        elif which == 2:
                            if c >= 2:
                                act.wait_ge(bound_done, 4 * (c - 1))
                            act.activation(val[:, c % 2, blk, :], src, ACT.Identity, bias=vb[:, blk:blk + 1],
                                           scale=1.0 / 16).then_inc(read, 1)
                        else:
                            if c >= 2:
                                act.wait_ge(reduced, 2 * (c - 1))
                            act.activation(th[:, c % 2, which - 3, blk, :], src, ACT.Tanh,
                                           bias=G.fvec[:, vec, blk:blk + 1]).then_inc(read, 1)
                        n += 1
                if c >= 1:
                    trigonometry(2 * c - 2)
                    trigonometry(2 * c - 1)
            trigonometry(2 * CHUNKS - 2)
            trigonometry(2 * CHUNKS - 1)

        @block.vector
        def _(dve):
            link = linker(dve, step)

            def reduce_phase(n):
                c, blk = units[n]
                dve.wait_ge(read, (c + 1) * TILES_C - (1 - blk))
                if n >= 2:
                    dve.wait_ge(trig, 2 * n - 2)
                p, k = ph[:, n % 2], turns[:, n % 2]
                link(dve.tensor_scalar(p, th[:, c % 2, :, blk, :], G.fvec[:, V_PS, blk:blk + 1], None, ALU.mult))
                link(dve.tensor_scalar(k, p, 1.0 / TWO_PI, ROUND, ALU.mult, ALU.add))
                link(dve.tensor_scalar(k, k, -ROUND, None, ALU.add))
                for cst in (C1, C2, C3):
                    link(dve.scalar_tensor_tensor(p, k, -cst, p, ALU.mult, ALU.add))
                dve.tensor_scalar(p, p, PI_IN, -PI_IN, ALU.min, ALU.max).then_inc(reduced, 1)

            def scan(n):
                dve.wait_ge(bound_done, 2 * n + 2)
                if n >= 2:
                    dve.wait_ge(filed, n - 1)
                for part in range(2):
                    dve.tensor_tensor_scan(mem[:, n % 2, part, :], keep[:], bound[:, n % 2, part, :], 0.0,
                                           ALU.mult, ALU.add).then_inc(scanned, 1)

            def file(n):
                c, blk = units[n]
                dve.wait_ge(mixed, 2 * n + 2)
                dve.tensor_tensor(G.AT[:, blk, c * CH:(c + 1) * CH], mem[:, n % 2, 0, :], mem[:, n % 2, 1, :],
                                  ALU.add).then_inc(filed, 1)
            N = len(units)
            dve.wait_ge(const, 3)
            for n in range(N + 2):
                if n < N:
                    reduce_phase(n)
                if 1 <= n <= N:
                    scan(n - 1)
                if n >= 2:
                    file(n - 2)


def stage_turn_back(nc, G, tag, src, tiles, dst):
    with ExitStack() as st:
        sem, sb, psum = makers(nc, st, tag)
        ps = psum("ps_back", [P, 4, CH], F32)
        turned, read = sem("turned"), sem("read")
        block = st.enter_context(nc.Block())

        @block.tensor
        def _(pe):
            for n in range(tiles // 2):
                if n >= 4:
                    pe.wait_ge(read, n - 3)
                for q in range(2):
                    for k in range(2):
                        t = 2 * n + q
                        mm = pe.transpose(ps[:, n % 4, q * D + k * P:q * D + (k + 1) * P], src[:, k, t * P:(t + 1) * P],
                                          G.ident[:])
                mm.then_inc(turned, 1)

        @block.scalar
        def _(act):
            for n in range(tiles // 2):
                act.wait_ge(turned, n + 1)
                act.activation(dst[:, 2 * n:2 * n + 2, :].rearrange("p t d -> p (t d)"), ps[:, n % 4, :],
                               ACT.Copy).then_inc(read, 1)


def stage_gather(nc, I, G):
    with ExitStack() as st:
        sem, sb, psum = makers(nc, st, "ga")
        col_i = sb("col_i", [P, 2, MT], I32)
        row_i = sb("row_i", [P, 2, NMOE], I32)
        col_f, row_f = sb("col_f", [P, 2, MT], F32), sb("row_f", [P, 2, NMOE], F32)
        rows = sb("row_token", [P, NMOE], F32)
        same = sb("same", [P, MT, NMOE], F32)
        dup = sb("dup", [P, MT], F32)
        loaded, gathered = sem("loaded"), sem("gathered")
        step, same_done, kept, turned, read = sem("step"), sem("same"), sem("kept"), sem("turned"), sem("read")
        tok_done = sem("tok")
        ps = psum("ps_ga", [P, 2, CH], F32)
        block = st.enter_context(nc.Block())

        @block.sync
        def _(sp):
            for n, name in enumerate(("index_b", "index_t")):
                with nc.allow_non_contiguous_dma(reason="512 indices"):
                    sp.dma_start(col_i[:, n, :], I[name].rearrange("(q p) -> p q", p=P)).then_inc(loaded, 16)
                sp.dma_start(row_i[:, n, :], I[name].rearrange("(o m) -> o m", o=1).broadcast_to([P, NMOE])).then_inc(loaded, 16)
            for k in range(2):
                sp.dma_start(G.ew1[:, k, :], I["ew1"][k]).then_inc(loaded, 16)
                sp.dma_start(G.ew2[:, k, :], I["ew2"][k]).then_inc(loaded, 16)
            sp.dma_start(G.ew3[:], I["ew3"]).then_inc(loaded, 16)
            sp.dma_start(G.sw12[:], I["sw12"].rearrange("k p c -> p k c")).then_inc(loaded, 16)
            sp.dma_start(G.sw3[:], I["sw3"]).then_inc(loaded, 16)
            sp.dma_start(G.gw[:], I["gw"].rearrange("k p c -> p k c")).then_inc(loaded, 16)
            sp.dma_start(G.eb[:], I["eb"]).then_inc(loaded, 16)
            sp.wait_ge(loaded, 16 * 13)

        @block.vector
        def _(dve):
            link = linker(dve, step)
            dve.wait_ge(loaded, 16 * 13)
            link(dve.tensor_copy(col_f[:], col_i[:]))
            link(dve.tensor_copy(row_f[:], row_i[:]))
            link(dve.scalar_tensor_tensor(G.tok_f[:], col_f[:, 0, :], float(S), col_f[:, 1, :], ALU.mult, ALU.add))
            dve.tensor_copy(G.tok[:], G.tok_f[:]).then_inc(tok_done, 1)
            link(dve.scalar_tensor_tensor(rows[:], row_f[:, 0, :], float(S), row_f[:, 1, :], ALU.mult, ALU.add))
            for q in range(MT):
                dve.tensor_scalar(same[:, q, :], rows[:], G.tok_f[:, q:q + 1], None, ALU.is_equal).then_inc(same_done, 1)
            dve.wait_ge(kept, MT)
            link(dve.tensor_reduce(dup[:], same[:], AX_X, ALU.max))
            link(dve.scalar_tensor_tensor(G.tok_f[:], dup[:], float(2 * TOK), G.tok_f[:], ALU.mult, ALU.add))
            link(dve.tensor_copy(G.tok_once[:], G.tok_f[:]))

        @block.gpsimd
        def _(pool):
            pool.wait_ge(tok_done, 1)
            for q in range(MT):
                pool.indirect_dma_start(G.X[:, TILES + q, :], None, G.x_dram.rearrange("t p d -> (t p) d"),
                                        bass.IndirectOffsetOnAxis(ap=G.tok[:, q:q + 1], axis=0)).then_inc(gathered, 16)
            for q in range(MT):
                pool.wait_ge(same_done, q + 1)
                pool.affine_select(out=same[:, q, :], in_=same[:, q, :], compare_op=ALU.is_gt, fill=0.0, base=q * P,
                                   pattern=[[-1, NMOE]], channel_multiplier=1).then_inc(kept, 1)

        @block.tensor
        def _(pe):
            pe.wait_ge(gathered, 16 * MT)
            for blk in range(2):
                for q in range(MT):
                    mm = pe.transpose(ps[:, blk, q * P:(q + 1) * P], G.X[:, TILES + q, blk * P:(blk + 1) * P], G.ident[:])
                mm.then_inc(turned, 1)

        @block.scalar
        def _(act):
            for blk in range(2):
                act.wait_ge(turned, blk + 1)
                act.activation(G.xT[:, blk, TOK:TOK + NMOE], ps[:, blk, :], ACT.Copy).then_inc(read, 1)


def stage_shared_hidden(nc, G):
    with ExitStack() as st:
        sem, sb, psum = makers(nc, st, "sh")
        h = sb("sh_h", [P, 4, D], F32)
        ps = psum("ps_sh", [P, 4, CH], F32)
        made, biased, silu, z_done = sem("made"), sem("biased"), sem("silu"), sem("z")
        block = st.enter_context(nc.Block())

        @block.tensor
        def _(pe):
            for t in range(XT):
                if t >= 4:
                    pe.wait_ge(biased, t - 3)
                for k in range(2):
                    mm = pe.matmul(ps[:, t % 4, 0:D], G.xT[:, k, t * P:(t + 1) * P], G.sw12[:, k, :],
                                   start=(k == 0), stop=(k == 1))
                mm.then_inc(made, 1)

        @block.vector
        def _(dve):
            for t in range(XT):
                dve.wait_ge(made, t + 1)
                if t >= 4:
                    dve.wait_ge(z_done, t - 3)
                dve.tensor_tensor(h[:, t % 4, :], ps[:, t % 4, 0:D], G.rvec[:, R_SB12, :], ALU.add).then_inc(biased, 1)

        @block.scalar
        def _(act):
            for t in range(XT):
                act.wait_ge(biased, t + 1)
                act.activation(G.Z[:, t, :], h[:, t % 4, 0:EH], ACT.Silu).then_inc(silu, 1)

        @block.gpsimd
        def _(pool):
            for t in range(XT):
                pool.wait_ge(silu, t + 1)
                pool.tensor_tensor(G.Z[:, t, :], G.Z[:, t, :], h[:, t % 4, EH:D], ALU.mult).then_inc(z_done, 1)


def stage_shared_out(nc, G):
    with ExitStack() as st:
        sem, sb, psum = makers(nc, st, "so")
        ps = psum("ps_so", [P, 4, CH], F32)
        made, added, biased = sem("made"), sem("added"), sem("biased")
        block = st.enter_context(nc.Block())

        @block.tensor
        def _(pe):
            for t in range(XT):
                if t >= 4:
                    pe.wait_ge(added, t - 3)
                pe.matmul(ps[:, t % 4, 0:D], G.ZT[:, 0, t * P:(t + 1) * P], G.sw3[:], start=True, stop=True).then_inc(made, 1)

        @block.gpsimd
        def _(pool):
            for t in range(TILES):
                pool.tensor_tensor(G.X[:, t, :], G.X[:, t, :], G.rvec[:, R_SB3, :], ALU.add).then_inc(biased, 1)

        @block.vector
        def _(dve):
            for t in range(XT):
                dve.wait_ge(made, t + 1)
                if t < TILES:
                    dve.wait_ge(biased, t + 1)
                    dve.tensor_tensor(G.X[:, t, :], ps[:, t % 4, 0:D], G.X[:, t, :], ALU.add).then_inc(added, 1)
                else:
                    dve.tensor_tensor(G.shared_g[:, t - TILES, :], ps[:, t % 4, 0:D], G.rvec[:, R_SB3, :],
                                      ALU.add).then_inc(added, 1)


def stage_experts(nc, G):
    with ExitStack() as st:
        sem, sb, psum = makers(nc, st, "ex")
        logits, scores = sb("logits", [P, MT, 9], F32), sb("scores", [P, MT, 9], F32)
        choice, best = sb("choice", [P, MT, NEXP], F32), sb("best", [P, MT, NEXP], F32)
        best_i = sb("best_i", [P, MT, NEXP], U32)
        best_f = sb("best_f", [P, MT], F32)
        lane_i, lane = sb("lane_i", [P, NEXP], I32), sb("lane", [P, NEXP], F32)
        onehot = sb("onehot", [P, MT, NEXP], F32)
        onehotT = sb("onehotT", [NEXP, MT, P], F32)
        pair, top = sb("pair", [P, MT, 2], F32), sb("top", [P, MT, NEXP], F32)
        pmax, psums = sb("pmax", [P, MT], F32), sb("psums", [P, MT], F32)
        bias = sb("bias", [P, MT, 2 * D], F32)
        hsel = sb("hsel", [P, MT, 2, EH], F32)
        ze = sb("ze", [P, MT, EH], F32)
        zeT = sb("zeT", [P, NMOE], F32)
        yexp = sb("yexp", [P, MT, D], F32)
        stats, mv, rstd = sb("stats", [P, MT, 6], F32), sb("mv", [P, 2, MT], F32), sb("rstd", [P, 2, MT], F32)
        ph = psum("ps_h", [P, 4, CH], F32)
        pg = psum("ps_g", [P, CH], F32)
        pt = psum("ps_t", [P, CH], F32)
        pb = psum("ps_b", [P, CH], F32)
        step, gates_made, logit_done, score_done, hot_done = sem("step"), sem("gates"), sem("logit"), sem("score"), sem("hot")
        hotT_made, hotT_read, bias_made, bias_read = sem("hotT"), sem("hotTr"), sem("biasm"), sem("biasr")
        h_made, h_read, silu, z_normed, zT_made, zT_read = sem("h"), sem("hr"), sem("silu"), sem("zn"), sem("zT"), sem("zTr")
        y_made, y_read, lanes, pmax_done, pair_done = sem("y"), sem("yr"), sem("lanes"), sem("pmax"), sem("pair")
        block = st.enter_context(nc.Block())

        @block.gpsimd
        def _(pool):
            pool.iota(lane_i[:], pattern=[[1, NEXP]], base=0, channel_multiplier=0).then_inc(lanes, 1)

        @block.tensor
        def _(pe):
            for q in range(MT):
                for k in range(2):
                    mm = pe.matmul(pg[:, q * 16:q * 16 + 9], G.xT[:, k, TOK + q * P:TOK + (q + 1) * P], G.gw[:, k, :],
                                   start=(k == 0), stop=(k == 1))
            mm.then_inc(gates_made, 1)
            for q in range(MT):
                if q >= 1:
                    pe.wait_ge(h_read, q)
                for w, wt in enumerate((G.ew1, G.ew2)):
                    for h in range(2):
                        for k in range(2):
                            mm = pe.matmul(ph[:, 2 * w + h, :], G.xT[:, k, TOK + q * P:TOK + (q + 1) * P],
                                           wt[:, k, h * CH:(h + 1) * CH], start=(k == 0), stop=(k == 1))
                mm.then_inc(h_made, 1)
                if q == 0:
                    pe.wait_ge(hot_done, 1)
                    for p in range(MT):
                        mm2 = pe.transpose(pt[0:NEXP, p * P:(p + 1) * P], onehot[:, p, :], G.ident[:])
                    mm2.then_inc(hotT_made, 1)
                    pe.wait_ge(hotT_read, 1)
                if q >= 1:
                    pe.wait_ge(bias_read, q)
                pe.matmul(pb[:], onehotT[:, q, :], G.eb[:], start=True, stop=True).then_inc(bias_made, 1)
            for q in range(MT):
                pe.wait_ge(z_normed, q + 1)
                pe.transpose(pt[:, q * P:(q + 1) * P], ze[:, q, :], G.ident[:]).then_inc(zT_made, 1)
            pe.wait_ge(h_read, MT)
            pe.wait_ge(zT_read, 1)
            for q in range(MT):
                if q >= 1:
                    pe.wait_ge(y_read, q)
                for h in range(4):
                    mm = pe.matmul(ph[:, h, :], zeT[:, q * P:(q + 1) * P], G.ew3[:, h * CH:(h + 1) * CH], start=True, stop=True)
                mm.then_inc(y_made, 1)

        @block.scalar
        def _(act):
            act.wait_ge(logit_done, 1)
            act.activation(scores[:], logits[:], ACT.Sigmoid).then_inc(score_done, 1)
            act.wait_ge(hotT_made, 1)
            act.activation(onehotT[:], pt[0:NEXP, :].rearrange("e (q p) -> e q p", q=MT), ACT.Copy).then_inc(hotT_read, 1)
            for q in range(MT):
                act.wait_ge(bias_made, q + 1)
                act.activation(bias[:, q, :], pb[:], ACT.Copy).then_inc(bias_read, 1)
                act.wait_ge(h_read, q + 1)
                act.activation(ze[:, q, :], hsel[:, q, 0, :], ACT.Silu).then_inc(silu, 1)
            act.wait_ge(pmax_done, 1)
            for q in range(MT):
                act.activation(pair[:, q, :], pair[:, q, :], ACT.Exp, bias=pmax[:, q:q + 1],
                               accum_out=psums[:, q:q + 1]).then_inc(pair_done, 1)
            act.wait_ge(zT_made, MT)
            act.activation(zeT[:], pt[:], ACT.Identity, bias=G.evec[:, 3:4], scale=G.evec[:, 2:3]).then_inc(zT_read, 1)

        @block.vector
        def _(dve):
            link = linker(dve, step)
            link(dve.memset(pair[:], 0.0))
            dve.wait_ge(lanes, 1)
            link(dve.tensor_copy(lane[:], lane_i[:]))
            dve.wait_ge(gates_made, 1)
            dve.tensor_tensor(logits[:], pg[:, 0:16 * MT].rearrange("p (q c) -> p q c", q=MT)[:, :, 0:9],
                              G.grow[:, 0:9].rearrange("p (o c) -> p o c", o=1).broadcast_to([P, MT, 9]),
                              ALU.add).then_inc(logit_done, 1)
            dve.wait_ge(score_done, 1)
            link(dve.tensor_tensor(choice[:], scores[:, :, 1:9],
                                   G.grow[:, 9:17].rearrange("p (o c) -> p o c", o=1).broadcast_to([P, MT, NEXP]), ALU.add))
            for q in range(MT):
                link(dve.max(best[:, q, :], choice[:, q, :]))
                link(dve.max_index(best_i[:, q, :], best[:, q, :], choice[:, q, :]))
            link(dve.tensor_copy(best_f[:], best_i[:, :, 0]))
            for q in range(MT):
                link(dve.tensor_scalar(onehot[:, q, :], lane[:], best_f[:, q:q + 1], None, ALU.is_equal))
            dve.sem_inc(hot_done, 1)
            link(dve.tensor_tensor(top[:], scores[:, :, 1:9], onehot[:], ALU.mult))
            link(dve.tensor_copy(pair[:, :, 0:1], scores[:, :, 0:1]))
            link(dve.tensor_reduce(pair[:, :, 1:2], top[:], AX_X, ALU.add))
            dve.tensor_reduce(pmax[:], pair[:], AX_X, ALU.max, negate=True).then_inc(pmax_done, 1)
            for q in range(MT):
                dve.wait_ge(h_made, q + 1)
                dve.wait_ge(bias_read, q + 1)
                for w in range(2):
                    out = hsel[:, q, w, :]
                    for e in range(NEXP):
                        src = ph[:, 2 * w + e // 4, (e % 4) * EH:(e % 4 + 1) * EH]
                        prev = bias[:, q, w * EH:(w + 1) * EH] if e == 0 else out
                        link(dve.scalar_tensor_tensor(out, src, onehot[:, q, e:e + 1], prev, ALU.mult, ALU.add))
                dve.sem_inc(h_read, 1)
                dve.wait_ge(silu, q + 1)
                link(dve.tensor_tensor(ze[:, q, :], ze[:, q, :], hsel[:, q, 1, :], ALU.mult))
                link(dve.bn_stats(stats[:, q, :], ze[:, q, :]))
                link(dve.bn_aggr(mv[:, :, q], stats[:, q, :]))
            newton_rsqrt(dve, link, rstd[:, 0, :], mv[:, 1, :], rstd[:, 1, :])
            for q in range(MT):
                dve.tensor_scalar(ze[:, q, :], ze[:, q, :], mv[:, 0, q:q + 1], rstd[:, 0, q:q + 1],
                                  ALU.subtract, ALU.mult).then_inc(z_normed, 1)
            dve.wait_ge(pair_done, MT)
            link(dve.reciprocal(psums[:], psums[:]))
            link(dve.tensor_tensor(pair[:], pair[:], psums[:].rearrange("p (q o) -> p q o", o=1).broadcast_to([P, MT, 2]),
                                   ALU.mult))
            for q in range(MT):
                dve.wait_ge(y_made, q + 1)
                for e in range(NEXP):
                    src = ph[:, e // 2, (e % 2) * D:(e % 2 + 1) * D]
                    prev = bias[:, q, D:2 * D] if e == 0 else yexp[:, q, :]
                    link(dve.scalar_tensor_tensor(yexp[:, q, :], src, onehot[:, q, e:e + 1], prev, ALU.mult, ALU.add))
                dve.sem_inc(y_read, 1)
                x = G.X[:, TILES + q, :]
                link(dve.scalar_tensor_tensor(x, G.shared_g[:, q, :], pair[:, q, 0:1], x, ALU.mult, ALU.add))
                link(dve.scalar_tensor_tensor(x, yexp[:, q, :], pair[:, q, 1:2], x, ALU.mult, ALU.add))


def stage_scatter(nc, G, out):
    with ExitStack() as st:
        done = st.enter_context(nc.semaphore("sc_done"))
        block = st.enter_context(nc.Block())

        @block.gpsimd
        def _(pool):
            for q in range(MT):
                pool.indirect_dma_start(out.rearrange("t p d -> (t p) d"),
                                        bass.IndirectOffsetOnAxis(ap=G.tok_once[:, q:q + 1], axis=0),
                                        G.X[:, TILES + q, :], None, bounds_check=TOK - 1, oob_is_err=False).then_inc(done, 16)
            pool.wait_ge(done, 16 * MT)


class Shared:

    def __init__(self, nc, st):
        sb = lambda *a: st.enter_context(nc.sbuf_tensor(*a))
        self.X = sb("X", [P, XT, D], F32)
        self.xT = sb("xT", [P, 2, TOK + NMOE], F32)
        self.ident = sb("ident", [P, P], F32)
        self.halfpi = sb("halfpi", [P, 1], F32)
        self.wmat = sb("wmat", [P, 14, 2, D], F32)
        self.fvec, self.evec = sb("fvec", [P, 10, 2], F32), sb("evec", [P, 4], F32)
        self.rvec, self.grow = sb("rvec", [P, NROWS, D], F32), sb("grow", [P, 17], F32)
        self.ffn_s = sb("ffn_s", [P, 4, MB], F32)
        self.tok, self.tok_once, self.tok_f = sb("tok", [P, MT], U32), sb("tok_once", [P, MT], U32), sb("tok_f", [P, MT], F32)
        dram = lambda name, shape, dt: nc.dram_tensor(name, shape, dt).ap()
        self.q_dram = dram("q_parts", [3, B, D, S], BF16)
        self.k_dram = dram("k_parts", [3, B, D, S], BF16)
        self.qx_dram = dram("qx_parts", [3, B, D, S], BF16)
        self.kx_dram = dram("kx_parts", [3, B, D, SK], BF16)
        self.x_dram = dram("x_rows", [TILES, P, D], F32)


def decoder_kernel(nc, I, out):
    with ExitStack() as st:
        G = Shared(nc, st)
        G.ffn_units, G.mask = I["ffn_units"], I["mask"]
        tile = lambda t: slice(t * P, (t + 1) * P)

        def out_products(mat):
            return lambda t: [(G.AT[:, k, tile(t)], G.wmat[:, mat, k, :]) for k in range(2)]

        def norm_x(tag, **kw):
            stage_norm(nc, G, tag, G.X, TILES, D, G.xT, **kw)

        with ExitStack() as st0:
            sb = lambda *a: st0.enter_context(nc.sbuf_tensor(*a))
            G.basis, G.holo = sb("basis", [P, 2, P], F32), sb("holo", [96, 2, 2, D], F32)
            G.V = sb("V", [P, SLOTS, TPB, DH], F32)
            G.ctxT, G.Vx = sb("ctxT", [P, 2, B * SK], F32), sb("Vx", [P, SLOTS, 2, DH], F32)
            G.ro = sb("ro", [HARM, TOK], F32)
            G.A, G.AT = sb("A", [P, TPB, B * D], F32), sb("AT", [P, 2, TOK], F32)
            stage_setup(nc, I, G)
            stage_project_self(nc, G)
            stage_attention(nc, G, "a0")
            stage_turn(nc, G, "t0")
            stage_resonance_out(nc, G)
            stage_out(nc, G, "o0", lambda t: [(G.ro[:, tile(t)], G.holo[0:HARM, 0, 1, :])], None)
            norm_x("n0")
            clear_used(nc)
            stage_project_cross(nc, G, "p1", M_X0Q, M_X0K, M_X0V, 1.0 / 16, None, None, None)
            stage_attention_over_queries(nc, G)
            stage_turn(nc, G, "t1")
            stage_out(nc, G, "o1", out_products(M_X0O), None)
            norm_x("n1")
        stage_ffn0(nc, G)
        norm_x("n2")
        clear_used(nc)
        sb = lambda *a: st.enter_context(nc.sbuf_tensor(*a))
        G.A, G.AT = sb("A_l1", [P, TPB, B * D], F32), sb("AT_l1", [P, 2, TOK], F32)
        stage_holographic(nc, G)
        az = G.A[:].rearrange("p t (b d) -> p (t b) d", d=D)
        stage_turn_back(nc, G, "b3", G.AT, TILES, az)
        stage_norm(nc, G, "m3", az, TILES, D, G.AT, gain=lambda k, g: G.fvec[:, V_LG, k:k + 1],
                   shift=lambda k, g: G.fvec[:, V_LB, k:k + 1])
        stage_out(nc, G, "o3", out_products(M_LO), R_LBO, keep=2.0)
        norm_x("n3")
        with ExitStack() as st0:
            sb = lambda *a: st0.enter_context(nc.sbuf_tensor(*a))
            G.ctxT, G.Vx = sb("ctxT2", [P, 2, B * SK], F32), sb("Vx2", [P, SLOTS, 2, DH], F32)
            stage_reload_context(nc, I, G)
            stage_project_cross(nc, G, "p4", M_X1Q, M_X1K, M_X1V, DH ** -0.5, V_X1BQ, V_X1BK, R_X1BV)
            stage_attention_cross(nc, G, "a4")
            stage_turn(nc, G, "t4")
            stage_out(nc, G, "o4", out_products(M_X1O), R_X1BO)
        norm_x("n4", scratch=G.x_dram)
        clear_used(nc)
        sb = lambda *a: st.enter_context(nc.sbuf_tensor(*a))
        G.ew1, G.ew2 = sb("ew1", [P, 2, NEXP * EH], F32), sb("ew2", [P, 2, NEXP * EH], F32)
        G.ew3, G.sw12, G.sw3 = sb("ew3", [P, NEXP * D], F32), sb("sw12", [P, 2, D], F32), sb("sw3", [P, D], F32)
        G.gw, G.eb = sb("gw", [P, 2, 9], F32), sb("eb", [NEXP, 2 * D], F32)
        G.Z, G.ZT = sb("Z", [P, XT, EH], F32), sb("ZT", [P, 1, TOK + NMOE], F32)
        G.shared_g = sb("shared_g", [P, MT, D], F32)
        stage_gather(nc, I, G)
        stage_shared_hidden(nc, G)
        stage_norm(nc, G, "m5", G.Z, XT, EH, G.ZT, gain=lambda k, g: G.evec[:, 0:1], shift=lambda k, g: G.evec[:, 1:2])
        stage_shared_out(nc, G)
        stage_experts(nc, G)
        stage_norm(nc, G, "n5", G.X, XT, D, None, out=out)
        stage_scatter(nc, G, out)


def stage_reload_context(nc, I, G):
    with ExitStack() as st:
        loaded = st.enter_context(nc.semaphore("ctx_loaded"))
        block = st.enter_context(nc.Block())

        @block.sync
        def _(sp):
            sp.dma_start(G.ctxT[:], I["ctx_fm"].rearrange("k p t -> p k t")).then_inc(loaded, 16)
            sp.wait_ge(loaded, 16)


def kernel(**inputs):
    import numpy as _np
    import concourse.bacc as _bacc
    from concourse import mybir as _mybir
    from concourse.bass_utils import run_bass_kernel_spmd as _run

    a = {k: _np.asarray(v) for k, v in inputs.items()}

    def fm(w):
        return w.reshape(w.shape[0] // 128, 128, -1).transpose(1, 0, 2)

    def col(v):
        return v.reshape(-1, 128).T

    x = a["x"].reshape(2048, 256)
    mats = [a["L0_xattn_Wq"].T, a["L0_xattn_Wk"].T, a["L0_xattn_Wv"].T, a["L0_xattn_Wo"].T,
            a["L1_attn_Wk"].T, a["L1_attn_Wv"].T, a["L1_attn_Wq"].T, a["L1_attn_Wkp"].T, a["L1_attn_Wqp"].T,
            a["L1_attn_Wo"].T, a["L1_xattn_Wq"], a["L1_xattn_Wk"], a["L1_xattn_Wv"], a["L1_xattn_Wo"]]
    w1, w2 = fm(a["L0_ffn_w1_w"].T), fm(a["L0_ffn_w2_w"].T)
    h1, h2, w3 = fm(a["L0_ffn_h1_w"].T), fm(a["L0_ffn_h2_w"].T), fm(a["L0_ffn_w3_w"].T)
    units = [_np.concatenate([w[:, k, m * 128:(m + 1) * 128] for m in (2 * u, 2 * u + 1) for w in (w1, w2)
                              for k in range(2)], axis=1) for u in range(4)]
    units += [h[:, :, m * 128:(m + 1) * 128].reshape(128, 1024) for h in (h1, h2) for m in range(8)]
    units += [w3[:, 4 * v:4 * v + 4, :].reshape(128, 1024) for v in range(2)]
    experts = lambda w: w.transpose(2, 0, 1).reshape(w.shape[2], -1)
    arrays = {
        "x_tm": x.reshape(16, 128, 256),
        "x_fm": x.T.reshape(2, 128, 2048),
        "ctx_fm": a["ctx_1024"].reshape(308, 256).T.reshape(2, 128, 308),
        "mask": a["mask_Bx1xS2_ik0"].reshape(2, 154),
        "basis": _np.concatenate([a["L0_attn_basis_" + c] for c in "qkvo"]).T.reshape(2, 128, 128),
        "phase_qkv": _np.concatenate([a["L0_attn_phase_" + c].T for c in "qkv"]),
        "amp_qkv": _np.concatenate([a["L0_attn_amp_" + c].T for c in "qkv"]),
        "phase_o": a["L0_attn_phase_o"].T, "amp_o": a["L0_attn_amp_o"].T,
        "wmat": _np.stack([fm(m) for m in mats], axis=1),
        "fvec": _np.stack([col(a[n]) for n in ("L1_attn_bk", "L1_attn_bv", "L1_attn_bq", "L1_attn_bkp", "L1_attn_bqp",
                                               "L1_attn_phase_scale", "L1_attn_ln_g", "L1_attn_ln_b",
                                               "L1_xattn_bq", "L1_xattn_bk")], axis=1),
        "evec": _np.stack([a["L1_ffn_" + n] for n in ("s_ln_g", "s_ln_b", "sel_ln_g", "sel_ln_b")], axis=1),
        "rvec": _np.stack([a["L1_attn_bo"], a["L1_xattn_bv"], a["L1_xattn_bo"], a["L0_ffn_w3_s"], a["L1_ffn_sb3"],
                           _np.concatenate([a["L1_ffn_sb1"], a["L1_ffn_sb2"]])]),
        "grow": _np.concatenate([a["L1_ffn_sg_b"], a["L1_ffn_eg_b"], a["L1_ffn_exp_bias"]]),
        "ffn_s": _np.stack([col(a["L0_ffn_" + n]) for n in ("w1_s", "w2_s", "h1_s", "h2_s")], axis=1),
        "ffn_units": _np.stack(units),
        "index_b": a["L1_ffn_index_b"], "index_t": a["L1_ffn_index_t"],
        "sw12": _np.concatenate([a["L1_ffn_sw1"], a["L1_ffn_sw2"]]).T.reshape(2, 128, 256),
        "sw3": a["L1_ffn_sw3"].T,
        "gw": _np.concatenate([a["L1_ffn_sg_w"], a["L1_ffn_eg_w"]]).T.reshape(2, 128, 9),
        "ew1": experts(a["L1_ffn_ew1"]).reshape(2, 128, 1024), "ew2": experts(a["L1_ffn_ew2"]).reshape(2, 128, 1024),
        "ew3": experts(a["L1_ffn_ew3"]),
        "eb": _np.concatenate([a["L1_ffn_eb1"], a["L1_ffn_eb2"], a["L1_ffn_eb3"]], axis=1),
    }
    arrays = {k: _np.ascontiguousarray(v) for k, v in arrays.items()}
    nc = _bacc.Bacc("TRN2", target_bir_lowering=False, num_devices=1)
    I = {k: nc.dram_tensor("in_" + k, v.shape, _mybir.dt.from_np(v.dtype), kind="ExternalInput").ap()
         for k, v in arrays.items()}
    out = nc.dram_tensor("out_x", (16, 128, 256), _mybir.dt.float32, kind="ExternalOutput").ap()
    decoder_kernel(nc, I, out)
    r = _run(nc, [{"in_" + k: v for k, v in arrays.items()}], core_ids=[0])
    return r.results[0]["out_x"].reshape(2, 1024, 256)
```

```python
from contextlib import ExitStack

import numpy as np
import concourse.bass as bass
from concourse import mybir

ALU = mybir.AluOpType
ACT = mybir.ActivationFunctionType
AX_X = mybir.AxisListType.X
F32 = mybir.dt.float32
F32R = mybir.dt.float32r
BF16 = mybir.dt.bfloat16
I32 = mybir.dt.int32
U32 = mybir.dt.uint32

P = 128
B = 2
S = 1024
D = 256
SK = 154
SKP = 160
TOK = B * S
TILES = TOK // P
TPB = S // P
HEADS = 16
DH = D // HEADS
SLOTS = B * HEADS
CH = 512
CHUNKS = TOK // CH
HARM = 32
HID = 1024
EPS = 1e-5
NMOE = 512
MT = NMOE // P
XT = TILES + MT
NEXP = 8
EH = 128
SCAN = 64
PROD = 6 * DH
MASKROW = PROD
MAXROW = PROD + 1
KROWS = PROD + 3
ONES = float(np.uint32(0x3F803F80).view(np.float32))
VW = 32
RSQRT_MAGIC = float(0x5F3759DF)
ROUND = 12582912.0
TWO_PI = 2.0 * np.pi
C1 = 6.28125
C2 = float((np.float32(TWO_PI - C1).view(np.uint32) & np.uint32(0xFFFFF000)).view(np.float32))
C3 = float(np.float32(TWO_PI - C1 - C2))
PI_IN = 3.1415925

M_X0Q, M_X0K, M_X0V, M_X0O, M_LK, M_LV, M_LQ, M_LKP, M_LQP, M_LO, M_X1Q, M_X1K, M_X1V, M_X1O = range(14)
V_LBK, V_LBV, V_LBQ, V_LBKP, V_LBQP, V_PS, V_LG, V_LB, V_X1BQ, V_X1BK = range(10)
R_LBO, R_X1BV, R_X1BO, R_W3S, R_SB3, R_SB12, NROWS = range(7)


USED = []


def clear_used(nc):
    nc.clear_and_free_semaphores(USED)
    USED.clear()
    nc.all_engine_barrier()


def makers(nc, st, stage):
    def semaphore(name):
        USED.append(nc.alloc_semaphore(f"{stage}_{name}"))
        return USED[-1]
    return (semaphore,
            lambda name, shape, dt: st.enter_context(nc.sbuf_tensor(f"{stage}_{name}", shape, dt)),
            lambda name, shape, dt: st.enter_context(nc.psum_tensor(f"{stage}_{name}", shape, dt)))


def linker(eng, sem):
    count = [0]

    def link(ins):
        count[0] += 1
        ins.then_inc(sem, 1)
        eng.wait_ge(sem, count[0])
    return link


def stage_setup(nc, I, G):
    with ExitStack() as st:
        sem, sb, psum = makers(nc, st, "setup")
        zeroed = sem("zeroed")
        G.basis_in, G.holo_in, G.rest_in = sem("basis_in"), sem("holo_in"), sem("rest_in")
        G.x_in = [sem(f"x_in{c}") for c in range(CHUNKS)]
        block = st.enter_context(nc.Block())

        @block.sync
        def _(sp):
            sp.dma_start(G.basis[:], I["basis"].rearrange("k p h -> p k h")).then_inc(G.basis_in, 16)
            for dst, src in ((G.holo[0:96, 0, 0, :], I["phase_qkv"]), (G.holo[0:HARM, 0, 1, :], I["phase_o"]),
                             (G.holo[0:96, 1, 0, :], I["amp_qkv"]), (G.holo[0:HARM, 1, 1, :], I["amp_o"])):
                sp.dma_start(dst, src).then_inc(G.holo_in, 16)
            for c in range(CHUNKS):
                sp.dma_start(G.xT[:, :, c * CH:(c + 1) * CH],
                             I["x_fm"][:, :, c * CH:(c + 1) * CH].rearrange("k p t -> p k t")).then_inc(G.x_in[c], 16)
            for dst, src in (
                (G.X[:, 0:TILES, :], I["x_tm"].rearrange("t p d -> p t d")),
                (G.ctxT[:, :, 0:B * SK], I["ctx_fm"].rearrange("k p t -> p k t")),
                (G.wmat[:], I["wmat"]), (G.fvec[:], I["fvec"]), (G.ffn_s[:], I["ffn_s"]),
                (G.evec[:], I["evec"]), (G.grow[:], I["grow"].rearrange("(o r) -> o r", o=1).broadcast_to([P, 17])),
                (G.rvec[:], I["rvec"].rearrange("(o r) d -> o r d", o=1).broadcast_to([P, NROWS, D])),
            ):
                sp.dma_start(dst, src).then_inc(G.rest_in, 16)

        @block.gpsimd
        def _(pool):
            pool.memset(G.ident[:], 0.0).then_inc(zeroed, 1)
            pool.wait_ge(zeroed, 1)
            pool.affine_select(out=G.ident[:], in_=G.ident[:], compare_op=ALU.not_equal, fill=1.0, base=0,
                               pattern=[[-1, P]], channel_multiplier=1).then_inc(zeroed, 1)
            pool.memset(G.halfpi[:], float(np.pi / 2)).then_inc(zeroed, 1)
            pool.memset(G.ctxT[:, :, B * SK:B * SK + SKP - SK], 0.0).then_inc(zeroed, 1)
            pool.wait_ge(zeroed, 4)


NB = 4


class Job:

    def __init__(self, products, cols, scale, bias, stores):
        self.products, self.cols, self.scale, self.bias, self.stores = products, cols, scale, bias, stores


def split_products(pe, jobs, ps, made, read, first=0, last=None):
    for j, job in list(enumerate(jobs))[first:last]:
        if j >= NB:
            pe.wait_ge(read, 3 * (j - NB + 1))
        for n, (lhsT, rhs) in enumerate(job.products):
            mm = pe.matmul(ps[:, j % NB, 0:job.cols], lhsT, rhs, start=(n == 0), stop=(n == len(job.products) - 1))
        mm.then_inc(made, 1)


def split_read(act, jobs, ps, full, parts, made, read, split, stored, first=0, last=None):
    for j, job in list(enumerate(jobs))[first:last]:
        act.wait_ge(made, j + 1)
        if j >= NB:
            act.wait_ge(split, j - NB + 1)
            act.wait_ge(stored[j % NB], 16 * len(job.stores) * (j // NB))
        c = job.cols
        for out in (full[:, j % NB, 0:c], parts[:, j % NB, 0, 0:c]):
            act.activation(out, ps[:, j % NB, 0:c], ACT.Identity, bias=job.bias if job.bias is not None else 0.0,
                           scale=job.scale).then_inc(read, 1)
        act.wait_ge(read, 3 * j + 2)
        act.sem_inc(read, 1)


def split_rest(dve, jobs, full, parts, read, rest, split):
    for j, job in enumerate(jobs):
        c = job.cols
        f, p1, p2, p3 = full[:, j % NB, 0:c], *(parts[:, j % NB, n, 0:c] for n in range(3))
        dve.wait_ge(read, 3 * j + 3)
        dve.tensor_tensor(f, f, p1, ALU.subtract).then_inc(rest, 1)
        dve.wait_ge(rest, 2 * j + 1)
        dve.tensor_copy(p2, f).then_inc(rest, 1)
        dve.wait_ge(rest, 2 * j + 2)
        dve.tensor_tensor(p3, f, p2, ALU.subtract).then_inc(split, 1)


def split_store(sp, jobs, parts, split, stored):
    for j, job in enumerate(jobs):
        sp.wait_ge(split, j + 1)
        for a, b, dst in job.stores:
            sp.dma_start(dst, parts[:, j % NB, :, a:b]).then_inc(stored[j % NB], 16)
    for r in range(NB):
        sp.wait_ge(stored[r], 16 * sum(len(j.stores) for j in jobs[r::NB]))


def parts_view(dram, b, blk, a, n):
    return dram[:, b, blk * P:(blk + 1) * P, a:a + n].rearrange("t p c -> p t c")


def stage_project_self(nc, G):
    with ExitStack() as st:
        sem, sb, psum = makers(nc, st, "ps")
        resT = sb("resT", [96, TOK], F32)
        full = sb("split_full", [P, NB, CH], F32)
        parts = sb("split_parts", [P, NB, 3, CH], BF16)
        tmp = sb("cos_tmp", [96, 2, D], F32)
        ps = psum("ps_split", [P, NB, CH], F32)
        ps_res = psum("ps_res", [P, 2, CH], F32)
        ps_v = psum("ps_v", [P, 2, CH], F32)
        res_made, res_read, w_made, w_step, cos_done = sem("res_made"), sem("res_read"), sem("w_made"), sem("w_step"), sem("cos")
        made, read, rest, split = sem("made"), sem("read"), sem("rest"), sem("split")
        stored = [sem(f"stored{r}") for r in range(NB)]
        v_made, v_read = sem("v_made"), sem("v_read")
        jobs = []
        for c in range(CHUNKS):
            for which, dram, scale in ((0, G.q_dram, DH ** -0.5), (1, G.k_dram, 1.0)):
                for blk in range(2):
                    r = slice(HARM * which, HARM * which + HARM)
                    jobs.append(Job([(G.holo[r, 0, 0, blk * P:(blk + 1) * P], resT[r, c * CH:(c + 1) * CH])], CH, scale,
                                    None, [(0, CH, parts_view(dram, c // 2, blk, (c % 2) * CH, CH))]))
        block = st.enter_context(nc.Block())

        @block.tensor
        def _(pe):
            def resonances(c):
                pe.wait_ge(G.x_in[c], 16)
                if c >= 2:
                    pe.wait_ge(res_read, c - 1)
                for k in range(2):
                    mm = pe.matmul(ps_res[0:96, c % 2, :], G.basis[:, k, 0:96], G.xT[:, k, c * CH:(c + 1) * CH],
                                   start=(k == 0), stop=(k == 1))
                mm.then_inc(res_made, 1)

            pe.wait_ge(G.basis_in, 16)
            resonances(0)
            resonances(1)
            pe.wait_ge(w_made, 1)
            for c in range(CHUNKS):
                pe.wait_ge(res_read, c + 1)
                split_products(pe, jobs, ps, made, read, 4 * c, 4 * c + 4)
                if c + 2 < CHUNKS:
                    resonances(c + 2)
            for t in range(TILES):
                if t >= 2:
                    pe.wait_ge(v_read, t - 1)
                pe.matmul(ps_v[:, t % 2, 0:D], resT[64:96, t * P:(t + 1) * P], G.holo[64:96, 0, 0, :],
                          start=True, stop=True).then_inc(v_made, 1)

        @block.vector
        def _(dve):
            link = linker(dve, w_step)
            dve.wait_ge(G.holo_in, 64)
            for rows, o in ((96, 0), (HARM, 1)):
                ph, k = G.holo[0:rows, 0, o, :], tmp[0:rows, o, :]
                link(dve.tensor_scalar(k, ph, 1.0 / TWO_PI, 0.25, ALU.mult, ALU.add))
                link(dve.tensor_scalar(k, k, ROUND, None, ALU.add))
                link(dve.tensor_scalar(k, k, -ROUND, None, ALU.add))
                for cst in (C1, C2, C3):
                    link(dve.scalar_tensor_tensor(ph, k, -cst, ph, ALU.mult, ALU.add))
                link(dve.tensor_scalar(ph, ph, float(np.pi / 2), PI_IN, ALU.add, ALU.min))
                link(dve.tensor_scalar(ph, ph, -PI_IN, None, ALU.max))
            dve.wait_ge(cos_done, 2)
            link(dve.tensor_tensor(G.holo[0:HARM, 0, 1, :], G.holo[0:HARM, 0, 1, :], G.holo[0:HARM, 1, 1, :], ALU.mult))
            dve.tensor_tensor(G.holo[0:96, 0, 0, :], G.holo[0:96, 0, 0, :], G.holo[0:96, 1, 0, :],
                              ALU.mult).then_inc(w_made, 1)
            split_rest(dve, jobs, full, parts, read, rest, split)

        @block.scalar
        def _(act):
            def resonances(c):
                act.wait_ge(res_made, c + 1)
                act.activation(resT[:, c * CH:(c + 1) * CH], ps_res[0:96, c % 2, :], ACT.Copy).then_inc(res_read, 1)

            act.wait_ge(w_step, 16)
            act.activation(G.holo[0:96, 0, 0, :], G.holo[0:96, 0, 0, :], ACT.Sin).then_inc(cos_done, 1)
            act.activation(G.holo[0:HARM, 0, 1, :], G.holo[0:HARM, 0, 1, :], ACT.Sin).then_inc(cos_done, 1)
            resonances(0)
            resonances(1)
            for c in range(CHUNKS):
                split_read(act, jobs, ps, full, parts, made, read, split, stored, 4 * c, 4 * c + 4)
                if c + 2 < CHUNKS:
                    resonances(c + 2)
            for t in range(TILES):
                act.wait_ge(v_made, t + 1)
                b, tau = t // TPB, t % TPB
                act.activation(G.V[:, b * HEADS:(b + 1) * HEADS, tau, :],
                               ps_v[:, t % 2, 0:D].rearrange("p (h d) -> p h d", d=DH), ACT.Copy).then_inc(v_read, 1)

        @block.sync
        def _(sp):
            split_store(sp, jobs, parts, split, stored)
            sp.wait_ge(G.rest_in, 16 * 8)


def stage_project_cross(nc, G, tag, mq, mk, mv, scale, bq, bk, bv_row, spread=False):
    with ExitStack() as st:
        sem, sb, psum = makers(nc, st, tag)
        full = sb("split_full", [P, NB, CH], F32)
        parts = sb("split_parts", [P, NB, 3, CH], BF16)
        qb = sb("q_bias", [P, 2], F32)
        ps = psum("ps_split", [P, NB, CH], F32)
        ps_v = psum("ps_v", [P, 2, CH], F32)
        made, read, rest, split = sem("made"), sem("read"), sem("rest"), sem("split")
        stored = [sem(f"stored{r}") for r in range(NB)]
        v_made, v_read, qb_made, ones = sem("v_made"), sem("v_read"), sem("qb_made"), sem("ones")
        jobs = []
        for blk in range(2):
            cols = slice(blk * P, (blk + 1) * P)
            jobs.append(Job([(G.wmat[:, mk, k, cols], G.ctxT[:, k, 0:B * SK]) for k in range(2)], B * SK, 1.0,
                            None if bk is None else G.fvec[:, bk, blk:blk + 1],
                            [(b * SK, (b + 1) * SK, parts_view(G.kx_dram, b, blk, 0, SK)) for b in range(B)]))
        for c in range(CHUNKS):
            for blk in range(2):
                cols = slice(blk * P, (blk + 1) * P)
                half = [(h * CH // 2, (h + 1) * CH // 2) for h in range(2)]
                jobs.append(Job([(G.wmat[:, mq, k, cols], G.xT[:, k, c * CH:(c + 1) * CH]) for k in range(2)], CH, scale,
                                None if bq is None else qb[:, blk:blk + 1],
                                [(a, z, parts_view(G.qx_dram, c // 2, blk, (c % 2) * CH + a, z - a)) for a, z in half]))
        block = st.enter_context(nc.Block())
        vt = [(b, kt, a, n) for b in range(B) for kt, (a, n) in enumerate(((0, P), (P, SK - P)))]

        @block.tensor
        def _(pe):
            split_products(pe, jobs, ps, made, read)
            for j, (b, kt, a, n) in enumerate(vt):
                if j >= 2:
                    pe.wait_ge(v_read, j - 1)
                outs = [(c * 32, 32) for c in range(4)] if spread and kt == 1 else [(0, n)]
                for p, w in outs:
                    for k in range(2):
                        mm = pe.matmul(ps_v[p:p + w, j % 2, 0:D], G.ctxT[:, k, b * SK + a:b * SK + a + w],
                                       G.wmat[:, mv, k, :], start=(k == 0), stop=(k == 1))
                mm.then_inc(v_made, 1)

        @block.vector
        def _(dve):
            if bq is not None:
                dve.tensor_scalar(qb[:], G.fvec[:, bq, :], scale, None, ALU.mult).then_inc(qb_made, 1)
            if spread:
                dve.memset(G.Vx[:, :, :, DH:DH + 1], 1.0).then_inc(ones, 1)
                dve.memset(G.Vx_rest[:, :, DH:DH + 1], 1.0).then_inc(ones, 1)
            split_rest(dve, jobs, full, parts, read, rest, split)
            for j, (b, kt, a, n) in enumerate(vt):
                dve.wait_ge(v_made, j + 1)
                if spread and kt == 1:
                    n, out = P, G.Vx_rest[:, b * HEADS:(b + 1) * HEADS, 0:DH]
                else:
                    out = G.Vx[0:n, b * HEADS:(b + 1) * HEADS, kt, 0:DH]
                src = ps_v[0:n, j % 2, 0:D].rearrange("p (h d) -> p h d", d=DH)
                if bv_row is None:
                    dve.tensor_copy(out, src).then_inc(v_read, 1)
                else:
                    dve.tensor_tensor(out, src, G.rvec[0:n, bv_row, :].rearrange("p (h d) -> p h d", d=DH),
                                      ALU.add).then_inc(v_read, 1)

        @block.scalar
        def _(act):
            if bq is not None:
                act.wait_ge(qb_made, 1)
            split_read(act, jobs, ps, full, parts, made, read, split, stored)

        @block.sync
        def _(sp):
            split_store(sp, jobs, parts, split, stored)


class Slot:

    def __init__(self, i, c, u=4):
        self.i, self.c, self.u = i, c, u

    def __add__(self, k):
        return Slot(self.i, self.c + k, self.u)

    def known(self):
        return isinstance(self.i, int)

    def ring(self, n=4):
        return self.c % n

    def times(self, m, more=0):
        return self.i * (self.u * m) + (self.c * m + more)

    def turn(self, m, more=0, ring=4):
        return self.i * (self.u // ring * m) + (self.c // ring * m + more)


def head_cols(s):
    return bass.ds(s.times(DH), DH) if not s.known() else slice(s.times(DH), s.times(DH) + DH)


def run_slots(eng, first, last, loop_from, loop_last, emit, u=4):
    for s in range(first, loop_from):
        emit(Slot(0, s, u))
    turns = (loop_last - loop_from + 1) // u
    with eng.Fori(0, turns) as i:
        for n in range(u):
            emit(Slot(i, loop_from + n, u))
    for s in range(loop_from + u * turns, last + 1):
        emit(Slot(0, s, u))


RUNS = [(0, 3 * DH, slice(0, 3), 0), (3 * DH, 2 * DH, slice(0, 2), 1), (5 * DH, DH, slice(0, 1), 2)]
LOADS = len(RUNS)


def load_queries(sp, n, stack, dram, ready):
    src = dram.rearrange("t b (h d) c -> t (b h) d c", d=DH)
    for row, rows, qp, kp in RUNS:
        sp.dma_start(stack[row:row + rows], src[qp, n.times(1)]).then_inc(ready, 16)


def load_keys(sp, n, stack, dram, ready):
    src = dram.rearrange("t b (h d) c -> t (b h) d c", d=DH)
    for row, rows, qp, kp in RUNS:
        one = src[kp:kp + 1, n.times(1)]
        sp.dma_start(stack[row:row + rows], one.broadcast_to([rows // DH, DH, one.shape[-1]])).then_inc(ready, 16)


def load_batch_keys(sp, b, stack, dram, ready):
    src = dram.rearrange("t b (h d) c -> t b d h c", d=DH)
    for row, rows, qp, kp in RUNS:
        for r in range(row, row + rows, DH):
            sp.dma_start(stack[r:r + DH, b * HEADS:(b + 1) * HEADS, 0:SK], src[kp, b]).then_inc(ready, 16)


def stage_attention(nc, G, tag):
    NKT = S // P
    EB = 4
    ROWS = PROD + 2
    HALF = NKT // 2
    STEP_O, STEP_M = 2, 4
    with ExitStack() as st:
        sem, sb, psum = makers(nc, st, tag)
        q_stack = sb("q_stack", [P, 4, S], BF16)
        k_stack = sb("k_stack", [P, 4, S], BF16)
        values = sb("values", [P, 4, NKT, VW], F32)
        probs = sb("probs", [P, EB, S], F32)
        neg_max = sb("neg_max", [P, 4, TPB], F32)
        max_rows = sb("max_rows", [TPB, 4, 2, P], BF16)
        out_raw = sb("out_raw", [P, 2, 2 * P], F32)
        inv_sum = sb("inv_sum", [P, 2, 2, 4], F32)
        pm = psum("ps_max", [P, 2, 2 * CH], F32)
        pscore = psum("ps_score", [P, 2, CH], F32)
        po = psum("ps_out", [P, CH], F32)
        pmisc = psum("ps_misc", [P, CH], F32)
        ready = [sem(f"stack{r}") for r in range(4)]
        rows_in = [sem(f"rows{r}") for r in range(4)]
        const, rows_set = sem("const"), sem("rows_set")
        max_made, max_done = sem("max_made"), sem("max_done")
        misc_made, misc_done = sem("misc_made"), sem("misc_done")
        row_hi, row_done = sem("row_hi"), sem("row_done")
        score_made, exp_done, pv_done = sem("score"), sem("exp"), sem("pv")
        out_read, recip, values_in = sem("out_read"), sem("recip"), sem("values_in")
        block = st.enter_context(nc.Block())

        def pos(x, n):
            return x.times(*n) if not x.known() or x.times(*n) > 0 else None

        def ahead_of(s, t):
            n, m = (s + 1, t + HALF) if t < HALF else (s + 2, t - HALF)
            return (n, m) if not s.known() or n.c < SLOTS else None

        def wait(eng, s, v):
            if v is not None:
                eng.wait_ge(s, v)

        @block.sync
        def _(sp):

            def rows(n):
                r = n.ring()
                sp.wait_ge(row_done, n.times(1, 1))
                for part in range(2):
                    sp.dma_start(q_stack[PROD + part:PROD + part + 1, r, :],
                                 max_rows[:, r, part, :]).then_inc(rows_in[r], 16)

            def slot(s):
                if s.c + 1 < SLOTS or not s.known():
                    rows(s + 1)
                if s.c + 4 < SLOTS or not s.known():
                    sp.wait_ge(pv_done, s.times(NKT, NKT))
                    load(s + 4)

            def load(n):
                r = n.ring()
                load_queries(sp, n, q_stack[:, r, :], G.q_dram, ready[r])
                load_keys(sp, n, k_stack[:, r, :], G.k_dram, ready[r])

            for n in range(4):
                load(Slot(0, n))
            sp.wait_ge(rows_set, 1)
            rows(Slot(0, 0))
            run_slots(sp, 0, SLOTS - 1, 0, SLOTS - 5, slot)

        @block.gpsimd
        def _(pool):
            link = linker(pool, const)
            link(pool.memset(values[:], 0.0))
            link(pool.memset(values[:, :, :, DH:DH + 1], 1.0))

            def copy_values(n):
                if not n.known() or n.c >= 4:
                    pool.wait_ge(pv_done, n.times(NKT, -3 * NKT))
                pool.tensor_copy(values[:, n.ring(), :, 0:DH], G.V[:, n.times(1), :, :]).then_inc(values_in, 1)
            run_slots(pool, 0, SLOTS - 1, 4, SLOTS - 1, copy_values)

        @block.tensor
        def _(pe):
            def max_unit(n, m):
                r = n.ring()
                if m == 0:
                    pe.wait_ge(ready[r], n.turn(32 * LOADS, 32 * LOADS))
                wait(pe, max_done, pos(n, (NKT, m - 1)))
                for h in range(2):
                    mm = pe.matmul(pm[:, m % 2, h * CH:(h + 1) * CH], q_stack[0:PROD, r, m * P:(m + 1) * P],
                                   k_stack[0:PROD, r, h * CH:(h + 1) * CH], start=True, stop=True)
                mm.then_inc(max_made, 1)

            def max_turn(n, index):
                pe.wait_ge(max_done, n.times(NKT, NKT))
                if index is not None:
                    pe.wait_ge(misc_done, index)
                pe.transpose(pmisc[0:TPB, 0:P], neg_max[:, n.ring(), :], G.ident[:]).then_inc(misc_made, 1)

            def score(s, t, h):
                r = s.ring()
                g = 2 * t + h
                if g == 0:
                    pe.wait_ge(rows_in[r], s.turn(32, 32))
                wait(pe, exp_done, pos(s, (2 * NKT, g - 1)))
                pe.matmul(pscore[:, h, :], k_stack[0:ROWS, r, t * P:(t + 1) * P], q_stack[0:ROWS, r, h * CH:(h + 1) * CH],
                          start=True, stop=True).then_inc(score_made, 1)

            def pv(s, t):
                if t == 0:
                    pe.wait_ge(values_in, s.times(1, 1))
                    wait(pe, out_read, pos(s, (1, 0)))
                pe.wait_ge(exp_done, s.times(2 * NKT, 2 * t + 2))
                e = (s.c * NKT + t) % EB
                for j in range(4):
                    mm = pe.matmul(po[j * VW:(j + 1) * VW, 0:2 * P], values[:, s.ring(), t, :],
                                   probs[:, e, j * 2 * P:(j + 1) * 2 * P], start=(t == 0), stop=(t == NKT - 1))
                mm.then_inc(pv_done, 1)

            def out_turn(s, index):
                pe.wait_ge(out_read, s.times(1, 1))
                pe.wait_ge(misc_done, index)
                for h in range(2):
                    mm = pe.transpose(pmisc[:, h * P:(h + 1) * P], out_raw[:, s.ring(2), h * P:(h + 1) * P], G.ident[:])
                mm.then_inc(misc_made, 1)

            def ahead(s, t):
                if ahead_of(s, t):
                    max_unit(*ahead_of(s, t))

            def slot(s):
                known = s.known()
                first = known and s.c == 0
                for t in range(NKT):
                    score(s, t, 0)
                    score(s, t, 1)
                    if t == 0 and not first:
                        pv(s + -1, NKT - 1)
                    ahead(s, t)
                    if t >= 1:
                        pv(s, t - 1)
                    if t == STEP_O and not first:
                        out_turn(s + -1, s.times(2, 0))
                    if t == STEP_M and (not known or s.c + 1 < SLOTS):
                        max_turn(s + 1, s.times(2, 1))

            pe.wait_ge(const, 2)
            pe.wait_ge(rows_set, 1)
            for u in range(NKT + HALF):
                max_unit(Slot(0, u // NKT), u % NKT)
            max_turn(Slot(0, 0), None)
            run_slots(pe, 0, SLOTS - 1, 1, SLOTS - 4, slot)
            pv(Slot(0, SLOTS - 1), NKT - 1)
            out_turn(Slot(0, SLOTS - 1), 2 * SLOTS - 1)

        @block.scalar
        def _(act):
            def slot(s):
                for t in range(NKT):
                    e = (s.c * NKT + t) % EB
                    for h in range(2):
                        act.wait_ge(score_made, s.times(2 * NKT, 2 * t + h + 1))
                        if h == 0:
                            wait(act, pv_done, pos(s, (NKT, t + 1 - EB)))
                        act.activation(probs[:, e, h * CH:(h + 1) * CH], pscore[:, h, :],
                                       ACT.Exp).then_inc(exp_done, 1)
                    if t == 0 and not (s.known() and s.c == 0):
                        read_out(s + -1)

            def read_out(s):
                act.wait_ge(pv_done, s.times(NKT, NKT))
                act.activation(out_raw[:, s.ring(2), :], po[:, 0:2 * P], ACT.Copy).then_inc(out_read, 1)

            run_slots(act, 0, SLOTS - 1, 1, SLOTS - 4, slot)
            read_out(Slot(0, SLOTS - 1))

        @block.vector
        def _(dve):
            dve.memset(k_stack[PROD:ROWS, :, :].bitcast(F32), ONES).then_inc(rows_set, 1)

            def max_unit(n, m):
                dve.wait_ge(max_made, n.times(NKT, m + 1))
                dve.tensor_reduce(neg_max[:, n.ring(), m:m + 1], pm[:, m % 2, :], AX_X, ALU.max,
                                  negate=True).then_inc(max_done, 1)

            def max_row(n, index):
                r = n.ring()
                dve.wait_ge(misc_made, index)
                dve.tensor_copy(max_rows[:, r, 0, :], pmisc[0:TPB, 0:P]).then_inc(row_hi, 1)
                dve.wait_ge(row_hi, n.times(1, 1))
                dve.tensor_tensor(max_rows[:, r, 1, :], pmisc[0:TPB, 0:P], max_rows[:, r, 0, :],
                                  ALU.subtract).then_inc(row_done, 1)
                dve.wait_ge(row_done, n.times(1, 1))
                dve.sem_inc(misc_done, 1)

            def normalise(s, index):
                par = s.ring(2)
                dve.wait_ge(misc_made, index)
                sums = pmisc[:, 0:2 * P].rearrange("p (h j c) -> p h j c", h=2, j=4)
                dve.reciprocal(inv_sum[:, par], sums[:, :, :, DH:DH + 1]).then_inc(recip, 1)
                dve.wait_ge(recip, s.times(1, 1))
                dst = G.A[:, :, head_cols(s)].rearrange("p (j h) d -> p h j d", h=2)
                dve.tensor_tensor(dst, sums[:, :, :, 0:DH],
                                  inv_sum[:, par].rearrange("p h (j o) -> p h j o", o=1).broadcast_to([P, 2, 4, DH]),
                                  ALU.mult).then_inc(misc_done, 1)

            def ahead(s, t):
                if ahead_of(s, t):
                    max_unit(*ahead_of(s, t))

            def slot(s):
                known = s.known()
                for t in range(NKT):
                    ahead(s, t)
                    if t == STEP_O and not (known and s.c == 0):
                        normalise(s + -1, s.times(2, 1))
                    if t == STEP_M and (not known or s.c + 1 < SLOTS):
                        max_row(s + 1, s.times(2, 2))

            for u in range(NKT + HALF):
                max_unit(Slot(0, u // NKT), u % NKT)
            max_row(Slot(0, 0), 1)
            run_slots(dve, 0, SLOTS - 1, 1, SLOTS - 4, slot)
            normalise(Slot(0, SLOTS - 1), 2 * SLOTS)


def stage_attention_cross(nc, G, tag):
    ktiles = [(0, P), (P, SK - P)]
    NKT = len(ktiles)
    RING = 8
    UNITS = 4
    QPU = TPB // UNITS
    with ExitStack() as st:
        sem, sb, psum = makers(nc, st, tag)
        q_stack = sb("q_stack", [P, RING, S], BF16)
        k_stack = sb("k_stack", [P, SLOTS, SK], BF16)
        values = sb("values", [P, 4, NKT, VW], F32)
        probs = sb("probs", [P, 4, S], F32)
        neg_max = sb("neg_max", [P, RING, TPB], F32)
        max_rows = sb("max_rows", [TPB, RING, 2, P], BF16)
        out_raw = sb("out_raw", [P, 2, 2 * P], F32)
        inv_sum = sb("inv_sum", [P, 2, 2, 4], F32)
        mask_f, mask_i, mask_b = sb("mask_f", [1, B, SK], F32), sb("mask_i", [1, B, SK], I32), sb("mask_b", [1, B, SK], BF16)
        pm = psum("ps_max", [P, 2, CH], F32)
        pscore = psum("ps_score", [P, NKT, 2 * CH], F32)
        po = psum("ps_out", [P, CH], F32)
        pmisc = psum("ps_misc", [P, CH], F32)
        ready = [sem(f"stack{r}") for r in range(RING)]
        rows_in = [sem(f"rows{r}") for r in range(RING)]
        const, rows_one, query_one, mask_in, mask_step = sem("const"), sem("rows_one"), sem("query_one"), sem("mask_in"), sem("mask_step")
        batch_in = [sem(f"keys{b}") for b in range(B)]
        max_made, max_done = sem("max_made"), sem("max_done")
        max_turned, row_hi, row_done, row_free = sem("max_turned"), sem("row_hi"), sem("row_done"), sem("row_free")
        out_turned, recip, filed = sem("out_turned"), sem("recip"), sem("filed")
        score_made, exp_done, pv_done = sem("score"), sem("exp"), sem("pv")
        out_read, values_in = sem("out_read"), sem("values_in")
        block = st.enter_context(nc.Block())

        def run(eng, first, last, loop_from, loop_last, emit):
            run_slots(eng, first, last, loop_from, loop_last, emit, RING)

        def slot0(c):
            return Slot(0, c, RING)

        @block.sync
        def _(sp):
            def load(n):
                load_queries(sp, n, q_stack[:, n.ring(RING), :], G.qx_dram, ready[n.ring(RING)])

            def rows(n):
                r = n.ring(RING)
                sp.wait_ge(row_done, n.times(1, 1))
                for part in range(2):
                    sp.dma_start(q_stack[MAXROW + part:MAXROW + part + 1, r, :],
                                 max_rows[:, r, part, :]).then_inc(rows_in[r], 16)

            def slot(s):
                if not s.known() or s.c + RING < SLOTS:
                    sp.wait_ge(score_made, s.times(NKT, NKT))
                    load(s + RING)
                if not s.known() or s.c + 3 < SLOTS:
                    rows(s + 3)

            sp.dma_start(mask_i[:], G.mask.rearrange("(o b) s -> o b s", o=1)).then_inc(mask_in, 16)
            load(slot0(0))
            for b in range(B):
                load_batch_keys(sp, b, k_stack, G.kx_dram, batch_in[b])
            sp.wait_ge(rows_one, 1)
            sp.wait_ge(mask_step, 2)
            for b in range(B):
                sp.dma_start(k_stack[MASKROW:MASKROW + 1, b * HEADS:(b + 1) * HEADS, :],
                             mask_b[:, b:b + 1, :].broadcast_to([1, HEADS, SK])).then_inc(batch_in[b], 16)
            for n in range(1, 4):
                load(slot0(n))
            sp.wait_ge(query_one, 2)
            for n in range(4, RING):
                if n < 7:
                    rows(slot0(n - 4))
                load(slot0(n))
            run(sp, 0, SLOTS - 1, 0, SLOTS - RING - 1, slot)

        @block.gpsimd
        def _(pool):
            link = linker(pool, const)
            for h in range(2):
                pool.memset(q_stack[PROD:KROWS, h * 4:(h + 1) * 4, :].bitcast(F32), ONES).then_inc(query_one, 1)
                pool.wait_ge(query_one, h + 1)
            link(pool.memset(values[:], 0.0))
            link(pool.memset(probs[:, 1:4:2, :], 0.0))
            for kt, (a, m) in enumerate(ktiles):
                link(pool.memset(values[0:m, :, kt, DH:DH + 1], 1.0))

            def copy_values(n):
                if not n.known() or n.c >= 4:
                    pool.wait_ge(pv_done, n.times(1, -3))
                for kt, (a, m) in enumerate(ktiles):
                    pool.tensor_copy(values[0:m, n.ring(), kt:kt + 1, 0:DH],
                                     G.Vx[0:m, n.times(1), kt:kt + 1, :]).then_inc(values_in, 1)
            run(pool, 0, SLOTS - 1, RING, SLOTS - 1, copy_values)

        @block.tensor
        def _(pe):
            def max_unit(n, m):
                r = n.ring(RING)
                if m == 0:
                    pe.wait_ge(ready[r], n.turn(16 * LOADS, 16 * LOADS, RING))
                if not n.known() or n.c > 0 or m >= 2:
                    pe.wait_ge(max_done, n.times(UNITS, m - 1))
                for q in range(QPU):
                    t = m * QPU + q
                    mm = pe.matmul(pm[:, m % 2, q * SK:(q + 1) * SK], q_stack[0:PROD + 1, r, t * P:(t + 1) * P],
                                   k_stack[0:PROD + 1, n.times(1), :], start=True, stop=True)
                mm.then_inc(max_made, 1)

            def max_turn(n, filed_before):
                pe.wait_ge(max_done, n.times(UNITS, UNITS))
                if not n.known() or n.c > 0:
                    pe.wait_ge(row_free, n.times(1))
                if filed_before is not None:
                    pe.wait_ge(filed, filed_before)
                pe.transpose(pmisc[0:TPB, 0:P], neg_max[:, n.ring(RING), :], G.ident[:]).then_inc(max_turned, 1)

            def scores(s, t):
                r, (a, m) = s.ring(RING), ktiles[t]
                if t == 0:
                    pe.wait_ge(rows_in[r], s.turn(32, 32, RING))
                if not s.known() or s.c > 0:
                    pe.wait_ge(exp_done, s.times(NKT, t - 1))
                for h in range(2):
                    mm = pe.matmul(pscore[0:m, t, h * CH:(h + 1) * CH], k_stack[0:KROWS, s.times(1), a:a + m],
                                   q_stack[0:KROWS, r, h * CH:(h + 1) * CH], start=True, stop=True)
                mm.then_inc(score_made, 1)

            def products(s):
                pe.wait_ge(values_in, s.times(NKT, NKT))
                if not s.known() or s.c > 0:
                    pe.wait_ge(out_read, s.times(1))
                for t, (a, m) in enumerate(ktiles):
                    pe.wait_ge(exp_done, s.times(NKT, t + 1))
                    e = (s.c * NKT + t) % 4
                    for j in range(4):
                        mm = pe.matmul(po[j * VW:(j + 1) * VW, 0:2 * P], values[:, s.ring(), t, :],
                                       probs[:, e, j * 2 * P:(j + 1) * 2 * P], start=(t == 0), stop=(t == NKT - 1))
                mm.then_inc(pv_done, 1)

            def out_turn(s):
                pe.wait_ge(out_read, s.times(1, 1))
                rows_before = s + 6 if s.c + 6 <= SLOTS or not s.known() else Slot(0, SLOTS, RING)
                pe.wait_ge(row_free, rows_before.times(1))
                if not s.known() or s.c > 0:
                    pe.wait_ge(filed, s.times(1))
                for h in range(2):
                    mm = pe.transpose(pmisc[:, h * P:(h + 1) * P], out_raw[:, s.ring(2), h * P:(h + 1) * P], G.ident[:])
                mm.then_inc(out_turned, 1)

            def slot(s):
                more = not s.known() or s.c + 4 < SLOTS
                scores(s, 0)
                if more:
                    max_unit(s + 4, 0)
                if not s.known() or s.c + 3 < SLOTS:
                    max_turn(s + 3, (s + -2).times(1) if not s.known() or s.c >= 3 else None)
                if more:
                    max_unit(s + 4, 1)
                if not s.known() or s.c >= 1:
                    products(s + -1)
                if not s.known() or s.c >= 2:
                    out_turn(s + -2)
                scores(s, 1)
                if more:
                    max_unit(s + 4, 2)
                    max_unit(s + 4, 3)

            pe.wait_ge(const, 4)
            pe.wait_ge(rows_one, 1)
            pe.wait_ge(query_one, 1)
            pe.wait_ge(batch_in[0], 16 * 7)
            for n in range(4):
                for m in range(UNITS):
                    max_unit(slot0(n), m)
                if n < 3:
                    max_turn(slot0(n), None)
            pe.wait_ge(query_one, 2)
            pe.wait_ge(batch_in[1], 16 * 7)
            run(pe, 0, SLOTS - 1, 3, SLOTS - 5, slot)
            products(slot0(SLOTS - 1))
            out_turn(slot0(SLOTS - 2))
            out_turn(slot0(SLOTS - 1))

        @block.scalar
        def _(act):
            def slot(s):
                for t, (a, m) in enumerate(ktiles):
                    act.wait_ge(score_made, s.times(NKT, t + 1))
                    if not s.known() or s.c >= 2:
                        act.wait_ge(pv_done, s.times(1, -1))
                    act.activation(probs[0:m, (s.c * NKT + t) % 4, :], pscore[0:m, t, :], ACT.Exp).then_inc(exp_done, 1)
                if not s.known() or s.c >= 1:
                    read_out(s + -1)

            def read_out(s):
                act.wait_ge(pv_done, s.times(1, 1))
                act.activation(out_raw[:, s.ring(2), :], po[:, 0:2 * P], ACT.Copy).then_inc(out_read, 1)
            act.wait_ge(const, 2)
            run(act, 0, SLOTS - 1, 2, SLOTS - 1, slot)
            read_out(slot0(SLOTS - 1))

        @block.vector
        def _(dve):
            dve.memset(k_stack[PROD:KROWS, :, :].bitcast(F32), ONES).then_inc(rows_one, 1)
            dve.wait_ge(mask_in, 16)
            dve.tensor_copy(mask_f[:], mask_i[:]).then_inc(mask_step, 1)
            dve.wait_ge(mask_step, 1)
            dve.tensor_scalar(mask_b[:], mask_f[:], 0.0, -1e30, ALU.is_equal, ALU.mult).then_inc(mask_step, 1)

            def max_unit(n, m):
                dve.wait_ge(max_made, n.times(UNITS, m + 1))
                src = pm[:, m % 2, 0:QPU * SK].rearrange("p (q c) -> p q c", q=QPU)
                dve.tensor_reduce(neg_max[:, n.ring(RING), m * QPU:(m + 1) * QPU], src, AX_X, ALU.max,
                                  negate=True).then_inc(max_done, 1)

            def max_row(n):
                r = n.ring(RING)
                dve.wait_ge(max_turned, n.times(1, 1))
                dve.tensor_copy(max_rows[:, r, 0, :], pmisc[0:TPB, 0:P]).then_inc(row_hi, 1)
                dve.wait_ge(row_hi, n.times(1, 1))
                dve.tensor_tensor(max_rows[:, r, 1, :], pmisc[0:TPB, 0:P], max_rows[:, r, 0, :],
                                  ALU.subtract).then_inc(row_done, 1)
                dve.wait_ge(row_done, n.times(1, 1))
                dve.sem_inc(row_free, 1)

            def normalise(s):
                par = s.ring(2)
                dve.wait_ge(out_turned, s.times(1, 1))
                sums = pmisc[:, 0:2 * P].rearrange("p (h j c) -> p h j c", h=2, j=4)
                dve.reciprocal(inv_sum[:, par], sums[:, :, :, DH:DH + 1]).then_inc(recip, 1)
                dve.wait_ge(recip, s.times(1, 1))
                dst = G.A[:, :, head_cols(s)].rearrange("p (j h) d -> p h j d", h=2)
                dve.tensor_tensor(dst, sums[:, :, :, 0:DH],
                                  inv_sum[:, par].rearrange("p h (j o) -> p h j o", o=1).broadcast_to([P, 2, 4, DH]),
                                  ALU.mult).then_inc(filed, 1)

            def slot(s):
                more = not s.known() or s.c + 4 < SLOTS
                if more:
                    max_unit(s + 4, 0)
                if not s.known() or s.c + 3 < SLOTS:
                    max_row(s + 3)
                if more:
                    max_unit(s + 4, 1)
                if not s.known() or s.c >= 2:
                    normalise(s + -2)
                if more:
                    max_unit(s + 4, 2)
                    max_unit(s + 4, 3)

            for n in range(4):
                for m in range(UNITS):
                    max_unit(slot0(n), m)
                if n < 3:
                    max_row(slot0(n))
            run(dve, 0, SLOTS - 1, 3, SLOTS - 5, slot)
            normalise(slot0(SLOTS - 2))
            normalise(slot0(SLOTS - 1))


def stage_attention_over_queries(nc, G):
    RING, GS = 8, 4
    with ExitStack() as st:
        sem, sb, psum = makers(nc, st, "x0")
        q_stack = sb("q_stack", [P, RING, S], BF16)
        k_stack = sb("k_stack", [P, SLOTS, SKP], BF16)
        rest_keys = sb("rest_keys", [P, 2, GS, SKP - P], BF16)
        values = sb("values", [P, GS, VW], F32)
        rest_values = sb("rest_values", [P, GS, VW], F32)
        probs, rest_probs = sb("probs", [P, GS, S], F32), sb("rest_probs", [P, 2, S], F32)
        neg_max, rest_neg = sb("neg_max", [P, RING], F32), sb("rest_neg_max", [P, 2], F32)
        row_sum, rest_sum = sb("row_sum", [P, RING], F32), sb("rest_row_sum", [P, 2], F32)
        inv_row, rest_inv = sb("inv_row", [P, RING], F32), sb("rest_inv_row", [P, 2], F32)
        out_raw = sb("out_raw", [P, 2, 2 * P], F32)
        inv_sum = sb("inv_sum", [P, 2, 2, 4], F32)
        pscore = psum("ps_score", [P, 2, 2 * CH], F32)
        prest = psum("ps_rest", [P, 2 * CH], F32)
        po = psum("ps_out", [P, CH], F32)
        pt = psum("ps_turn", [P, CH], F32)
        ready = [sem(f"stack{r}") for r in range(RING)]
        const, padded, batch_in = sem("const"), sem("padded"), [sem(f"keys{b}") for b in range(B)]
        keys_copied = sem("keys_copied")
        score_made, max_done, exp_done, inv_done = sem("score"), sem("max"), sem("exp"), sem("inv")
        rest_made, rest_max, rest_exp, rest_inverted = sem("rest_made"), sem("rest_max"), sem("rest_exp"), sem("rest_inv")
        values_in, pv_done, out_read, turned, recip, filed = (sem("values_in"), sem("pv"), sem("out_read"),
                                                              sem("turned"), sem("recip"), sem("filed"))
        block = st.enter_context(nc.Block())

        def slot0(c):
            return Slot(0, c, RING)

        def run(eng, slot):
            run_slots(eng, 0, SLOTS - 1, GS, SLOTS - GS - 1, slot, RING)

        def rest_now(s):
            return s.c % GS == 2 and (not s.known() or s.c + GS < SLOTS)

        @block.sync
        def _(sp):
            def load(n):
                load_queries(sp, n, q_stack[:, n.ring(RING), :], G.qx_dram, ready[n.ring(RING)])

            def slot(s):
                sp.wait_ge(score_made, s.times(1, 1))
                load(s + RING)
            load_batch_keys(sp, 0, k_stack, G.kx_dram, batch_in[0])
            for n in range(GS):
                load(slot0(n))
            load_batch_keys(sp, 1, k_stack, G.kx_dram, batch_in[1])
            for n in range(GS, RING):
                load(slot0(n))
            run_slots(sp, 0, SLOTS - RING - 1, 0, SLOTS - RING - 1, slot, RING)

        @block.gpsimd
        def _(pool):
            link = linker(pool, const)
            link(pool.memset(rest_values[:], 0.0))
            link(pool.memset(values[:], 0.0))

            def copy_rest_keys(first, g):
                pool.tensor_copy(rest_keys[0:PROD, g % 2], k_stack[0:PROD, bass.ds(first, GS), P:SKP]).then_inc(keys_copied, 1)

            pool.wait_ge(padded, 1)
            pool.wait_ge(batch_in[0], 96)
            copy_rest_keys(0, 0)
            copy_rest_keys(GS, 1)
            pool.wait_ge(batch_in[1], 96)

            def scale_values(n):
                j = n.c % GS
                r = slice(32 * j, 32 * j + SK - P)
                inv = inv_row[:, n.ring(RING):n.ring(RING) + 1]
                g = n.c // GS % 2
                rinv = rest_inv[r, g:g + 1]
                pool.wait_ge(inv_done, n.times(1, 1))
                pool.tensor_tensor(values[:, j, 0:DH + 1], G.Vx[:, n.times(1), 0, :], inv.broadcast_to([P, DH + 1]),
                                   ALU.mult).then_inc(values_in, 1)
                pool.wait_ge(values_in, n.times(2, 1))
                pool.wait_ge(rest_inverted, n.turn(1, 1, GS))
                pool.tensor_tensor(rest_values[r, j, 0:DH + 1], G.Vx_rest[r, n.times(1), :],
                                   rinv.broadcast_to([SK - P, DH + 1]), ALU.mult).then_inc(values_in, 1)
                pool.wait_ge(values_in, n.times(2, 2))
                if j == 0 and (not n.known() or n.c + 2 * GS < SLOTS):
                    pool.wait_ge(rest_made, n.turn(1, 1, GS))
                    copy_rest_keys(n.times(1, 2 * GS), n.c // GS)
            run_slots(pool, 0, SLOTS - 1, 0, 2 * RING - 1, scale_values, RING)

        @block.tensor
        def _(pe):
            def scores(s):
                if not s.known() or s.c >= 2:
                    pe.wait_ge(exp_done, s.times(1, -1))
                for h in range(2):
                    mm = pe.matmul(pscore[:, s.ring(2), h * CH:(h + 1) * CH], k_stack[0:PROD, s.times(1), 0:P],
                                   q_stack[0:PROD, s.ring(RING), h * CH:(h + 1) * CH], start=True, stop=True)
                mm.then_inc(score_made, 1)

            def rest_ready(n):
                for j in range(GS):
                    pe.wait_ge(ready[(n + j).ring(RING)], (n + j).turn(16 * LOADS, 16 * LOADS, RING))
                pe.wait_ge(keys_copied, n.turn(1, 1, GS))
                if not n.known() or n.c > 0:
                    pe.wait_ge(rest_exp, n.turn(1, 0, GS))

            def rest_scores(n):
                for j in range(GS):
                    for h in range(2):
                        mm = pe.matmul(prest[32 * j:32 * j + 32, h * CH:(h + 1) * CH],
                                       rest_keys[0:PROD, n.c // GS % 2, j, :],
                                       q_stack[0:PROD, (n + j).ring(RING), h * CH:(h + 1) * CH], start=True, stop=True)
                mm.then_inc(rest_made, 1)

            def products(s):
                if not s.known() or s.c > 0:
                    pe.wait_ge(out_read, s.times(1))
                pe.wait_ge(values_in, s.times(2, 2))
                j = s.c % GS
                pairs = ((values[:, j, :], probs[:, j, :]), (rest_values[:, j, :], rest_probs[:, s.c // GS % 2, :]))
                for n, (v, p) in enumerate(pairs):
                    for q in range(4):
                        mm = pe.matmul(po[q * VW:(q + 1) * VW, 0:2 * P], v, p[:, q * 2 * P:(q + 1) * 2 * P],
                                       start=(n == 0), stop=(n == 1))
                mm.then_inc(pv_done, 1)

            def turn(s):
                pe.wait_ge(out_read, s.times(1, 1))
                if not s.known() or s.c > 0:
                    pe.wait_ge(filed, s.times(1))
                for h in range(2):
                    mm = pe.transpose(pt[:, h * P:(h + 1) * P], out_raw[:, s.ring(2), h * P:(h + 1) * P], G.ident[:])
                mm.then_inc(turned, 1)

            def slot(s):
                if rest_now(s):
                    rest_ready(s + 2)
                if s.known() and s.c == 2:
                    pe.wait_ge(batch_in[1], 96)
                scores(s)
                if rest_now(s):
                    rest_scores(s + 2)
                if not s.known() or s.c >= 2:
                    products(s + -2)
                if not s.known() or s.c >= 3:
                    turn(s + -3)
            pe.wait_ge(const, 2)
            pe.wait_ge(padded, 1)
            pe.wait_ge(batch_in[0], 96)
            rest_ready(slot0(0))
            rest_scores(slot0(0))
            run(pe, slot)
            for n in (2, 1):
                products(slot0(SLOTS - n))
                turn(slot0(SLOTS - n - 1))
            turn(slot0(SLOTS - 1))

        @block.scalar
        def _(act):
            def exponentials(s):
                act.wait_ge(max_done, s.times(1, 1))
                if not s.known() or s.c >= GS:
                    act.wait_ge(pv_done, s.times(1, 1 - GS))
                act.activation(probs[:, s.c % GS, :], pscore[:, s.ring(2), :], ACT.Exp,
                               bias=neg_max[:, s.ring(RING):s.ring(RING) + 1],
                               accum_out=row_sum[:, s.ring(RING):s.ring(RING) + 1]).then_inc(exp_done, 1)

            def rest_exponentials(n):
                g = n.c // GS % 2
                act.wait_ge(rest_max, n.turn(1, 1, GS))
                if not n.known() or n.c >= 2 * GS:
                    act.wait_ge(pv_done, n.times(1, -GS))
                act.activation(rest_probs[:, g, :], prest[:], ACT.Exp, bias=rest_neg[:, g:g + 1],
                               accum_out=rest_sum[:, g:g + 1]).then_inc(rest_exp, 1)

            def read_out(s):
                act.wait_ge(pv_done, s.times(1, 1))
                act.activation(out_raw[:, s.ring(2), :], po[:, 0:2 * P], ACT.Copy).then_inc(out_read, 1)

            def slot(s):
                exponentials(s)
                if not s.known() or s.c >= 2:
                    read_out(s + -2)
                if rest_now(s):
                    rest_exponentials(s + 2)
            rest_exponentials(slot0(0))
            run(act, slot)
            read_out(slot0(SLOTS - 2))
            read_out(slot0(SLOTS - 1))

        @block.vector
        def _(dve):
            def maximum(s):
                dve.wait_ge(score_made, s.times(1, 1))
                dve.tensor_reduce(neg_max[:, s.ring(RING):s.ring(RING) + 1], pscore[:, s.ring(2), :], AX_X, ALU.max,
                                  negate=True).then_inc(max_done, 1)

            def rest_maximum(n):
                g = n.c // GS % 2
                dve.wait_ge(rest_made, n.turn(1, 1, GS))
                dve.tensor_reduce(rest_neg[:, g:g + 1], prest[:], AX_X, ALU.max, negate=True).then_inc(rest_max, 1)

            def invert(s):
                r = slice(s.ring(RING), s.ring(RING) + 1)
                dve.wait_ge(exp_done, s.times(1, 1))
                dve.reciprocal(inv_row[:, r], row_sum[:, r]).then_inc(inv_done, 1)

            def rest_invert(n):
                g = n.c // GS % 2
                dve.wait_ge(rest_exp, n.turn(1, 1, GS))
                dve.reciprocal(rest_inv[:, g:g + 1], rest_sum[:, g:g + 1]).then_inc(rest_inverted, 1)

            def normalise(s):
                par = s.ring(2)
                dve.wait_ge(turned, s.times(1, 1))
                sums = pt[:, 0:2 * P].rearrange("p (h j c) -> p h j c", h=2, j=4)
                dve.reciprocal(inv_sum[:, par], sums[:, :, :, DH:DH + 1]).then_inc(recip, 1)
                dve.wait_ge(recip, s.times(1, 1))
                dst = G.A[:, :, head_cols(s)].rearrange("p (j h) d -> p h j d", h=2)
                dve.tensor_tensor(dst, sums[:, :, :, 0:DH],
                                  inv_sum[:, par].rearrange("p h (j o) -> p h j o", o=1).broadcast_to([P, 2, 4, DH]),
                                  ALU.mult).then_inc(filed, 1)

            def slot(s):
                maximum(s)
                if not s.known() or s.c >= 1:
                    invert(s + -1)
                if rest_now(s):
                    rest_maximum(s + 2)
                if rest_now(s + -1):
                    rest_invert(s + 1)
                if not s.known() or s.c >= 3:
                    normalise(s + -3)
            dve.memset(k_stack[0:PROD, :, SK:SKP], 0.0).then_inc(padded, 1)
            rest_maximum(slot0(0))
            rest_invert(slot0(0))
            run(dve, slot)
            invert(slot0(SLOTS - 1))
            for n in (3, 2, 1):
                normalise(slot0(SLOTS - n))


def newton_rsqrt(dve, link, y, v, t):
    link(dve.tensor_scalar(v, v, EPS, None, ALU.add))
    link(dve.tensor_scalar(y.bitcast(I32), v.bitcast(I32), 1, None, ALU.logical_shift_right))
    link(dve.tensor_scalar(y.bitcast(I32), y.bitcast(I32), -1.0, RSQRT_MAGIC, ALU.mult, ALU.add))
    link(dve.tensor_scalar(v, v, -0.5, None, ALU.mult))
    for _ in range(3):
        link(dve.tensor_tensor(t, y, y, ALU.mult))
        link(dve.tensor_tensor(t, t, v, ALU.mult))
        link(dve.scalar_tensor_tensor(y, t, 1.5, y, ALU.add, ALU.mult))


def stage_finish(nc, G, tag, source, operands, row=None, scratch=None, prefetch=False):
    memory, resonance = source == "memory", source == "resonance"
    with ExitStack() as st:
        sem, sb, psum = makers(nc, st, tag)
        stats = sb("stats", [P, 2, TILES, 6], F32)
        mv = sb("mean_var", [P, 2, CHUNKS, 2, 4], F32)
        rstd = sb("rstd", [P, 2, CHUNKS, 4], F32)
        newton = sb("newton", [P, 4], F32)
        shift = sb("shift", [P, TILES], F32)
        ps_t = psum("ps_turn", [P, 2, CH], F32)
        ps_ro = psum("ps_ro", [HARM, CH], F32)
        ps_y = psum("ps_y", [P, 2, CH], F32)
        ps_b = psum("ps_back", [P, 2, CH], F32)
        turned, turn_read = sem("turned"), sem("turn_read")
        ro_made, ro_read = sem("ro_made"), sem("ro_read")
        y_made, y_added, biased = sem("y_made"), sem("y_added"), sem("biased")
        step, affine, normed = sem("step"), sem("affine"), sem("normed")
        back_made, back_read, stored = sem("back_made"), sem("back_read"), sem("stored")
        w_step, col_made, w_ready = sem("w_step"), sem("col_made"), sem("w_ready")
        if memory:
            wc, ones = sb("w_centred", [P, 2, D], F32), sb("ones", [P, P], F32)
            shift_cols, brow = sb("shift_cols", [P, 2, P], F32), sb("bias_row", [P, D], F32)
            operands = lambda t: [(G.AT[:, k, t * P:(t + 1) * P], wc[:, k, :]) for k in range(2)]
        block = st.enter_context(nc.Block())

        def tile(t):
            return slice(t * P, (t + 1) * P)

        @block.tensor
        def _(pe):
            def turn(c):
                for n in range(2):
                    if c >= 1:
                        pe.wait_ge(turn_read, 2 * c - 1 + n)
                    for q in range(4):
                        if memory:
                            t, k = 4 * c + 2 * n + q // 2, q % 2
                            src = G.AT[:, k, tile(t)]
                        else:
                            t = 4 * c + q
                            b, tau = t // TPB, t % TPB
                            src = G.A[:, tau, b * D + n * P:b * D + (n + 1) * P]
                        mm = pe.transpose(ps_t[:, n, q * P:(q + 1) * P], src, G.ident[:])
                    mm.then_inc(turned, 1)

            def resonances(c):
                pe.wait_ge(turn_read, 2 * c + 2)
                if c >= 1:
                    pe.wait_ge(ro_read, c)
                for k in range(2):
                    mm = pe.matmul(ps_ro[:], G.basis[:, k, 96:128], G.AT[:, k, c * CH:(c + 1) * CH],
                                   start=(k == 0), stop=(k == 1))
                mm.then_inc(ro_made, 1)

            def out(c):
                if memory:
                    pe.wait_ge(w_ready, 2)
                elif resonance:
                    pe.wait_ge(ro_read, c + 1)
                else:
                    pe.wait_ge(turn_read, 2 * c + 2)
                for n in range(2):
                    if 2 * c + n >= 2:
                        pe.wait_ge(y_added, 2 * c + n - 1)
                    for q in range(2):
                        ops = operands(4 * c + 2 * n + q)
                        for m, (lhsT, rhs) in enumerate(ops):
                            mm = pe.matmul(ps_y[:, n, q * D:(q + 1) * D], lhsT, rhs, start=(m == 0),
                                           stop=(m == len(ops) - 1))
                    mm.then_inc(y_made, 1)

            def back(c):
                pe.wait_ge(normed, 4 * c + 4)
                for k in range(2):
                    if c >= 1:
                        pe.wait_ge(back_read, 2 * c - 1 + k)
                    for q in range(4):
                        mm = pe.transpose(ps_b[:, k, q * P:(q + 1) * P], G.X[:, 4 * c + q, k * P:(k + 1) * P], G.ident[:])
                    mm.then_inc(back_made, 1)

            if memory:
                pe.wait_ge(w_step, 3)
                for k in range(2):
                    mm = pe.matmul(ps_y[:, 0, 0:D], ones[:], wc[:, k, :], start=(k == 0), stop=(k == 1))
                mm.then_inc(col_made, 1)
                pe.wait_ge(w_step, 5)
                for k in range(2):
                    mm = pe.matmul(ps_y[:, 1, 0:D], shift_cols[:, k, :], G.wmat[:, M_LO, k, :],
                                   start=(k == 0), stop=(k == 1))
                mm.then_inc(col_made, 1)
            for i in range(CHUNKS + 2):
                if i < CHUNKS:
                    turn(i)
                if 1 <= i <= CHUNKS:
                    out(i - 1)
                if resonance and i < CHUNKS:
                    resonances(i)
                if i >= 2:
                    back(i - 2)

        @block.gpsimd
        def _(pool):
            if memory:
                pool.wait_ge(w_ready, 2)
            if row is not None:
                for t in range(TILES):
                    pool.tensor_tensor(G.X[:, t, :], G.X[:, t, :], brow[:] if memory else G.rvec[:, row, :],
                                       ALU.add).then_inc(biased, 1)

        @block.scalar
        def _(act):
            for i in range(CHUNKS + 2):
                if i < CHUNKS and not memory:
                    for k in range(2):
                        act.wait_ge(turned, 2 * i + k + 1)
                        act.activation(G.AT[:, k, i * CH:(i + 1) * CH], ps_t[:, k, :], ACT.Copy).then_inc(turn_read, 1)
                if i >= 2:
                    c = i - 2
                    act.wait_ge(affine, c + 1)
                    for t in range(4 * c, 4 * c + 4):
                        act.activation(G.X[:, t, :], G.X[:, t, :], ACT.Identity, bias=shift[:, t:t + 1],
                                       scale=rstd[:, 1, c, t % 4:t % 4 + 1]).then_inc(normed, 1)
                if resonance and i < CHUNKS:
                    act.wait_ge(ro_made, i + 1)
                    act.activation(G.ro[:, i * CH:(i + 1) * CH], ps_ro[:], ACT.Copy).then_inc(ro_read, 1)
                if i >= 2:
                    for k in range(2):
                        act.wait_ge(back_made, 2 * c + k + 1)
                        act.activation(G.xT[:, k, c * CH:(c + 1) * CH], ps_b[:, k, :], ACT.Copy).then_inc(back_read, 1)

        @block.vector
        def _(dve):
            link = linker(dve, step)

            def reduce(which, c):
                for q in range(4):
                    ins = dve.bn_aggr(mv[:, which, c, :, q], stats[:, which, 4 * c + q, :])
                link(ins)
                newton_rsqrt(dve, link, rstd[:, which, c, :], mv[:, which, c, 1, :], newton[:])

            def memory_stats(c):
                for n in range(2):
                    dve.wait_ge(turned, 2 * c + n + 1)
                    for q in range(2):
                        ins = dve.bn_stats(stats[:, 0, 4 * c + 2 * n + q, :], ps_t[:, n, q * D:(q + 1) * D])
                    ins.then_inc(turn_read, 1)
                dve.wait_ge(turn_read, 2 * c + 2)
                reduce(0, c)

            def add(c):
                for n in range(2):
                    dve.wait_ge(y_made, 2 * c + n + 1)
                    t = 4 * c + 2 * n
                    if row is not None:
                        dve.wait_ge(biased, t + 2)
                    if memory:
                        for q in range(2):
                            ins = dve.scalar_tensor_tensor(G.X[:, t + q, :], ps_y[:, n, q * D:(q + 1) * D],
                                                           rstd[:, 0, c, 2 * n + q:2 * n + q + 1], G.X[:, t + q, :],
                                                           ALU.mult, ALU.add)
                    else:
                        ins = dve.tensor_tensor(G.X[:, t:t + 2, :], ps_y[:, n, :].rearrange("p (q d) -> p q d", q=2),
                                                G.X[:, t:t + 2, :], ALU.add)
                    ins.then_inc(y_added, 1)
                    dve.wait_ge(y_added, 2 * c + n + 1)
                    for q in range(2):
                        ins = dve.bn_stats(stats[:, 1, t + q, :], G.X[:, t + q, :])
                link(ins)
                reduce(1, c)
                dve.scalar_tensor_tensor(shift[:, 4 * c:4 * c + 4], mv[:, 1, c, 0, :], -1.0, rstd[:, 1, c, :],
                                         ALU.mult, ALU.mult).then_inc(affine, 1)

            if memory:
                dve.memset(ones[:], 1.0 / D).then_inc(w_step, 1)
                for k in range(2):
                    dve.tensor_scalar(wc[:, k, :], G.wmat[:, M_LO, k, :], G.fvec[:, V_LG, k:k + 1], None,
                                      ALU.mult).then_inc(w_step, 1)
                dve.wait_ge(w_step, 1)
                for k in range(2):
                    dve.tensor_scalar(shift_cols[:, k, :], ones[:], float(D), G.fvec[:, V_LB, k:k + 1],
                                      ALU.mult, ALU.mult).then_inc(w_step, 1)
                dve.wait_ge(col_made, 1)
                for k in range(2):
                    ins = dve.tensor_tensor(wc[:, k, :], wc[:, k, :], ps_y[:, 0, 0:D], ALU.subtract)
                ins.then_inc(w_ready, 1)
                dve.wait_ge(col_made, 2)
                dve.tensor_tensor(brow[:], ps_y[:, 1, 0:D], G.rvec[:, row, :], ALU.add).then_inc(w_ready, 1)
            for i in range(CHUNKS + 1):
                if memory and i < CHUNKS:
                    memory_stats(i)
                if i >= 1:
                    add(i - 1)

        if prefetch:
            G.w_in = [sem(f"w_in{r}") for r in range(RW)]

            @block.sync
            def _(sp):
                for u in range(RW):
                    sp.dma_start(G.w_raw[:, u, :], G.ffn_units[u]).then_inc(G.w_in[u], 16)

        if scratch is not None:
            @block.sync
            def _(sp):
                for c in range(CHUNKS):
                    sp.wait_ge(normed, 4 * c + 4)
                    sp.dma_start(scratch[4 * c:4 * c + 4].rearrange("t p d -> p t d"),
                                 G.X[:, 4 * c:4 * c + 4, :]).then_inc(stored, 16)
                sp.wait_ge(stored, 16 * CHUNKS)


def stage_turn(nc, G, tag):
    with ExitStack() as st:
        sem, sb, psum = makers(nc, st, tag)
        ps = psum("ps_turn", [P, 4, CH], F32)
        turned, read = sem("turned"), sem("read")
        block = st.enter_context(nc.Block())
        groups = [(c, k) for c in range(CHUNKS) for k in range(2)]

        @block.tensor
        def _(pe):
            for n, (c, k) in enumerate(groups):
                if n >= 4:
                    pe.wait_ge(read, n - 3)
                for q in range(4):
                    mm = pe.transpose(ps[:, n % 4, q * P:(q + 1) * P], G.X[:, 4 * c + q, k * P:(k + 1) * P], G.ident[:])
                mm.then_inc(turned, 1)

        @block.scalar
        def _(act):
            for n, (c, k) in enumerate(groups):
                act.wait_ge(turned, n + 1)
                act.activation(G.xT[:, k, c * CH:(c + 1) * CH], ps[:, n % 4, :], ACT.Copy).then_inc(read, 1)


UNITS_A, UNITS_BC, UNITS_D = 4, 8, 4
UNITS = UNITS_A + 2 * UNITS_BC + UNITS_D
RW = 3
MB = HID // P


def stage_ffn0(nc, G):
    with ExitStack() as st:
        sem, sb, psum = makers(nc, st, "f0")
        raw, w_in = G.w_raw, G.w_in
        w_hi, w_lo = sb("w_hi", [P, RW, 1024], F32R), sb("w_lo", [P, RW, 1024], F32R)
        h_hi, h_lo = sb("h_hi", [P, 2, MB, CH], F32R), sb("h_lo", [P, 2, MB, CH], F32R)
        x_hi, x_lo = h_hi[:, 1, 0:2, :], h_lo[:, 1, 0:2, :]
        full = sb("h_full", [P, 2, CH], F32)
        gate = sb("gate", [P, 2, CH], F32)
        y_tmp, x_new, newton = sb("y_tmp", [P, 2, D], F32), sb("x_new", [P, 4, D], F32), sb("newton", [P, 1], F32)
        pp = psum("ps_h", [P, 4, CH], F32)
        pd = psum("ps_y", [P, 4, CH], F32)
        w_hi_done, w_lo_done = sem("w_hi"), sem("w_lo")
        x_hi_done, x_lo_done = sem("x_hi"), sem("x_lo")
        gate_lo_done = sem("gate_lo")
        made, gate_done, full_done, hi_done, lo_done = sem("made"), sem("gate"), sem("full"), sem("hi"), sem("lo")
        y_made, y_done, y_step, y_normed = sem("y_made"), sem("y_done"), sem("y_step"), sem("y_normed")
        low_summed, exact_col, exact_row, exact_done = sem("low_sum"), sem("exact_col"), sem("exact_row"), sem("exact")
        low_sum, low_abs = sb("low_sum", [P, UNITS], F32), sb("low_abs", [P, 1024], BF16)
        low_all, exact_f = sb("low_all", [P, 1], F32), sb("exact_f", [1, 1], F32)
        stats, mv, rstd = sb("stats", [P, 4, 6], F32), sb("mean_var", [P, 2, 4], F32), sb("rstd", [P, 2, 4], F32)
        NORM_STEPS = 2 + 4 + 9
        exact, exact_i = sb("exact", [P, 1], F32), sb("exact_i", [1, 1], I32)
        block = st.enter_context(nc.Block())
        TUR = 24
        LOW = 16

        def each_chunk(eng, chunk):
            chunk(0, False, True)
            with eng.Fori(1, CHUNKS - 1) as c:
                chunk(c, False)
            chunk(CHUNKS - 1, True)

        @block.sync
        def _(sp):
            def load(u):
                n = 1024 if u < UNITS - UNITS_D else 512
                src = G.ffn_units[u] if u < UNITS - UNITS_D else G.ffn_w3[u - (UNITS - UNITS_D)]
                sp.dma_start(raw[:, u % RW, 0:n], src).then_inc(w_in[u % RW], 16)

            def chunk(c, last, first=False):
                for u in range(UNITS - RW * last):
                    sp.wait_ge(w_lo_done, c * UNITS + (u + 1))
                    load((u + RW) % UNITS)
            each_chunk(sp, chunk)

        def cols(u):
            return 1024 if u % UNITS < UNITS - UNITS_D else 512

        def split_hi(act, c, u):
            act.wait_ge(w_in[u % RW], c * (16 * UNITS // RW) + 16 * (u // RW + 1))
            n = cols(u)
            act.activation(w_hi[:, u % RW, 0:n], raw[:, u % RW, 0:n], ACT.Copy).then_inc(w_hi_done, 1)

        def split_lo(dve, c, u):
            dve.wait_ge(w_hi_done, c * UNITS + (u + 1))
            n = cols(u)
            dve.tensor_tensor(w_lo[:, u % RW, 0:n], raw[:, u % RW, 0:n], w_hi[:, u % RW, 0:n].bitcast(F32),
                              ALU.subtract).then_inc(w_lo_done, 1)

        @block.tensor
        def _(pe):
            def parts(out, wcols, slot, hi, lo, first, last, low):
                pairs = ((w_hi, hi), (w_hi, lo), (w_lo, hi)) if low else ((w_hi, hi), (w_hi, lo))
                for n, (w, x) in enumerate(pairs):
                    mm = pe.matmul(out, w[:, slot, wcols], x, start=(first and n == 0),
                                   stop=(last and n == len(pairs) - 1))
                return mm

            def chunk(c, low):
                for u in range(UNITS_A):
                    pe.wait_ge(w_lo_done, c * UNITS + (u + 1))
                    if u == 0:
                        pe.wait_ge(x_lo_done, c + 1)
                    for m in (2 * u, 2 * u + 1):
                        for w in range(2):
                            bank = 2 * m + w
                            if m >= 2:
                                pe.wait_ge(gate_done if w == 0 else full_done, c * 8 + (m - 1))
                            for k in range(2):
                                off = (m % 2) * 512 + w * 256 + k * P
                                mm = parts(pp[:, bank % 4, :], slice(off, off + P), u % RW, x_hi[:, k, :], x_lo[:, k, :],
                                           k == 0, k == 1, low)
                            mm.then_inc(made, 1)
                for layer in range(2):
                    for m in range(MB):
                        u = UNITS_A + layer * UNITS_BC + m
                        tile = 8 + layer * 8 + m
                        pe.wait_ge(w_lo_done, c * UNITS + (u + 1))
                        if layer == 0 and m < 4:
                            pe.wait_ge(gate_done if m % 2 == 0 else full_done, c * 8 + (7 + m // 2))
                        else:
                            pe.wait_ge(hi_done, c * TUR + (tile - 3))
                        for k in range(MB):
                            if m == 0 and layer == 0:
                                pe.wait_ge(gate_lo_done, c * MB + (k + 1))
                            if m == 0 and layer == 1:
                                pe.wait_ge(lo_done, c * LOW + (k + 1))
                            mm = parts(pp[:, m % 4, :], slice(k * P, (k + 1) * P), u % RW, h_hi[:, layer, k, :],
                                       h_lo[:, layer, k, :], k == 0, k == MB - 1, low)
                        mm.then_inc(made, 1)
                if not isinstance(c, int):
                    pe.wait_ge(y_done, c * 8)
                for v in range(UNITS_D):
                    u = UNITS_A + 2 * UNITS_BC + v
                    pe.wait_ge(w_lo_done, c * UNITS + (u + 1))
                    for kk in range(2):
                        k = 2 * v + kk
                        pe.wait_ge(lo_done, c * LOW + (MB + k + 1))
                        for q in range(4):
                            pairs = ((h_hi, w_hi), (h_lo, w_hi)) + (((h_hi, w_lo),) if low else ())
                            for n, (h, w) in enumerate(pairs):
                                mm = pe.matmul(pd[:, q, 0:D], h[:, 0, k, q * P:(q + 1) * P],
                                               w[:, u % RW, kk * D:(kk + 1) * D], start=(k == 0 and n == 0),
                                               stop=(k == MB - 1 and n == len(pairs) - 1))
                    mm.then_inc(y_made, 1)

            chunk(0, True)
            pe.wait_ge(exact_col, 1)
            pe.transpose(pp[0:1, 0, 0:P], exact[:], G.ident[:]).then_inc(exact_row, 1)
            pe.wait_ge(exact_done, 1)
            all_exact = pe.value_load(exact_i[0:1, 0:1], min_val=0, max_val=1)
            with pe.If(all_exact == 1):
                with pe.Fori(1, CHUNKS) as c:
                    chunk(c, False)
            with pe.Else():
                with pe.Fori(1, CHUNKS) as c:
                    chunk(c, True)

        MADE = 32

        @block.scalar
        def _(act):
            def free_hi(c, u, last):
                if last and u + RW >= UNITS:
                    return
                if u < UNITS_A + 2 * UNITS_BC:
                    act.wait_ge(made, c * MADE + (4 * (u + 1) if u < UNITS_A else 16 + u - UNITS_A + 1))
                else:
                    act.wait_ge(y_made, c * UNITS_D + (u - UNITS_A - 2 * UNITS_BC + 1))
                split_hi(act, c, u + RW)

            def sum_low(u):
                act.wait_ge(w_lo_done, u + 1)
                if u > 0:
                    act.wait_ge(low_summed, u)
                act.activation(low_abs[:, 0:cols(u)], w_lo[:, u % RW, 0:cols(u)].bitcast(F32), ACT.Abs,
                               accum_out=low_sum[:, u:u + 1]).then_inc(low_summed, 1)

            def high(c, m):
                act.wait_ge(full_done, c * 8 + (m + 1))
                act.activation(h_hi[:, 0, m, :], full[:, m % 2, :], ACT.Copy).then_inc(hi_done, 1)

            def split_x(c):
                act.activation(x_hi, G.xT[:, :, bass.ds(c * CH, CH)], ACT.Copy).then_inc(x_hi_done, 1)

            def chunk(c, last, first=False):
                for u in range(UNITS_A):
                    for m in (2 * u, 2 * u + 1):
                        act.wait_ge(made, c * MADE + (2 * m + 1))
                        if m >= 2:
                            act.wait_ge(full_done, c * 8 + (m - 1))
                        act.activation(gate[:, m % 2, :], pp[:, (2 * m) % 4, :], ACT.Silu,
                                       scale=G.ffn_s[:, 0, m:m + 1]).then_inc(gate_done, 1)
                        if m >= 1:
                            high(c, m - 1)
                    if u == UNITS_A - 1:
                        high(c, MB - 1)
                    if first:
                        sum_low(u)
                    free_hi(c, u, last)
                for layer in range(2):
                    for m in range(MB):
                        n = 8 + 8 * layer + m
                        act.wait_ge(made, c * MADE + (16 + 8 * layer + m + 1))
                        if n < 10:
                            act.wait_ge(gate_lo_done, c * MB + (n - 1))
                        else:
                            act.wait_ge(lo_done, c * LOW + (n - 9))
                        act.activation(full[:, m % 2, :], pp[:, m % 4, :], ACT.Gelu,
                                       scale=G.ffn_s[:, 2 + layer, m:m + 1])
                        act.activation(h_hi[:, 1 - layer, m, :], pp[:, m % 4, :], ACT.Gelu,
                                       scale=G.ffn_s[:, 2 + layer, m:m + 1]).then_inc(hi_done, 1)
                        if first:
                            sum_low(UNITS_A + layer * UNITS_BC + m)
                        free_hi(c, UNITS_A + layer * UNITS_BC + m, last)
                if not last:
                    split_x(c + 1)
                for v in range(UNITS_D):
                    if first:
                        sum_low(UNITS_A + 2 * UNITS_BC + v)
                    free_hi(c, UNITS_A + 2 * UNITS_BC + v, last)
            split_x(0)
            for u in range(RW):
                split_hi(act, 0, u)
            each_chunk(act, chunk)

        @block.gpsimd
        def _(pool):
            def chunk(c, last, first=False):
                for m in range(MB):
                    pool.wait_ge(hi_done, c * TUR + (m + 1))
                    pool.tensor_tensor(h_lo[:, 0, m, :], full[:, m % 2, :], h_hi[:, 0, m, :].bitcast(F32),
                                       ALU.subtract).then_inc(gate_lo_done, 1)
            each_chunk(pool, chunk)

        @block.vector
        def _(dve):
            def split_x(c):
                dve.wait_ge(x_hi_done, c + 1)
                dve.tensor_tensor(x_lo, G.xT[:, :, bass.ds(c * CH, CH)], x_hi.bitcast(F32),
                                  ALU.subtract).then_inc(x_lo_done, 1)

            def finish(c, step):
                count = [0] if step < 3 else [2]

                def link(ins):
                    count[0] += 1
                    ins.then_inc(y_step, 1)
                    dve.wait_ge(y_step, c * NORM_STEPS + count[0])
                if step < 2:
                    if step == 0:
                        dve.wait_ge(y_made, c * UNITS_D + UNITS_D)
                    for q in (2 * step, 2 * step + 1):
                        dve.tensor_tensor(y_tmp[:, q % 2, :], pd[:, q, 0:D], G.rvec[:, R_W3S, :],
                                          ALU.mult).then_inc(y_done, 1)
                        dve.wait_ge(y_done, c * 8 + (2 * q + 1))
                        dve.tensor_tensor(x_new[:, q, :], y_tmp[:, q % 2, :], G.X[:, c * 4 + q, :],
                                          ALU.add).then_inc(y_done, 1)
                elif step == 2:
                    dve.wait_ge(y_done, c * 8 + 8)
                    for q in range(4):
                        ins = dve.bn_stats(stats[:, q, :], x_new[:, q, :])
                    link(ins)
                    dve.memset(newton[:, 0:1], 0.0)
                    for q in range(4):
                        ins = dve.bn_aggr(mv[:, :, q], stats[:, q, :])
                    link(ins)
                elif step == 3:
                    newton_rsqrt(dve, link, rstd[:, 0, :], mv[:, 1, :], rstd[:, 1, :])
                    assert count[0] == NORM_STEPS
                else:
                    for q in range(4):
                        dve.tensor_scalar(G.X[:, c * 4 + q, :], x_new[:, q, :], mv[:, 0, q:q + 1], rstd[:, 0, q:q + 1], ALU.subtract,
                                          ALU.mult).then_inc(y_normed, 1)

            def chunk(c, last, first=False):
                def next_lo(u):
                    if first:
                        dve.wait_ge(low_summed, u + 1)
                    if not (last and u + RW >= UNITS):
                        split_lo(dve, c, u + RW)
                for u in range(UNITS_A):
                    for m in (2 * u, 2 * u + 1):
                        dve.wait_ge(made, c * MADE + (2 * m + 2))
                        dve.wait_ge(gate_done, c * 8 + (m + 1))
                        if m >= 2:
                            dve.wait_ge(gate_lo_done, c * MB + (m - 1))
                        dve.scalar_tensor_tensor(full[:, m % 2, :], pp[:, (2 * m + 1) % 4, :], G.ffn_s[:, 1, m:m + 1],
                                                 gate[:, m % 2, :], ALU.mult, ALU.mult).then_inc(full_done, 1)
                    next_lo(u)
                for layer in range(2):
                    for m in range(MB):
                        dve.wait_ge(hi_done, c * TUR + (8 + 8 * layer + m + 1))
                        dve.tensor_tensor(h_lo[:, 1 - layer, m, :], full[:, m % 2, :],
                                          h_hi[:, 1 - layer, m, :].bitcast(F32), ALU.subtract).then_inc(lo_done, 1)
                        next_lo(UNITS_A + layer * UNITS_BC + m)
                        if not first and layer == 0 and 1 <= m <= 5:
                            finish(c - 1, m - 1)
                if not last:
                    split_x(c + 1)
                for v in range(UNITS_D):
                    next_lo(UNITS - UNITS_D + v)
                if first:
                    dve.tensor_reduce(low_all[:], low_sum[:], AX_X, ALU.add).then_inc(low_summed, 1)
                    dve.wait_ge(low_summed, UNITS + 1)
                    dve.tensor_scalar(exact[:], low_all[:], 0.0, None, ALU.is_equal).then_inc(exact_col, 1)
                    dve.wait_ge(exact_row, 1)
                    dve.tensor_reduce(exact_f[:], pp[0:1, 0, 0:P], AX_X, ALU.min).then_inc(exact_row, 1)
                    dve.wait_ge(exact_row, 2)
                    dve.tensor_copy(exact_i[:], exact_f[:]).then_inc(exact_done, 1)
                if last:
                    for step in range(5):
                        finish(c, step)
            split_x(0)
            for u in range(RW):
                split_lo(dve, 0, u)
            each_chunk(dve, chunk)


def stage_holographic(nc, G):
    with ExitStack() as st:
        sem, sb, psum = makers(nc, st, "lo")
        kq = sb("key_query", [P, 2, 2, CH], F32)
        val = sb("value", [P, 2, 2, CH], F32)
        th = sb("tanh", [P, 2, 2, 2, CH], F32)
        ph, turns = sb("phase", [P, 2, 2, CH], F32), sb("turns", [P, 2, 2, CH], F32)
        sn, cs = sb("sine", [P, 3, 2, CH], F32), sb("cosine", [P, 3, 2, CH], F32)
        bound, mem = sb("bound", [P, 2, 2, CH], F32), sb("memory", [P, 2, 2, CH], F32)
        keep = sb("keep", [P, CH], F32)
        vb = sb("value_bias", [P, 2], F32)
        ps = psum("ps_lo", [P, 8, CH], F32)
        const, made, read = sem("const"), sem("made"), sem("read")
        step, reduced, trig, magnitude = sem("step"), sem("reduced"), sem("trig"), sem("magnitude")
        doubled = sem("doubled")
        rev = sb("per_revolution", [P, 2], F32)
        bound_done, scanned, mixed, filed = sem("bound"), sem("scanned"), sem("mixed"), sem("filed")
        block = st.enter_context(nc.Block())
        TILES_C = 10
        ORDER = [(which, blk) for which in range(3) for blk in range(2)] + [(3, 0), (4, 0), (3, 1), (4, 1)]
        units = [(c, blk) for c in range(CHUNKS) for blk in range(2)]

        @block.gpsimd
        def _(pool):
            pool.memset(keep[:], 1.0).then_inc(const, 1)
            pool.wait_ge(const, 1)
            pool.memset(keep[:].rearrange("p (g t) -> p g t", t=SCAN)[:, :, 0:1], 0.0).then_inc(const, 1)
            pool.tensor_scalar(vb[:], G.fvec[:, V_LBV, :], 1.0 / 16, None, ALU.mult).then_inc(const, 1)

            def bind(n):
                c, blk = units[n]
                pool.wait_ge(trig, 2 * n + 2)
                for part, src in enumerate((cs, sn)):
                    pool.tensor_tensor(bound[:, n % 2, part, :], val[:, c % 2, blk, :], src[:, n % 3, 0, :],
                                       ALU.mult).then_inc(bound_done, 1)

            def retrieve(n):
                pool.wait_ge(scanned, 2 * n + 2)
                for part, src in enumerate((cs, sn)):
                    pool.tensor_tensor(mem[:, n % 2, part, :], mem[:, n % 2, part, :], src[:, n % 3, 1, :],
                                       ALU.mult).then_inc(mixed, 1)
            for t in range(TILES):
                pool.tensor_scalar(G.X[:, t, :], G.X[:, t, :], 2.0, None, ALU.mult).then_inc(doubled, 1)
            for n in range(len(units)):
                bind(n)
                if n >= 1:
                    retrieve(n - 1)
            retrieve(len(units) - 1)

        @block.tensor
        def _(pe):
            n = 0
            for c in range(CHUNKS):
                for which, blk in ORDER:
                    mat = (M_LK, M_LQ, M_LV, M_LKP, M_LQP)[which]
                    if n >= 8:
                        pe.wait_ge(read, n - 7)
                    if which >= 3:
                        pe.wait_ge(read, c * TILES_C + (2 if which == 3 else 4))
                    for k in range(2):
                        rhs = kq[:, which - 3, k, :] if which >= 3 else G.xT[:, k, c * CH:(c + 1) * CH]
                        mm = pe.matmul(ps[:, n % 8, :], G.wmat[:, mat, k, blk * P:(blk + 1) * P], rhs,
                                       start=(k == 0), stop=(k == 1))
                    mm.then_inc(made, 1)
                    n += 1

        @block.scalar
        def _(act):
            act.wait_ge(const, 3)

            def trigonometry(n):
                act.wait_ge(reduced, n + 1)
                if n >= 3:
                    act.wait_ge(mixed, 2 * n - 4)
                act.activation(turns[:, n % 2], ph[:, n % 2], ACT.Abs).then_inc(magnitude, 1)
                act.activation(sn[:, n % 3], ph[:, n % 2], ACT.Sin).then_inc(trig, 1)
                act.wait_ge(magnitude, n + 1)
                act.activation(cs[:, n % 3], turns[:, n % 2], ACT.Sin, bias=G.halfpi[:, 0:1],
                               scale=-1.0).then_inc(trig, 1)
            n = 0
            for c in range(CHUNKS):
                for which, blk in ORDER:
                    vec = (V_LBK, V_LBQ, V_LBV, V_LBKP, V_LBQP)[which]
                    if c >= 1 and (which, blk) in ((2, 0), (3, 0)):
                        trigonometry(2 * c - 2 if which == 2 else 2 * c - 1)
                    act.wait_ge(made, n + 1)
                    src = ps[:, n % 8, :]
                    if which < 2:
                        act.activation(kq[:, which, blk, :], src, ACT.Identity,
                                       bias=G.fvec[:, vec, blk:blk + 1]).then_inc(read, 1)
                    elif which == 2:
                        if c >= 2:
                            act.wait_ge(bound_done, 4 * (c - 1))
                        act.activation(val[:, c % 2, blk, :], src, ACT.Identity, bias=vb[:, blk:blk + 1],
                                       scale=1.0 / 16).then_inc(read, 1)
                    else:
                        if c >= 2:
                            act.wait_ge(reduced, 2 * (c - 1))
                        act.activation(th[:, c % 2, which - 3, blk, :], src, ACT.Tanh,
                                       bias=G.fvec[:, vec, blk:blk + 1]).then_inc(read, 1)
                    n += 1
            trigonometry(2 * CHUNKS - 2)
            trigonometry(2 * CHUNKS - 1)

        @block.vector
        def _(dve):
            link = linker(dve, step)

            def reduce_phase(n):
                c, blk = units[n]
                dve.wait_ge(read, (c + 1) * TILES_C - 2 * (1 - blk))
                if n >= 2:
                    dve.wait_ge(trig, 2 * n - 2)
                p, k = ph[:, n % 2], turns[:, n % 2]
                dve.tensor_scalar(p, th[:, c % 2, :, blk, :], G.fvec[:, V_PS, blk:blk + 1], None, ALU.mult)
                link(dve.tensor_scalar(k, th[:, c % 2, :, blk, :], rev[:, blk:blk + 1], ROUND, ALU.mult, ALU.add))
                link(dve.tensor_scalar(k, k, -ROUND, None, ALU.add))
                link(dve.scalar_tensor_tensor(p, k, -C1, p, ALU.mult, ALU.add))
                link(dve.scalar_tensor_tensor(p, k, -(C2 + C3), p, ALU.mult, ALU.add))
                dve.tensor_scalar(p, p, PI_IN, -PI_IN, ALU.min, ALU.max).then_inc(reduced, 1)

            def scan(n):
                dve.wait_ge(bound_done, 2 * n + 2)
                if n >= 2:
                    dve.wait_ge(filed, n - 1)
                for part in range(2):
                    dve.tensor_tensor_scan(mem[:, n % 2, part, :], keep[:], bound[:, n % 2, part, :], 0.0,
                                           ALU.mult, ALU.add).then_inc(scanned, 1)

            def file(n):
                c, blk = units[n]
                dve.wait_ge(mixed, 2 * n + 2)
                dve.tensor_tensor(G.AT[:, blk, c * CH:(c + 1) * CH], mem[:, n % 2, 0, :], mem[:, n % 2, 1, :],
                                  ALU.add).then_inc(filed, 1)
            N = len(units)
            dve.wait_ge(const, 3)
            link(dve.tensor_scalar(rev[:], G.fvec[:, V_PS, :], 1.0 / TWO_PI, None, ALU.mult))
            for n in range(N + 2):
                if n < N:
                    reduce_phase(n)
                if 1 <= n <= N:
                    scan(n - 1)
                if n >= 2:
                    file(n - 2)


def stage_gather(nc, I, G):
    with ExitStack() as st:
        sem, sb, psum = makers(nc, st, "ga")
        col_i = sb("col_i", [P, 2, MT], I32)
        row_i = sb("row_i", [P, 2, NMOE], I32)
        col_f, row_f = sb("col_f", [P, 2, MT], F32), sb("row_f", [P, 2, NMOE], F32)
        rows = sb("row_token", [P, NMOE], F32)
        same = sb("same", [P, MT, NMOE], F32)
        dup = sb("dup", [P, MT], F32)
        col_in, row_in, gathered = sem("col_in"), sem("row_in"), sem("gathered")
        step, same_done, kept, turned, read = sem("step"), sem("same"), sem("kept"), sem("turned"), sem("read")
        tok_done = sem("tok")
        G.small_in, G.expert_in, G.shared_in = sem("small_in"), sem("expert_in"), sem("shared_in")
        ps = psum("ps_ga", [P, 2, CH], F32)
        block = st.enter_context(nc.Block())

        @block.sync
        def _(sp):
            for n, name in enumerate(("index_b", "index_t")):
                with nc.allow_non_contiguous_dma(reason="512 indices"):
                    sp.dma_start(col_i[:, n, :], I[name].rearrange("(q p) -> p q", p=P)).then_inc(col_in, 16)
            for n, name in enumerate(("index_b", "index_t")):
                sp.dma_start(row_i[:, n, :], I[name].rearrange("(o m) -> o m", o=1).broadcast_to([P, NMOE])).then_inc(row_in, 16)
            sp.dma_start(G.gw[:], I["gw"].rearrange("k p c -> p k c")).then_inc(G.small_in, 16)
            sp.dma_start(G.sw12[:], I["sw12"].rearrange("k p c -> p k c")).then_inc(G.small_in, 16)
            sp.wait_ge(gathered, 16 * MT)
            for k in range(2):
                sp.dma_start(G.ew12[:, k], I["ew12"][k]).then_inc(G.expert_in, 16)
            sp.dma_start(G.eb[:], I["eb"]).then_inc(G.expert_in, 16)
            sp.dma_start(G.sw3[:], I["sw3"]).then_inc(G.shared_in, 16)
            sp.dma_start(G.ew3[:], I["ew3"]).then_inc(G.shared_in, 16)

        @block.vector
        def _(dve):
            link = linker(dve, step)
            dve.wait_ge(col_in, 32)
            link(dve.tensor_copy(col_f[:], col_i[:]))
            link(dve.scalar_tensor_tensor(G.tok_f[:], col_f[:, 0, :], float(S), col_f[:, 1, :], ALU.mult, ALU.add))
            dve.tensor_copy(G.tok[:], G.tok_f[:]).then_inc(tok_done, 1)
            dve.wait_ge(row_in, 32)
            link(dve.tensor_copy(row_f[:], row_i[:]))
            link(dve.scalar_tensor_tensor(rows[:], row_f[:, 0, :], float(S), row_f[:, 1, :], ALU.mult, ALU.add))
            for q in range(MT):
                dve.tensor_scalar(same[:, q, :], rows[:], G.tok_f[:, q:q + 1], None, ALU.is_equal).then_inc(same_done, 1)
            dve.wait_ge(kept, MT)
            link(dve.tensor_reduce(dup[:], same[:], AX_X, ALU.max))
            link(dve.scalar_tensor_tensor(G.tok_f[:], dup[:], float(2 * TOK), G.tok_f[:], ALU.mult, ALU.add))
            link(dve.tensor_copy(G.tok_once[:], G.tok_f[:]))

        @block.gpsimd
        def _(pool):
            pool.wait_ge(tok_done, 1)
            for q in range(MT):
                pool.indirect_dma_start(G.X[:, TILES + q, :], None, G.x_dram.rearrange("t p d -> (t p) d"),
                                        bass.IndirectOffsetOnAxis(ap=G.tok[:, q:q + 1], axis=0)).then_inc(gathered, 16)
            for q in range(MT):
                pool.wait_ge(same_done, q + 1)
                pool.affine_select(out=same[:, q, :], in_=same[:, q, :], compare_op=ALU.is_gt, fill=0.0, base=q * P,
                                   pattern=[[-1, NMOE]], channel_multiplier=1).then_inc(kept, 1)

        @block.tensor
        def _(pe):
            pe.wait_ge(gathered, 16 * MT)
            for blk in range(2):
                for q in range(MT):
                    mm = pe.transpose(ps[:, blk, q * P:(q + 1) * P], G.X[:, TILES + q, blk * P:(blk + 1) * P], G.ident[:])
                mm.then_inc(turned, 1)

        @block.scalar
        def _(act):
            for blk in range(2):
                act.wait_ge(turned, blk + 1)
                act.activation(G.xT[:, blk, TOK:TOK + NMOE], ps[:, blk, :], ACT.Copy).then_inc(read, 1)


def stage_gates(nc, G):
    with ExitStack() as st:
        sem, sb, psum = makers(nc, st, "sh")
        h = sb("sh_h", [P, 4, D], F32)
        logits, scores = sb("logits", [P, MT, 9], F32), sb("scores", [P, MT, 9], F32)
        choice, best = sb("choice", [P, MT, NEXP], F32), sb("best", [P, MT, NEXP], F32)
        best_i, best_f = sb("best_i", [P, MT, NEXP], U32), sb("best_f", [P, MT], F32)
        lane_i, lane = sb("lane_i", [P, NEXP], I32), sb("lane", [P, NEXP], F32)
        onehot, top = sb("onehot", [P, MT, NEXP], F32), sb("top", [P, MT, NEXP], F32)
        pmax, psums = sb("pmax", [P, MT], F32), sb("psums", [P, MT], F32)
        pick_f = sb("pick_f", [NEXP, NEXP, P], F32)
        ps = psum("ps_sh", [P, 4, CH], F32)
        pg = psum("ps_g", [P, CH], F32)
        pt = psum("ps_t", [P, CH], F32)
        made, biased, silu, z_done = sem("made"), sem("biased"), sem("silu"), sem("z")
        step, gates_made, logit_done, score_done = sem("step"), sem("gates"), sem("logit"), sem("score")
        hot_done, hotT_made, hotT_read = sem("hot"), sem("hotT"), sem("hotTr")
        lanes, pmax_done, pair_done, picked = sem("lanes"), sem("pmax"), sem("pair"), sem("picked")
        block = st.enter_context(nc.Block())

        @block.tensor
        def _(pe):
            pe.wait_ge(G.small_in, 32)
            for q in range(MT):
                for k in range(2):
                    mm = pe.matmul(pg[:, q * 16:q * 16 + 9], G.xT[:, k, TOK + q * P:TOK + (q + 1) * P], G.gw[:, k, :],
                                   start=(k == 0), stop=(k == 1))
            mm.then_inc(gates_made, 1)
            for t in range(XT):
                if t >= 4:
                    pe.wait_ge(biased, t - 3)
                for k in range(2):
                    mm = pe.matmul(ps[:, t % 4, 0:D], G.xT[:, k, t * P:(t + 1) * P], G.sw12[:, k, :],
                                   start=(k == 0), stop=(k == 1))
                mm.then_inc(made, 1)
                if t == XT - 5:
                    pe.wait_ge(hot_done, MT)
                    for q in range(MT):
                        mm = pe.transpose(pt[0:NEXP, q * P:(q + 1) * P], onehot[:, q, :], G.ident[:])
                    mm.then_inc(hotT_made, 1)

        @block.gpsimd
        def _(pool):
            pool.iota(lane_i[:], pattern=[[1, NEXP]], base=0, channel_multiplier=0).then_inc(lanes, 1)
            pool.memset(pick_f[:], 0.0).then_inc(picked, 1)
            pool.wait_ge(picked, 1)
            pool.affine_select(out=pick_f[:], in_=pick_f[:], compare_op=ALU.not_equal, fill=1.0, base=0,
                               pattern=[[-1, NEXP], [0, P]], channel_multiplier=1).then_inc(picked, 1)
            pool.wait_ge(picked, 2)
            pool.tensor_copy(G.pick[:], pick_f[:]).then_inc(picked, 1)
            for t in range(XT):
                pool.wait_ge(silu, t + 1)
                pool.tensor_tensor(G.Z[:, t, :], G.Z[:, t, :], h[:, t % 4, EH:D], ALU.mult).then_inc(z_done, 1)

        @block.scalar
        def _(act):
            act.wait_ge(logit_done, 1)
            act.activation(scores[:], logits[:], ACT.Sigmoid).then_inc(score_done, 1)
            for t in range(XT):
                act.wait_ge(biased, t + 1)
                act.activation(G.Z[:, t, :], h[:, t % 4, 0:EH], ACT.Silu).then_inc(silu, 1)
                if t == XT - 5:
                    act.wait_ge(hotT_made, 1)
                    for dst in (G.hotT, G.hotT_b):
                        act.activation(dst[:], pt[0:NEXP, :], ACT.Copy).then_inc(hotT_read, 1)
            act.wait_ge(pmax_done, 1)
            for q in range(MT):
                act.activation(G.pair[:, q, :], G.pair[:, q, :], ACT.Exp, bias=pmax[:, q:q + 1],
                               accum_out=psums[:, q:q + 1]).then_inc(pair_done, 1)

        @block.vector
        def _(dve):
            link = linker(dve, step)

            def shared(t):
                dve.wait_ge(made, t + 1)
                if t >= 4:
                    dve.wait_ge(z_done, t - 3)
                dve.tensor_tensor(h[:, t % 4, :], ps[:, t % 4, 0:D], G.rvec[:, R_SB12, :], ALU.add).then_inc(biased, 1)

            dve.memset(G.pair[:], 0.0)
            dve.wait_ge(lanes, 1)
            dve.tensor_copy(lane[:], lane_i[:])
            dve.wait_ge(gates_made, 1)
            dve.tensor_tensor(logits[:], pg[:, 0:16 * MT].rearrange("p (q c) -> p q c", q=MT)[:, :, 0:9],
                              G.grow[:, 0:9].rearrange("p (o c) -> p o c", o=1).broadcast_to([P, MT, 9]),
                              ALU.add).then_inc(logit_done, 1)
            for t in range(4):
                shared(t)
            dve.wait_ge(score_done, 1)
            link(dve.tensor_tensor(choice[:], scores[:, :, 1:9],
                                   G.grow[:, 9:17].rearrange("p (o c) -> p o c", o=1).broadcast_to([P, MT, NEXP]), ALU.add))
            for q in range(MT):
                ins = dve.max(best[:, q, :], choice[:, q, :])
            link(ins)
            for q in range(MT):
                ins = dve.max_index(best_i[:, q, :], best[:, q, :], choice[:, q, :])
            link(ins)
            link(dve.tensor_copy(best_f[:], best_i[:, :, 0]))
            for q in range(MT):
                dve.tensor_scalar(onehot[:, q, :], lane[:], best_f[:, q:q + 1], None, ALU.is_equal).then_inc(hot_done, 1)
            for t in range(4, 8):
                shared(t)
            dve.wait_ge(hot_done, MT)
            link(dve.tensor_tensor(top[:], scores[:, :, 1:9], onehot[:], ALU.mult))
            dve.tensor_copy(G.pair[:, :, 0:1], scores[:, :, 0:1])
            link(dve.tensor_reduce(G.pair[:, :, 1:2], top[:], AX_X, ALU.add))
            dve.tensor_reduce(pmax[:], G.pair[:], AX_X, ALU.max, negate=True).then_inc(pmax_done, 1)
            for t in range(8, XT):
                shared(t)
            dve.wait_ge(pair_done, MT)
            link(dve.reciprocal(psums[:], psums[:]))
            link(dve.tensor_tensor(G.pair[:], G.pair[:], psums[:].rearrange("p (q o) -> p q o", o=1).broadcast_to([P, MT, 2]),
                                   ALU.mult))


def stage_mixture(nc, G, out):
    with ExitStack() as st:
        sem, sb, psum = makers(nc, st, "mx")
        masked = sb("masked_x", [P, 3, 2, NMOE], F32)
        zmasked = sb("masked_z", [P, 3, NMOE], F32)
        gate = sb("gate", [P, MT, EH], F32)
        ze, zeT = sb("ze", [P, MT, EH], F32), sb("zeT", [P, NMOE], F32)
        zstat, zmv = sb("zstat", [P, XT, 6], F32), sb("zmv", [P, 2, XT], F32)
        zrstd, zshift, ztmp = sb("zrstd", [P, XT], F32), sb("zshift", [P, XT], F32), sb("ztmp", [P, XT], F32)
        stats, mv = sb("stats", [P, XT, 6], F32), sb("mv", [P, MT + 2, 2, 4], F32)
        rstd, shift, tmp = sb("rstd", [P, XT + 4], F32), sb("shift", [P, XT], F32), sb("tmp", [P, 4], F32)
        ph = psum("ps_h", [P, MT, CH], F32)
        pmask = psum("ps_mask", [P, CH], F32)
        pt = psum("ps_turn", [P, CH], F32)
        pso = psum("ps_shared", [P, 2, CH], F32)
        mask_made, x_masked, h_made = sem("mask_made"), sem("x_masked"), sem("h_made")
        h_used, z_masked, y_used, y_made = sem("h_used"), sem("z_masked"), sem("y_used"), sem("y_made")
        z_affine, z_normed, turned, turn_read = sem("z_affine"), sem("z_normed"), sem("turned"), sem("turn_read")
        gated, z_read, ze_normed = sem("gated"), sem("z_read"), sem("ze_normed")
        so_made, so_added, biased = sem("so_made"), sem("so_added"), sem("biased")
        step, affine, normed, last_normed = sem("step"), sem("affine"), sem("normed"), sem("last_normed")
        stored, scattered = sem("stored"), sem("scattered")
        block = st.enter_context(nc.Block())
        ZG = XT // 4
        PAIRS = TILES // 2

        def tile(t):
            return slice(t * P, (t + 1) * P)

        @block.tensor
        def _(pe):
            def mask(n):
                if n >= 1:
                    pe.wait_ge(x_masked, min(n, NEXP))
                if n > NEXP:
                    pe.wait_ge(z_masked, n - NEXP)
                pe.matmul(pmask[:], G.pick[:, n % NEXP, :], G.hotT_b[:], start=True, stop=True).then_inc(mask_made, 1)

            def hidden(e):
                pe.wait_ge(x_masked, e + 1)
                for t in range(MT):
                    for k in range(2):
                        mm = pe.matmul(ph[:, t, 0:D], masked[:, e % 3, k, tile(t)], G.ew12[:, k, e, :],
                                       start=(e == 0 and k == 0), stop=False)
                    if e == NEXP - 1:
                        pe.matmul(ph[:, t, 0:D], G.hotT[:, tile(t)], G.eb[:, 0:D], start=False, stop=True).then_inc(h_made, 1)
                if e < NEXP - 1:
                    mm.then_inc(h_used, 1)

            def turn(g, src, ready, count):
                pe.wait_ge(ready, count)
                if g >= 1:
                    pe.wait_ge(turn_read, g)
                for q in range(4):
                    mm = pe.transpose(pt[:, tile(q)], src(q), G.ident[:])
                mm.then_inc(turned, 1)

            def shared(n, pair):
                if n >= 2:
                    pe.wait_ge(so_added, n - 1)
                for q in range(2):
                    mm = pe.matmul(pso[:, n % 2, q * D:(q + 1) * D], G.ZT[:, 0, tile(2 * pair + q)], G.sw3[:],
                                   start=True, stop=True)
                mm.then_inc(so_made, 1)

            def outputs(e):
                pe.wait_ge(z_masked, e + 1)
                for t in range(MT):
                    if e == 0:
                        pe.wait_ge(z_read, t + 1)
                    mm = pe.matmul(ph[:, t, 0:D], zmasked[:, e % 3, tile(t)], G.ew3[:, e, :], start=(e == 0), stop=False)
                    if e == NEXP - 1:
                        pe.matmul(ph[:, t, 0:D], G.hotT[:, tile(t)], G.eb[:, D:2 * D], start=False,
                                  stop=True).then_inc(y_made, 1)
                if e < NEXP - 1:
                    mm.then_inc(y_used, 1)

            mask(0)
            pe.wait_ge(G.expert_in, 48)
            for e in range(NEXP):
                mask(e + 1)
                hidden(e)
            for g in range(ZG):
                turn(g, lambda q: G.Z[:, 4 * g + q, :], z_normed, 4 * g + 4)
            turn(ZG, lambda q: ze[:, q, :], ze_normed, MT)
            pe.wait_ge(G.shared_in, 32)
            pe.wait_ge(turn_read, ZG)
            for n in range(2):
                shared(n, PAIRS + n)
            for e in range(NEXP):
                shared(2 + e, e)
                if e >= 1:
                    mask(NEXP + e)
                    outputs(e - 1)
            outputs(NEXP - 1)

        @block.gpsimd
        def _(pool):
            for t in range(TILES):
                pool.tensor_tensor(G.X[:, t, :], G.X[:, t, :], G.rvec[:, R_SB3, :], ALU.add).then_inc(biased, 1)
            pool.wait_ge(stored, 16 * CHUNKS)
            pool.wait_ge(last_normed, MT)
            for q in range(MT):
                pool.indirect_dma_start(out.rearrange("t p d -> (t p) d"),
                                        bass.IndirectOffsetOnAxis(ap=G.tok_once[:, q:q + 1], axis=0),
                                        G.X[:, TILES + q, :], None, bounds_check=TOK - 1,
                                        oob_is_err=False).then_inc(scattered, 16)
            pool.wait_ge(scattered, 16 * MT)

        @block.scalar
        def _(act):
            act.wait_ge(z_affine, 1)
            for t in range(XT):
                act.activation(G.Z[:, t, :], G.Z[:, t, :], ACT.Identity, bias=zshift[:, t:t + 1],
                               scale=zrstd[:, t:t + 1]).then_inc(z_normed, 1)
            for t in range(MT):
                act.wait_ge(h_made, t + 1)
                act.activation(gate[:, t, :], ph[:, t, 0:EH], ACT.Silu).then_inc(gated, 1)
            for g in range(ZG + 1):
                act.wait_ge(turned, g + 1)
                dst, n = (G.ZT[:, 0, g * CH:(g + 1) * CH], 0) if g < ZG else (zeT[:], 2)
                act.activation(dst, pt[:], ACT.Identity, bias=G.evec[:, n + 1:n + 2],
                               scale=G.evec[:, n:n + 1]).then_inc(turn_read, 1)
            for c in range(CHUNKS):
                act.wait_ge(affine, c + 1)
                for t in range(4 * c, 4 * c + 4):
                    act.activation(G.X[:, t, :], G.X[:, t, :], ACT.Identity, bias=shift[:, t:t + 1],
                                   scale=rstd[:, t:t + 1]).then_inc(normed, 1)

        @block.vector
        def _(dve):
            link = linker(dve, step)

            def mask_x(e):
                dve.wait_ge(mask_made, e + 1)
                if e >= 3:
                    dve.wait_ge(h_used, e - 2)
                dve.tensor_tensor(masked[:, e % 3], pmask[:].rearrange("p (o t) -> p o t", o=1).broadcast_to([P, 2, NMOE]),
                                  G.xT[:, :, TOK:TOK + NMOE], ALU.mult).then_inc(x_masked, 1)

            def mask_z(e):
                dve.wait_ge(mask_made, NEXP + e + 1)
                if e == 0:
                    dve.wait_ge(turn_read, ZG + 1)
                if e >= 3:
                    dve.wait_ge(y_used, e - 2)
                dve.tensor_tensor(zmasked[:, e % 3, :], pmask[:], zeT[:], ALU.mult).then_inc(z_masked, 1)

            def z_stats(first, last):
                for t in range(first, last):
                    ins = dve.bn_stats(zstat[:, t, :], G.Z[:, t, :])
                link(ins)

            def chunk_affine(c):
                for q in range(4):
                    ins = dve.bn_aggr(mv[:, c, :, q], stats[:, 4 * c + q, :])
                link(ins)
                r = rstd[:, 4 * c:4 * c + 4]
                newton_rsqrt(dve, link, r, mv[:, c, 1, :], tmp[:])
                ins = dve.scalar_tensor_tensor(shift[:, 4 * c:4 * c + 4], mv[:, c, 0, :], -1.0, r, ALU.mult, ALU.mult)
                if c < CHUNKS:
                    ins.then_inc(affine, 1)

            def add_shared(n, pair):
                dve.wait_ge(so_made, n + 1)
                src = pso[:, n % 2, :].rearrange("p (q d) -> p q d", q=2)
                if pair >= PAIRS:
                    q = 2 * (pair - PAIRS)
                    dve.tensor_tensor(G.shared_g[:, q:q + 2, :], src,
                                      G.rvec[:, R_SB3:R_SB3 + 1, :].broadcast_to([P, 2, D]), ALU.add).then_inc(so_added, 1)
                    return
                dve.wait_ge(biased, 2 * pair + 2)
                dve.tensor_tensor(G.X[:, 2 * pair:2 * pair + 2, :], src, G.X[:, 2 * pair:2 * pair + 2, :],
                                  ALU.add).then_inc(so_added, 1)
                dve.wait_ge(so_added, n + 1)
                for t in (2 * pair, 2 * pair + 1):
                    ins = dve.bn_stats(stats[:, t, :], G.X[:, t, :])
                link(ins)

            mask_x(0)
            mask_x(1)
            z_stats(0, 10)
            mask_x(2)
            z_stats(10, XT)
            mask_x(3)
            for t in range(XT):
                ins = dve.bn_aggr(zmv[:, :, t], zstat[:, t, :])
            link(ins)
            mask_x(4)
            newton_rsqrt(dve, link, zrstd[:], zmv[:, 1, :], ztmp[:])
            dve.scalar_tensor_tensor(zshift[:], zmv[:, 0, :], -1.0, zrstd[:], ALU.mult, ALU.mult).then_inc(z_affine, 1)
            for e in range(5, NEXP):
                mask_x(e)
            for t in range(MT):
                dve.wait_ge(gated, t + 1)
                dve.tensor_tensor(ze[:, t, :], ph[:, t, EH:D], gate[:, t, :], ALU.mult).then_inc(z_read, 1)
            dve.wait_ge(z_read, MT)
            for t in range(MT):
                ins = dve.bn_stats(stats[:, TILES + t, :], ze[:, t, :])
            link(ins)
            E = MT + 1
            for q in range(MT):
                ins = dve.bn_aggr(mv[:, E, :, q], stats[:, TILES + q, :])
            link(ins)
            newton_rsqrt(dve, link, rstd[:, XT:XT + 4], mv[:, E, 1, :], tmp[:])
            for q in range(MT):
                dve.tensor_scalar(ze[:, q, :], ze[:, q, :], mv[:, E, 0, q:q + 1], rstd[:, XT + q:XT + q + 1],
                                  ALU.subtract, ALU.mult).then_inc(ze_normed, 1)
            for n in range(2):
                add_shared(n, PAIRS + n)
            dve.wait_ge(so_added, 2)
            for e in range(NEXP):
                mask_z(e)
                add_shared(2 + e, e)
                if e % 2 == 1:
                    chunk_affine(e // 2)
                if e < MT:
                    x = G.X[:, TILES + e, :]
                    link(dve.scalar_tensor_tensor(x, G.shared_g[:, e, :], G.pair[:, e, 0:1], x, ALU.mult, ALU.add))
            for t in range(MT):
                dve.wait_ge(y_made, t + 1)
                x = G.X[:, TILES + t, :]
                link(dve.scalar_tensor_tensor(x, ph[:, t, 0:D], G.pair[:, t, 1:2], x, ALU.mult, ALU.add))
                ins = dve.bn_stats(stats[:, TILES + t, :], x)
            link(ins)
            chunk_affine(CHUNKS)
            for q in range(MT):
                x = G.X[:, TILES + q, :]
                dve.tensor_scalar(x, x, mv[:, CHUNKS, 0, q:q + 1], rstd[:, TILES + q:TILES + q + 1],
                                  ALU.subtract, ALU.mult).then_inc(last_normed, 1)

        @block.sync
        def _(sp):
            for c in range(CHUNKS):
                sp.wait_ge(normed, 4 * c + 4)
                sp.dma_start(out[4 * c:4 * c + 4].rearrange("t p d -> p t d"), G.X[:, 4 * c:4 * c + 4, :]).then_inc(stored, 16)
            sp.wait_ge(stored, 16 * CHUNKS)


class Shared:

    def __init__(self, nc, st):
        sb = lambda *a: st.enter_context(nc.sbuf_tensor(*a))
        self.X = sb("X", [P, XT, D], F32)
        self.xT = sb("xT", [P, 2, TOK + NMOE], F32)
        self.ident = sb("ident", [P, P], F32)
        self.halfpi = sb("halfpi", [P, 1], F32)
        self.wmat = sb("wmat", [P, 14, 2, D], F32)
        self.fvec, self.evec = sb("fvec", [P, 10, 2], F32), sb("evec", [P, 4], F32)
        self.rvec, self.grow = sb("rvec", [P, NROWS, D], F32), sb("grow", [P, 17], F32)
        self.ffn_s = sb("ffn_s", [P, 4, MB], F32)
        self.tok, self.tok_once, self.tok_f = sb("tok", [P, MT], U32), sb("tok_once", [P, MT], U32), sb("tok_f", [P, MT], F32)
        dram = lambda name, shape, dt: nc.dram_tensor(name, shape, dt).ap()
        self.q_dram = dram("q_parts", [3, B, D, S], BF16)
        self.k_dram = dram("k_parts", [3, B, D, S], BF16)
        self.qx_dram = dram("qx_parts", [3, B, D, S], BF16)
        self.kx_dram = dram("kx_parts", [3, B, D, SK], BF16)
        self.x_dram = dram("x_rows", [TILES, P, D], F32)


def decoder_kernel(nc, I, out):
    with ExitStack() as st:
        G = Shared(nc, st)
        G.ffn_units, G.ffn_w3, G.mask = I["ffn_units"], I["ffn_w3"], I["mask"]
        tile = lambda t: slice(t * P, (t + 1) * P)

        def out_products(mat):
            return lambda t: [(G.AT[:, k, tile(t)], G.wmat[:, mat, k, :]) for k in range(2)]

        with nc.sbuf_tensor("w_raw", [P, RW, 1024], F32) as G.w_raw:
            with ExitStack() as st0:
                sb = lambda *a: st0.enter_context(nc.sbuf_tensor(*a))
                G.basis, G.holo = sb("basis", [P, 2, P], F32), sb("holo", [96, 2, 2, D], F32)
                G.ctxT, G.Vx = sb("ctxT", [P, 2, B * SK + SKP - SK], F32), sb("Vx", [P, SLOTS, 1, DH + 1], F32)
                G.Vx_rest = sb("Vx_rest", [P, SLOTS, DH + 1], F32)
                G.ro = sb("ro", [HARM, TOK], F32)
                G.A, G.AT = sb("A", [P, TPB, B * D], F32), sb("AT", [P, 2, TOK], F32)
                stage_setup(nc, I, G)
                with nc.sbuf_tensor("V", [P, SLOTS, TPB, DH], F32) as G.V:
                    stage_project_self(nc, G)
                    stage_attention(nc, G, "a0")
                stage_finish(nc, G, "end0", "resonance", lambda t: [(G.ro[:, tile(t)], G.holo[0:HARM, 0, 1, :])])
                clear_used(nc)
                stage_project_cross(nc, G, "p1", M_X0Q, M_X0K, M_X0V, 1.0 / 16, None, None, None, spread=True)
                stage_attention_over_queries(nc, G)
                stage_finish(nc, G, "end1", "heads", out_products(M_X0O), prefetch=True)
            stage_ffn0(nc, G)
        stage_turn(nc, G, "t2")
        clear_used(nc)
        sb = lambda *a: st.enter_context(nc.sbuf_tensor(*a))
        G.A, G.AT = sb("A_l1", [P, TPB, B * D], F32), sb("AT_l1", [P, 2, TOK], F32)
        stage_holographic(nc, G)
        stage_finish(nc, G, "end3", "memory", None, row=R_LBO)
        with ExitStack() as st0:
            sb = lambda *a: st0.enter_context(nc.sbuf_tensor(*a))
            G.ctxT, G.Vx = sb("ctxT2", [P, 2, B * SK], F32), sb("Vx2", [P, SLOTS, 2, DH], F32)
            stage_reload_context(nc, I, G)
            stage_project_cross(nc, G, "p4", M_X1Q, M_X1K, M_X1V, DH ** -0.5, V_X1BQ, V_X1BK, R_X1BV)
            stage_attention_cross(nc, G, "a4")
            stage_finish(nc, G, "end4", "heads", out_products(M_X1O), row=R_X1BO, scratch=G.x_dram)
        clear_used(nc)
        sb = lambda *a: st.enter_context(nc.sbuf_tensor(*a))
        G.ew12, G.ew3 = sb("ew12", [P, 2, NEXP, D], F32), sb("ew3", [P, NEXP, D], F32)
        G.sw12, G.sw3 = sb("sw12", [P, 2, D], F32), sb("sw3", [P, D], F32)
        G.gw, G.eb = sb("gw", [P, 2, 9], F32), sb("eb", [NEXP, 2 * D], F32)
        G.Z, G.ZT = sb("Z", [P, XT, EH], F32), sb("ZT", [P, 1, TOK + NMOE], F32)
        G.shared_g, G.pair = sb("shared_g", [P, MT, D], F32), sb("pair", [P, MT, 2], F32)
        G.hotT, G.hotT_b = sb("hotT", [NEXP, NMOE], F32), sb("hotT_b", [NEXP, NMOE], BF16)
        G.pick = sb("pick", [NEXP, NEXP, P], BF16)
        stage_gather(nc, I, G)
        stage_gates(nc, G)
        stage_mixture(nc, G, out)


def stage_reload_context(nc, I, G):
    with ExitStack() as st:
        loaded = st.enter_context(nc.semaphore("ctx_loaded"))
        block = st.enter_context(nc.Block())

        @block.sync
        def _(sp):
            sp.dma_start(G.ctxT[:], I["ctx_fm"].rearrange("k p t -> p k t")).then_inc(loaded, 16)
            sp.wait_ge(loaded, 16)


def kernel(**inputs):
    import numpy as _np
    import concourse.bacc as _bacc
    from concourse import mybir as _mybir
    from concourse.bass_utils import run_bass_kernel_spmd as _run

    a = {k: _np.asarray(v) for k, v in inputs.items()}

    def fm(w):
        return w.reshape(w.shape[0] // 128, 128, -1).transpose(1, 0, 2)

    def col(v):
        return v.reshape(-1, 128).T

    x = a["x"].reshape(2048, 256)
    mats = [a["L0_xattn_Wq"].T, a["L0_xattn_Wk"].T, a["L0_xattn_Wv"].T, a["L0_xattn_Wo"].T,
            a["L1_attn_Wk"].T, a["L1_attn_Wv"].T, a["L1_attn_Wq"].T, a["L1_attn_Wkp"].T, a["L1_attn_Wqp"].T,
            a["L1_attn_Wo"].T, a["L1_xattn_Wq"], a["L1_xattn_Wk"], a["L1_xattn_Wv"], a["L1_xattn_Wo"]]
    w1, w2 = fm(a["L0_ffn_w1_w"].T), fm(a["L0_ffn_w2_w"].T)
    h1, h2, w3 = fm(a["L0_ffn_h1_w"].T), fm(a["L0_ffn_h2_w"].T), fm(a["L0_ffn_w3_w"].T)
    units = [_np.concatenate([w[:, k, m * 128:(m + 1) * 128] for m in (2 * u, 2 * u + 1) for w in (w1, w2)
                              for k in range(2)], axis=1) for u in range(4)]
    units += [h[:, :, m * 128:(m + 1) * 128].reshape(128, 1024) for h in (h1, h2) for m in range(8)]
    experts = lambda w: w.transpose(2, 0, 1)
    arrays = {
        "x_tm": x.reshape(16, 128, 256),
        "x_fm": x.T.reshape(2, 128, 2048),
        "ctx_fm": a["ctx_1024"].reshape(308, 256).T.reshape(2, 128, 308),
        "mask": a["mask_Bx1xS2_ik0"].reshape(2, 154),
        "basis": _np.concatenate([a["L0_attn_basis_" + c] for c in "qkvo"]).T.reshape(2, 128, 128),
        "phase_qkv": _np.concatenate([a["L0_attn_phase_" + c].T for c in "qkv"]),
        "amp_qkv": _np.concatenate([a["L0_attn_amp_" + c].T for c in "qkv"]),
        "phase_o": a["L0_attn_phase_o"].T, "amp_o": a["L0_attn_amp_o"].T,
        "wmat": _np.stack([fm(m) for m in mats], axis=1),
        "fvec": _np.stack([col(a[n]) for n in ("L1_attn_bk", "L1_attn_bv", "L1_attn_bq", "L1_attn_bkp", "L1_attn_bqp",
                                               "L1_attn_phase_scale", "L1_attn_ln_g", "L1_attn_ln_b",
                                               "L1_xattn_bq", "L1_xattn_bk")], axis=1),
        "evec": _np.stack([a["L1_ffn_" + n] for n in ("s_ln_g", "s_ln_b", "sel_ln_g", "sel_ln_b")], axis=1),
        "rvec": _np.stack([a["L1_attn_bo"], a["L1_xattn_bv"], a["L1_xattn_bo"], a["L0_ffn_w3_s"], a["L1_ffn_sb3"],
                           _np.concatenate([a["L1_ffn_sb1"], a["L1_ffn_sb2"]])]),
        "grow": _np.concatenate([a["L1_ffn_sg_b"], a["L1_ffn_eg_b"], a["L1_ffn_exp_bias"]]),
        "ffn_s": _np.stack([col(a["L0_ffn_" + n]) for n in ("w1_s", "w2_s", "h1_s", "h2_s")], axis=1),
        "ffn_units": _np.stack(units),
        "ffn_w3": _np.stack([w3[:, 2 * v:2 * v + 2, :].reshape(128, 512) for v in range(4)]),
        "index_b": a["L1_ffn_index_b"], "index_t": a["L1_ffn_index_t"],
        "sw12": _np.concatenate([a["L1_ffn_sw1"], a["L1_ffn_sw2"]]).T.reshape(2, 128, 256),
        "sw3": a["L1_ffn_sw3"].T,
        "gw": _np.concatenate([a["L1_ffn_sg_w"], a["L1_ffn_eg_w"]]).T.reshape(2, 128, 9),
        "ew12": _np.concatenate([experts(a["L1_ffn_ew1"]), experts(a["L1_ffn_ew2"])], axis=2).reshape(2, 128, 8, 256),
        "ew3": experts(a["L1_ffn_ew3"]),
        "eb": _np.concatenate([a["L1_ffn_eb1"], a["L1_ffn_eb2"], a["L1_ffn_eb3"]], axis=1),
    }
    arrays = {k: _np.ascontiguousarray(v) for k, v in arrays.items()}
    nc = _bacc.Bacc("TRN2", target_bir_lowering=False, num_devices=1)
    I = {k: nc.dram_tensor("in_" + k, v.shape, _mybir.dt.from_np(v.dtype), kind="ExternalInput").ap()
         for k, v in arrays.items()}
    out = nc.dram_tensor("out_x", (16, 128, 256), _mybir.dt.float32, kind="ExternalOutput").ap()
    decoder_kernel(nc, I, out)
    r = _run(nc, [{"in_" + k: v for k, v in arrays.items()}], core_ids=[0])
    return r.results[0]["out_x"].reshape(2, 1024, 256)
```
